# Optimizing a Trainium2 kernel written in Bass

```python
import numpy as np
import jax
import jax.numpy as jnp

def _softmax(x, axis=-1):
    return jax.nn.softmax(x, axis=axis)

def _gelu(x):
    return jax.nn.gelu(x, approximate=True)

def _silu(x):
    return jax.nn.silu(x)

def _sigmoid(x):
    return jax.nn.sigmoid(x)

def _layernorm(x, axis=-1, eps=1e-05):
    m = jnp.mean(x, axis=axis, keepdims=True)
    v = jnp.var(x, axis=axis, keepdims=True)
    return (x - m) / jnp.sqrt(v + eps)

def _scatter_add(tgt, idx, src, axis=0):
    return tgt.at[idx].add(src)

def _segment_sum(src, seg, n):
    return jax.ops.segment_sum(src, seg, n)
kernel_name = 'mk_recurrent_d2_jaxref_r8_426158'

def setup_inputs(seed: int=0):
    np.random.seed(seed)
    _w = jnp.asarray

    def _L0_attn_setup():
        import jax, jax.numpy as jnp
        import numpy as np
        C = 128
        H = 16
        K = 2
        B, N = (4, 512)

        def _heads(t):
            shp = t.shape
            d = shp[-1] // H
            t = t.reshape(shp[:-1] + (H, d))
            return jnp.swapaxes(t, -2, -3)
        key = jax.random.key(seed)
        ks_ = jax.random.split(key, 12)
        s = 1.0 / np.sqrt(C)
        inp = {'x': jax.random.normal(ks_[0], (B, N, C), dtype=jnp.float32), 'Wq': jax.random.normal(ks_[1], (C, C), dtype=jnp.float32) * s, 'bq': jnp.zeros((C,), dtype=jnp.float32), 'Wk': jax.random.normal(ks_[2], (K, C, C), dtype=jnp.float32) * s, 'bk': jnp.zeros((K, C), dtype=jnp.float32), 'Wv': jax.random.normal(ks_[3], (K, C, C), dtype=jnp.float32) * s, 'bv': jnp.zeros((K, C), dtype=jnp.float32), 'Wo': jax.random.normal(ks_[4], (C, C), dtype=jnp.float32) * s, 'bo': jnp.zeros((C,), dtype=jnp.float32), 'ln_g': jnp.ones((C,), dtype=jnp.float32), 'ln_b': jnp.zeros((C,), dtype=jnp.float32)}
        return inp
    _L0_attn_in = _L0_attn_setup()

    def _L0_ffn_setup():
        import jax, jax.numpy as jnp
        import numpy as np
        N_EXPERTS = 32
        TOP_K = 8
        N_GROUP = 4
        TOPK_GROUP = 2
        ROUTED_SCALING = 2.5

        def _gate(x, gate_w, gate_bias):
            T, E = (x.shape[0], gate_w.shape[0])
            logits = jnp.einsum('th,eh->te', x, gate_w)
            scores = jax.nn.sigmoid(logits)
            scores_choice = scores + gate_bias[None, :]
            grp = scores_choice.reshape(T, N_GROUP, E // N_GROUP)
            top2, _ = jax.lax.top_k(grp, 2)
            group_scores = top2.sum(-1)
            _, grp_idx = jax.lax.top_k(group_scores, TOPK_GROUP)
            group_mask = jax.nn.one_hot(grp_idx, N_GROUP, dtype=scores.dtype).sum(1)
            expert_mask = jnp.repeat(group_mask, E // N_GROUP, axis=1)
            masked = jnp.where(expert_mask > 0, scores_choice, 0.0)
            _, topk_idx = jax.lax.top_k(masked, TOP_K)
            topk_w = jnp.take_along_axis(scores, topk_idx, axis=1)
            topk_w = topk_w / (topk_w.sum(-1, keepdims=True) + 1e-20)
            topk_w = topk_w * ROUTED_SCALING
            return (topk_idx, topk_w)

        def _mlp(x, wg, wu, wd):
            return jnp.einsum('...i,hi->...h', jax.nn.silu(jnp.einsum('...h,ih->...i', x, wg)) * jnp.einsum('...h,ih->...i', x, wu), wd)
        key = jax.random.key(seed)
        ks = jax.random.split(key, 9)
        B, S, H, I = (2, 64, 128, 64)
        w = 0.02
        return {'hidden_states': jax.random.normal(ks[0], (B, S, H), jnp.float32), 'gate_w': jax.random.normal(ks[1], (N_EXPERTS, H), jnp.float32) * w, 'gate_bias': jax.random.normal(ks[2], (N_EXPERTS,), jnp.float32) * w, 'expert_gate': jax.random.normal(ks[3], (N_EXPERTS, I, H), jnp.float32) * w, 'expert_up': jax.random.normal(ks[4], (N_EXPERTS, I, H), jnp.float32) * w, 'expert_down': jax.random.normal(ks[5], (N_EXPERTS, H, I), jnp.float32) * w, 'shared_gate': jax.random.normal(ks[6], (2 * I, H), jnp.float32) * w, 'shared_up': jax.random.normal(ks[7], (2 * I, H), jnp.float32) * w, 'shared_down': jax.random.normal(ks[8], (H, 2 * I), jnp.float32) * w}
    _L0_ffn_in = _L0_ffn_setup()

    def _L1_attn_setup():
        import jax, jax.numpy as jnp
        import numpy as np
        LANES = 4
        EPS = 1e-08

        def _rms_norm(z):
            return z * jax.lax.rsqrt(jnp.mean(z * z, axis=-1, keepdims=True) + EPS)

        def _combine(left, right, W):
            B, T, C = left.shape
            hd = C // LANES
            q = left.reshape(B, T, LANES, hd)
            k = right.reshape(B, T, LANES, hd)
            v = ((left + right) @ W).reshape(B, T, LANES, hd)
            scores = jnp.einsum('btld,btmd->btlm', q, k) * hd ** (-0.5)
            att = jax.nn.softmax(scores, axis=-1)
            z = jnp.einsum('btlm,btmd->btld', att, v)
            denom = (1.0 + jnp.arange(LANES, dtype=z.dtype))[None, None, :, None]
            z = _rms_norm(z) / denom
            return left + z.reshape(B, T, C)

        def _pscan2(x, W, identity):
            B, T, C = x.shape
            d = 1
            while d < T:
                ident = jnp.broadcast_to(identity.astype(x.dtype), (B, d, C))
                shifted = jnp.concatenate([ident, x[:, :-d]], axis=1)
                x = _combine(shifted, x, W)
                d *= 2
            return x

        def _reference_tuple_inner(x, W_up, W_v, W_proj, identity, W_scan_raw):
            U, _, Vt = jnp.linalg.svd(W_scan_raw, full_matrices=False)
            W = U @ Vt
            q = x @ W_up.T
            v = x @ W_v.T
            q = _pscan2(q, W, identity)
            Y = q * v @ W_proj.T
            return (Y, q)
        key = jax.random.key(seed)
        ks = jax.random.split(key, 6)
        B, T, C = (4, 256, 128)
        s = 0.02
        x = jax.random.normal(ks[0], (B, T, C), dtype=jnp.float32)
        W_up = jax.random.normal(ks[1], (C, C), dtype=jnp.float32) * s
        W_v = jax.random.normal(ks[2], (C, C), dtype=jnp.float32) * s
        W_proj = jax.random.normal(ks[3], (C, C), dtype=jnp.float32) * s
        identity = jax.random.uniform(ks[4], (C,), dtype=jnp.float32)
        W_scan_raw = jax.random.normal(ks[5], (C, C), dtype=jnp.float32) * s
        return {'x': x, 'W_up': W_up, 'W_v': W_v, 'W_proj': W_proj, 'identity': identity, 'W_scan_raw': W_scan_raw}
    _L1_attn_in = _L1_attn_setup()

    def _L1_ffn_setup():
        import jax, jax.numpy as jnp
        import numpy as np
        D, H, O, E, TOPK = (128, 512, 128, 8, 2)
        B, L = (2, 256)
        ROUTE_SCALE = 1.0
        key = jax.random.key(seed)
        ks = jax.random.split(key, 7)
        gb = float(np.sqrt(6.0 / (E + D)))
        return {'x': jax.random.normal(ks[0], (B, L, D), dtype=jnp.float32), 'gate_w': jax.random.uniform(ks[1], (E, D), jnp.float32, -gb, gb), 'gate_b': jnp.zeros((E,), jnp.float32), 'w1': jax.random.normal(ks[2], (E, D, H), jnp.float32) * 0.02, 'b1': jnp.zeros((E, H), jnp.float32), 'w2': jax.random.normal(ks[3], (E, H, O), jnp.float32) * 0.02, 'b2': jnp.zeros((E, O), jnp.float32)}
    _L1_ffn_in = _L1_ffn_setup()
    _d = {'L0_attn_x': _L0_attn_in['x'], 'L0_attn_Wq': _L0_attn_in['Wq'], 'L0_attn_bq': _L0_attn_in['bq'], 'L0_attn_Wk': _L0_attn_in['Wk'], 'L0_attn_bk': _L0_attn_in['bk'], 'L0_attn_Wv': _L0_attn_in['Wv'], 'L0_attn_bv': _L0_attn_in['bv'], 'L0_attn_Wo': _L0_attn_in['Wo'], 'L0_attn_bo': _L0_attn_in['bo'], 'L0_attn_ln_g': _L0_attn_in['ln_g'], 'L0_attn_ln_b': _L0_attn_in['ln_b'], 'L0_ffn_gate_w': _L0_ffn_in['gate_w'], 'L0_ffn_gate_bias': _L0_ffn_in['gate_bias'], 'L0_ffn_expert_gate': _L0_ffn_in['expert_gate'], 'L0_ffn_expert_up': _L0_ffn_in['expert_up'], 'L0_ffn_expert_down': _L0_ffn_in['expert_down'], 'L0_ffn_shared_gate': _L0_ffn_in['shared_gate'], 'L0_ffn_shared_up': _L0_ffn_in['shared_up'], 'L0_ffn_shared_down': _L0_ffn_in['shared_down'], 'L1_attn_W_up': _L1_attn_in['W_up'], 'L1_attn_W_v': _L1_attn_in['W_v'], 'L1_attn_W_proj': _L1_attn_in['W_proj'], 'L1_attn_identity': _L1_attn_in['identity'], 'L1_attn_W_scan_raw': _L1_attn_in['W_scan_raw'], 'L1_ffn_gate_w': _L1_ffn_in['gate_w'], 'L1_ffn_gate_b': _L1_ffn_in['gate_b'], 'L1_ffn_w1': _L1_ffn_in['w1'], 'L1_ffn_b1': _L1_ffn_in['b1'], 'L1_ffn_w2': _L1_ffn_in['w2'], 'L1_ffn_b2': _L1_ffn_in['b2']}
    _x0 = _d['L0_attn_x']
    _d['L0_attn_x'] = jax.random.normal(jax.random.fold_in(jax.random.key(seed), 1), (4, 512, 128), dtype=_x0.dtype)
    del _x0
    return _d

def reference(L0_attn_x, L0_attn_Wq, L0_attn_bq, L0_attn_Wk, L0_attn_bk, L0_attn_Wv, L0_attn_bv, L0_attn_Wo, L0_attn_bo, L0_attn_ln_g, L0_attn_ln_b, L0_ffn_gate_w, L0_ffn_gate_bias, L0_ffn_expert_gate, L0_ffn_expert_up, L0_ffn_expert_down, L0_ffn_shared_gate, L0_ffn_shared_up, L0_ffn_shared_down, L1_attn_W_up, L1_attn_W_v, L1_attn_W_proj, L1_attn_identity, L1_attn_W_scan_raw, L1_ffn_gate_w, L1_ffn_gate_b, L1_ffn_w1, L1_ffn_b1, L1_ffn_w2, L1_ffn_b2):

    def _L0_attn_ref(x, Wq, bq, Wk, bk, Wv, bv, Wo, bo, ln_g, ln_b):
        import jax, jax.numpy as jnp
        import numpy as np
        C = 128
        H = 16
        K = 2
        B, N = (4, 512)

        def _heads(t):
            shp = t.shape
            d = shp[-1] // H
            t = t.reshape(shp[:-1] + (H, d))
            return jnp.swapaxes(t, -2, -3)
        dtype = x.dtype
        q = x + jnp.einsum('bnc,cd->bnd', x, Wq) + bq
        ks = x[None] + jnp.einsum('bnc,kcd->kbnd', x, Wk) + bk[:, None, None, :]
        vs = x[None] + jnp.einsum('bnc,kcd->kbnd', x, Wv) + bv[:, None, None, :]
        q = _heads(q)
        ks = _heads(ks)
        vs = _heads(vs)
        scale = 1.0 / jnp.sqrt(jnp.asarray(N, dtype=jnp.float32))
        ks = ks.astype(jnp.float32) * scale
        vs = vs.astype(jnp.float32) * scale
        states = jnp.einsum('kbhnd,kbhne->kbhde', ks, vs)
        state = jnp.prod(states, axis=0)
        out = jnp.einsum('bhnd,bhde->bhne', q.astype(jnp.float32), state)
        out = out.astype(dtype)
        out = jnp.swapaxes(out, 1, 2).reshape(x.shape[0], x.shape[1], C)
        mu = jnp.mean(out, axis=-1, keepdims=True)
        var = jnp.var(out, axis=-1, keepdims=True)
        out = (out - mu) / jnp.sqrt(var + 1e-05) * ln_g + ln_b
        out = jnp.einsum('bnc,cd->bnd', out, Wo) + bo
        return out

    def _L0_ffn_ref(hidden_states, gate_w, gate_bias, expert_gate, expert_up, expert_down, shared_gate, shared_up, shared_down):
        import jax, jax.numpy as jnp
        import numpy as np
        N_EXPERTS = 32
        TOP_K = 8
        N_GROUP = 4
        TOPK_GROUP = 2
        ROUTED_SCALING = 2.5

        def _gate(x, gate_w, gate_bias):
            T, E = (x.shape[0], gate_w.shape[0])
            logits = jnp.einsum('th,eh->te', x, gate_w)
            scores = jax.nn.sigmoid(logits)
            scores_choice = scores + gate_bias[None, :]
            grp = scores_choice.reshape(T, N_GROUP, E // N_GROUP)
            top2, _ = jax.lax.top_k(grp, 2)
            group_scores = top2.sum(-1)
            _, grp_idx = jax.lax.top_k(group_scores, TOPK_GROUP)
            group_mask = jax.nn.one_hot(grp_idx, N_GROUP, dtype=scores.dtype).sum(1)
            expert_mask = jnp.repeat(group_mask, E // N_GROUP, axis=1)
            masked = jnp.where(expert_mask > 0, scores_choice, 0.0)
            _, topk_idx = jax.lax.top_k(masked, TOP_K)
            topk_w = jnp.take_along_axis(scores, topk_idx, axis=1)
            topk_w = topk_w / (topk_w.sum(-1, keepdims=True) + 1e-20)
            topk_w = topk_w * ROUTED_SCALING
            return (topk_idx, topk_w)

        def _mlp(x, wg, wu, wd):
            return jnp.einsum('...i,hi->...h', jax.nn.silu(jnp.einsum('...h,ih->...i', x, wg)) * jnp.einsum('...h,ih->...i', x, wu), wd)
        orig_shape = hidden_states.shape
        H = orig_shape[-1]
        residuals = hidden_states
        x = hidden_states.reshape(-1, H)
        topk_idx, topk_w = _gate(x, gate_w, gate_bias)
        g = jnp.einsum('th,eih->eti', x, expert_gate)
        u = jnp.einsum('th,eih->eti', x, expert_up)
        outs = jnp.einsum('eti,ehi->eth', jax.nn.silu(g) * u, expert_down)
        outs_t = jnp.transpose(outs, (1, 0, 2))
        gathered = jnp.take_along_axis(outs_t, topk_idx[:, :, None], axis=1)
        final = (gathered * topk_w[:, :, None]).sum(1)
        shared = _mlp(residuals, shared_gate, shared_up, shared_down)
        return final.reshape(orig_shape) + shared

    def _L1_attn_ref(x, W_up, W_v, W_proj, identity, W_scan_raw):
        import jax, jax.numpy as jnp
        import numpy as np
        LANES = 4
        EPS = 1e-08

        def _rms_norm(z):
            return z * jax.lax.rsqrt(jnp.mean(z * z, axis=-1, keepdims=True) + EPS)

        def _combine(left, right, W):
            B, T, C = left.shape
            hd = C // LANES
            q = left.reshape(B, T, LANES, hd)
            k = right.reshape(B, T, LANES, hd)
            v = ((left + right) @ W).reshape(B, T, LANES, hd)
            scores = jnp.einsum('btld,btmd->btlm', q, k) * hd ** (-0.5)
            att = jax.nn.softmax(scores, axis=-1)
            z = jnp.einsum('btlm,btmd->btld', att, v)
            denom = (1.0 + jnp.arange(LANES, dtype=z.dtype))[None, None, :, None]
            z = _rms_norm(z) / denom
            return left + z.reshape(B, T, C)

        def _pscan2(x, W, identity):
            B, T, C = x.shape
            d = 1
            while d < T:
                ident = jnp.broadcast_to(identity.astype(x.dtype), (B, d, C))
                shifted = jnp.concatenate([ident, x[:, :-d]], axis=1)
                x = _combine(shifted, x, W)
                d *= 2
            return x

        def _reference_tuple_inner(x, W_up, W_v, W_proj, identity, W_scan_raw):
            U, _, Vt = jnp.linalg.svd(W_scan_raw, full_matrices=False)
            W = U @ Vt
            q = x @ W_up.T
            v = x @ W_v.T
            q = _pscan2(q, W, identity)
            Y = q * v @ W_proj.T
            return (Y, q)
        return _reference_tuple_inner(x, W_up, W_v, W_proj, identity, W_scan_raw)[0]

    def _L1_ffn_ref(x, gate_w, gate_b, w1, b1, w2, b2):
        import jax, jax.numpy as jnp
        import numpy as np
        D, H, O, E, TOPK = (128, 512, 128, 8, 2)
        B, L = (2, 256)
        ROUTE_SCALE = 1.0
        Bb, Ll, Dd = x.shape
        N = Bb * Ll
        x_flat = x.reshape(N, Dd)
        logits = x_flat @ gate_w.T + gate_b
        probs = jax.nn.softmax(logits * ROUTE_SCALE, axis=-1)
        topk_vals, topk_idx = jax.lax.top_k(probs, TOPK)
        dense_gate = jnp.zeros((N, E), probs.dtype).at[jnp.arange(N)[:, None], topk_idx].set(topk_vals)
        h = jax.nn.relu(jnp.einsum('nd,edh->neh', x_flat, w1) + b1)
        y = jnp.einsum('neh,eho->neo', h, w2) + b2
        out_flat = jnp.einsum('ne,neo->no', dense_gate, y)
        return out_flat.reshape(Bb, Ll, O)
    x = L0_attn_x
    xn = _layernorm(x, axis=-1)
    s = _L0_attn_ref(xn, L0_attn_Wq, L0_attn_bq, L0_attn_Wk, L0_attn_bk, L0_attn_Wv, L0_attn_bv, L0_attn_Wo, L0_attn_bo, L0_attn_ln_g, L0_attn_ln_b)
    g = _silu(_L0_ffn_ref(xn, L0_ffn_gate_w, L0_ffn_gate_bias, L0_ffn_expert_gate, L0_ffn_expert_up, L0_ffn_expert_down, L0_ffn_shared_gate, L0_ffn_shared_up, L0_ffn_shared_down))
    x = x + s * g
    xn = _layernorm(x, axis=-1)
    s = _L1_attn_ref(xn, L1_attn_W_up, L1_attn_W_v, L1_attn_W_proj, L1_attn_identity, L1_attn_W_scan_raw)
    g = _silu(_L1_ffn_ref(xn, L1_ffn_gate_w, L1_ffn_gate_b, L1_ffn_w1, L1_ffn_b1, L1_ffn_w2, L1_ffn_b2))
    x = x + s * g
    return x

_drawn_inputs = setup_inputs


def setup_inputs(seed=0):
    import zlib

    import numpy as np

    out = dict(_drawn_inputs(seed))
    spreads = {'L0_attn_bq': (0.0, 0.8),
     'L0_attn_bk': (0.0, 0.8),
     'L0_attn_bv': (0.0, 0.8),
     'L0_attn_bo': (0.0, 0.8),
     'L0_attn_ln_g': (1.0, 0.6),
     'L0_attn_ln_b': (0.0, 0.8),
     'L1_ffn_gate_b': (0.0, 0.8),
     'L1_ffn_b1': (0.0, 0.8),
     'L1_ffn_b2': (0.0, 0.8)}
    factors = {'L0_attn_Wq': 8.0,
     'L0_attn_Wk': 8.0,
     'L0_attn_Wv': 8.0,
     'L0_attn_Wo': 8.0,
     'L0_ffn_gate_w': 8.0,
     'L0_ffn_gate_bias': 8.0,
     'L0_ffn_expert_gate': 8.0,
     'L0_ffn_expert_up': 8.0,
     'L0_ffn_expert_down': 8.0,
     'L0_ffn_shared_gate': 8.0,
     'L0_ffn_shared_up': 8.0,
     'L0_ffn_shared_down': 8.0,
     'L1_attn_W_up': 8.0,
     'L1_attn_W_v': 8.0,
     'L1_attn_W_proj': 8.0,
     'L1_attn_identity': 8.0,
     'L1_attn_W_scan_raw': 8.0,
     'L1_ffn_gate_w': 8.0,
     'L1_ffn_w1': 8.0,
     'L1_ffn_w2': 8.0}
    for name, (base, spread) in spreads.items():
        noise = np.random.default_rng([zlib.crc32(name.encode()), seed]).standard_normal(out[name].shape)
        drawn = base * np.exp(spread * noise) if base else spread * noise
        out[name] = jnp.asarray(drawn.astype(out[name].dtype))
    for name, factor in factors.items():
        out[name] = (out[name] * factor).astype(out[name].dtype)
    return out
```

```python
from contextlib import ExitStack

import numpy as np
import concourse.bass as bass
from concourse import mybir

F32 = mybir.dt.float32
BF16 = mybir.dt.bfloat16
ALU = mybir.AluOpType
ACT = mybir.ActivationFunctionType
AX_X = mybir.AxisListType.X

P = 128
B, N = 4, 512
TB = N // P
NT = B * TB
E0, I0 = 32, 64
PAIRS = E0 * I0 // P
GROUPS, GE = 4, 8
TOP0 = 8
E1, H1 = 8, 512
HC = H1 // P
HEADS, HD = 16, 8
LANES, LD = 4, 32
LEVELS = 9
PAD = N // 2
LN_EPS = 1e-5
RMS_EPS = 1e-8
ROUTED = 2.5
FAR = -2.0 ** 127
SHARED = 30 * 1024
CONSTS = 22

POLAR = [(8.51425808, -25.281576, 18.7673094), (4.2570752, -3.16016629, 0.586476766),
         (4.25682787, -3.15999522, 0.586457253), (4.25577537, -3.15926721, 0.586374211),
         (4.25130191, -3.15617245, 0.586021201), (4.23238747, -3.14307812, 0.584527605),
         (4.15415638, -3.08875796, 0.578332236), (3.85835916, -2.88082531, 0.554631634),
         (3.0495984, -2.2849888, 0.487060827), (2.11205594, -1.49383647, 0.400102503),
         (1.87838366, -1.2537545, 0.375375648), (1.87500002, -1.25000002, 0.375000005)]
POLAR_PER_BATCH = len(POLAR) // B


def after(engine, semaphore, value):
    if not isinstance(value, int) or value > 0:
        engine.wait_ge(semaphore, value)


def build(nc, x_d, cols_d, rows_d, gate0_bias_d, gate1_bias_d, attn_w_d, gate0_d, wg_d, wu_d, wd_d,
          scan_raw_d, l1_w_d, gate1_d, w1_d, b1_d, w2_d, b2_d, out_d):
    ctx = ExitStack()
    with ctx:
        def sb(name, shape, dt=F32):
            return ctx.enter_context(nc.sbuf_tensor(name, shape, dt))

        def sem(name):
            return ctx.enter_context(nc.semaphore(name))

        shared = sb("shared", [P, SHARED])
        used = {0: 0, 1: 0}

        def carve(layer, shape):
            size = int(np.prod(shape[1:]))
            v = shared[:, used[layer]:used[layer] + size]
            used[layer] += size
            assert used[layer] <= SHARED, used
            dims = "abcdef"[:len(shape) - 1]
            if len(dims) > 1:
                v = v.rearrange(f"p ({' '.join(dims)}) -> p {' '.join(dims)}", **dict(zip(dims, shape[1:])))
            return v

        bank = [ctx.enter_context(nc.psum_tensor(f"bank{k}", [P, 512], F32)) for k in range(8)]

        cols = sb("cols", [P, 4])
        rows = sb("rows", [1, 5 * P])
        gate0_bias = sb("gate0_bias", [P, E0])
        gate1_bias = sb("gate1_bias", [P, E1])
        attn_w = carve(0, [P, 6, P])
        gate0_w = sb("gate0_w", [P, E0])
        wg = carve(0, [P, PAIRS + 1, P])
        wu = carve(0, [P, PAIRS + 1, P])
        wd = carve(0, [P, PAIRS + 1, P])
        polar_x = sb("polar_x", [P, P])
        l1_w = sb("l1_w", [P, 3, P])
        gate1_w = sb("gate1_w", [P, E1])
        w1 = sb("w1", [P, HC, P])
        b1 = sb("b1", [P, E1, HC])
        w2 = sb("w2", [P, E1, HC, P])
        b2 = sb("b2", [E1, P])

        ident = sb("ident", [P, P])
        ident_bf = sb("ident_bf", [P, P], BF16)
        ones = sb("ones", [P, P])
        tokens_n = sb("tokens_n", [1, 1])
        minus_half = sb("minus_half", [P, NT])
        head_mask = sb("head_mask", [P, P])
        lane_mask = sb("lane_mask", [P, LANES])
        lane_sel = sb("lane_sel", [P, LANES, LANES * LANES])
        inv_lane = sb("inv_lane", [P, TB, LANES])
        pair_sel = sb("pair_sel", [3 * E0, E0, I0], BF16)
        coef = sb("coef", [P, 3 * len(POLAR)])

        x = sb("x", [P, NT, P])
        xn = sb("xn", [P, NT, P + 1])
        xnT = sb("xnT", [P, B * N])
        s_tok = carve(0, [P, NT, P])
        ln_stats = sb("ln_stats", [P, NT, 6])
        ln_mv = sb("ln_mv", [P, NT, 2])
        ln_var = sb("ln_var", [P, NT])
        ln_rstd = sb("ln_rstd", [P, NT])

        gram = carve(0, [P, B, P + 1])
        srow = sb("srow", [1, B, P])
        m1 = carve(0, [P, B, 2 * P])
        m1row = sb("m1row", [1, B, 2 * P])
        state0 = carve(0, [P, B, P])
        state = carve(0, [P, B, P])
        mq = carve(0, [P, B, P])
        mqrow = sb("mqrow", [1, B, P])
        attn_n = carve(0, [P, NT, P])
        attn_nT = carve(0, [P, B * N])
        wo_g = carve(0, [P, P])
        borow = sb("borow", [1, P])

        scores0 = carve(0, [P, NT, E0])
        choice = carve(0, [P, NT, E0])
        top8 = carve(0, [P, NT, GROUPS, 8])
        gscore = carve(0, [P, NT, GROUPS])
        gcmp = carve(0, [P, NT, GROUPS, GROUPS])
        grank = carve(0, [P, NT, GROUPS])
        gmask = carve(0, [P, NT, GROUPS])
        masked = carve(0, [P, NT, E0])
        best8 = carve(0, [P, NT, 8])
        replaced = carve(0, [P, NT, E0])
        taken = carve(0, [P, NT, E0])
        wsum = sb("wsum", [P, NT])
        wsum_eps = sb("wsum_eps", [P, NT])
        wrec = sb("wrec", [P, NT])
        gate0 = carve(0, [P, NT, E0])
        gate0_rest = carve(0, [P, NT, E0])
        gate0_rest2 = carve(0, [P, NT, E0])
        gate0_parts = sb("gate0_parts", [P, NT, 3, E0], BF16)
        gate0T = sb("gate0T", [3 * E0, B * N], BF16)

        silu_g = carve(0, [P, 2, N])
        silu_gu = carve(0, [P, 2, N])
        h0 = carve(0, [P, 2, N])
        gl0T = carve(0, [P, N])
        sg = carve(0, [P, N])
        polar_gx = sb("polar_gx", [P, 2 * P])
        polar_ai = carve(0, [P, P])
        polar_ab = carve(0, [P, P])
        polar_b = carve(0, [P, P])
        polar_sq = carve(0, [P, P])
        polar_col = sb("polar_col", [P, 1])
        polar_sum = sb("polar_sum", [P, 1])
        polar_r = sb("polar_r", [P, 1])

        logits1 = sb("logits1", [P, NT, E1])
        lmax = sb("lmax", [P, NT])
        lsub = sb("lsub", [P, NT, E1])
        lexp = sb("lexp", [P, NT, E1])
        lsum = sb("lsum", [P, NT])
        lrec = sb("lrec", [P, NT])
        ecmp = carve(1, [P, NT, E1, E1])
        erank = sb("erank", [P, NT, E1])
        emask = sb("emask", [P, NT, E1])
        probs1 = sb("probs1", [P, NT, E1])
        gate1 = sb("gate1", [P, NT, E1])
        gate1T = sb("gate1T", [E1, B * N])

        xT = carve(1, [P, B, PAD + N])
        x_tok = carve(1, [P, B, TB, P + 3 * LD])
        leftT = carve(1, [P, B, N])
        sumT = carve(1, [P, B, N])
        prod = carve(1, [P, 2, LANES, N])
        smax = sb("smax", [P, 2, TB, LANES])
        ssub = carve(1, [P, 2, TB, LANES, LANES])
        sexp = carve(1, [P, 2, TB, LANES, LANES])
        ssum = sb("ssum", [P, 2, TB, LANES])
        mix = carve(1, [P, 2, TB, LANES, LANES, LD])
        mix2 = carve(1, [P, 2, TB, LANES, 2, LD])
        z = carve(1, [P, 2, TB, P])
        z_sq = carve(1, [P, 2, TB, P])
        z_ss = sb("z_ss", [P, 2, TB, LANES])
        eps_ss = sb("eps_ss", [P, 2, TB, LANES])
        z_ms = sb("z_ms", [P, 2, TB, LANES])
        z_rs = sb("z_rs", [P, 2, TB, LANES])
        z_r = sb("z_r", [P, 2, TB, LANES])
        zn = carve(1, [P, TB, P])
        hT = carve(1, [P, HC, N])
        b1_now = sb("b1_now", [P, HC])
        gate1_now = sb("gate1_now", [P, NT])
        acc = carve(1, [P, NT, P])
        qvT = leftT
        gl1 = z_sq

        S = {}

        def s(name):
            if name not in S:
                S[name] = sem(name)
            return S[name]

        for name in (
            "ld_x0 ld_x1 ld_x2 ld_x3 ld_w1_0 ld_w1_1 ld_w1_2 ld_w1_3 ld_scan ld_small ld_moe ld_l1 st_out "
            "const polar_const polar_sq_done polar_sum_mm polar_sum_cp polar_r_done polar_x0 "
            "ln_stat ln_var_done ln_pow ln_norm xnT_mm xnT_cp "
            "wfold wog_done borow_mm borow_cp "
            "gram_mm gram_cp m1_mm m1_cp st_mm st0_cp st_cp mq_mm mq_cp at_mm at_stat at_var at_pow at_norm "
            "atT_mm atT_cp so_mm so_cp logit_mm sig_done choice_done gtop gsum gcmp0 gcmp_done grank_done gmask_done "
            "masked_done best_done repl_done taken_done wraw_done wsum_done wsume_done wrec_done gate0_done "
            "hi_done rest_done mid_done rest2_done parts_done g0T_mm g0T_cp "
            "g_mm u_mm gb_mm silu_done gu_done h0_done dn_mm y0_silu y0T_mm sg_done x1_done "
            "polar_ai_done polar_a_mm polar_gx_cp polar_ab_done polar_a2_mm polar_b_done polar_x_mm polar_x_cp "
            "l1_stat l1_var l1_pow l1_norm x1T_mm x1T_cp log1_mm log1_cp lmax_done lsub_done lexp_done lsum_done "
            "lrec_done probs_done ecmp0 ecmp_done erank_done emask_done gate1_done g1T_mm g1T_cp acc_mm acc_cp "
            "up_mm up_cp uptok_mm pad_done "
            "rot_mm xT_cp left_cp right_prod rot_prod sum_done score_mm v_mm smax_done ssub_done sexp_done "
            "ssum_done mix_done mix2_done z_done zsq_done zss_done epsss_done zms_done zpow_done zr_done left_mm "
            "zn_done xtok_done dup_done ffn_up ffn_relu ffn_down ffn_acc "
            "b1_now_done gate_now_done v1_mm v1_cp qv_done yp_mm gl1_done o_mul o_done"
        ).split():
            s(name)

        block = ctx.enter_context(nc.Block())

        @block.sync
        def _(sp):
            xv = x_d.rearrange("b (j p) c -> p b j c", p=P)
            for b in range(B):
                sp.dma_start(x[:, b * TB:(b + 1) * TB, :], xv[:, b]).then_inc(s(f"ld_x{b}"), 16)
            sp.dma_start(polar_x[:], scan_raw_d).then_inc(s("ld_scan"), 16)
            sp.dma_start(attn_w[:], attn_w_d).then_inc(s("ld_small"), 16)
            sp.dma_start(cols[:], cols_d).then_inc(s("ld_small"), 16)
            sp.dma_start(rows[:], rows_d).then_inc(s("ld_small"), 16)
            sp.dma_start(gate0_w[:], gate0_d).then_inc(s("ld_small"), 16)
            sp.dma_start(gate0_bias[:], gate0_bias_d.partition_broadcast(P)).then_inc(s("ld_small"), 16)
            sp.dma_start(wg[:], wg_d).then_inc(s("ld_moe"), 16)
            sp.dma_start(wu[:], wu_d).then_inc(s("ld_moe"), 16)
            sp.dma_start(wd[:], wd_d).then_inc(s("ld_moe"), 16)
            sp.dma_start(l1_w[:], l1_w_d).then_inc(s("ld_l1"), 16)
            sp.dma_start(gate1_w[:], gate1_d).then_inc(s("ld_l1"), 16)
            sp.dma_start(gate1_bias[:], gate1_bias_d.partition_broadcast(P)).then_inc(s("ld_l1"), 16)
            sp.dma_start(b1[:], b1_d).then_inc(s("ld_l1"), 16)
            sp.dma_start(b2[:], b2_d).then_inc(s("ld_l1"), 16)
            sp.dma_start(w2[:], w2_d).then_inc(s("ld_l1"), 16)
            for c in range(HC):
                sp.dma_start(w1[:, c], w1_d[0, :, c]).then_inc(s(f"ld_w1_{c}"), 16)
            with sp.Fori(0, E1 - 1) as e:
                for c in range(HC):
                    sp.wait_ge(s("ffn_up"), e * (B * HC) + (B - 1) * HC + c + 1)
                    sp.dma_start(w1[:, c], w1_d[bass.ds(e + 1, 1), :, c].rearrange("e p h -> (e p) h")).then_inc(s(f"ld_w1_{c}"), 16)
            ov = out_d.rearrange("b (j p) c -> p b j c", p=P)
            for b in range(B):
                sp.wait_ge(s("o_done"), b + 1)
                sp.dma_start(ov[:, b], x[:, b * TB:(b + 1) * TB, :]).then_inc(s("st_out"), 16)
            sp.wait_ge(s("st_out"), 16 * B)

        LD_SMALL, LD_MOE, LD_L1 = 16 * 5, 16 * 3, 16 * 6

        @block.gpsimd
        def _(pool):
            g = nc.gpsimd
            cdone = s("const")
            n = 0
            for k, abc in enumerate(POLAR):
                for m, v in enumerate(abc):
                    g.memset(coef[:, 3 * k + m:3 * k + m + 1], float(v)).then_inc(s("polar_const"), 1)
            g.memset(ones[:], 1.0).then_inc(cdone, 1)
            g.memset(ident[:], 0.0).then_inc(cdone, 1)
            g.memset(minus_half[:], -0.5).then_inc(cdone, 1)
            g.memset(tokens_n[:], float(N)).then_inc(cdone, 1)
            g.memset(xn[:, :, P:P + 1], 1.0).then_inc(cdone, 1)
            g.memset(head_mask[:], 1.0).then_inc(cdone, 1)
            g.memset(lane_sel[:], 0.0).then_inc(cdone, 1)
            g.memset(pair_sel[:], 0.0).then_inc(cdone, 1)
            g.memset(lane_mask[:], 1.0).then_inc(cdone, 1)
            n = 9
            for lane in range(LANES):
                g.memset(inv_lane[:, :, lane:lane + 1], 1.0 / (1 + lane)).then_inc(cdone, 1)
                n += 1
            g.memset(gcmp[:], 0.0).then_inc(cdone, 1)
            n += 1
            pool.wait_ge(cdone, n)
            g.affine_select(out=ident[:], in_=ident[:], compare_op=ALU.not_equal, fill=1.0, base=0,
                            pattern=[[-1, P]], channel_multiplier=1).then_inc(cdone, 1)
            n += 1
            hm = head_mask[:].rearrange("p (h d) -> p h d", h=HEADS)
            g.affine_select(out=hm, in_=hm, compare_op=ALU.is_ge, fill=0.0, base=0,
                            pattern=[[-HD, HEADS], [0, HD]], channel_multiplier=1).then_inc(cdone, 1)
            n += 1
            pool.wait_ge(cdone, n)
            g.affine_select(out=hm, in_=hm, compare_op=ALU.is_ge, fill=0.0, base=HD - 1,
                            pattern=[[HD, HEADS], [0, HD]], channel_multiplier=-1).then_inc(cdone, 1)
            n += 1
            g.affine_select(out=lane_mask[:], in_=lane_mask[:], compare_op=ALU.is_ge, fill=0.0, base=0,
                            pattern=[[-LD, LANES]], channel_multiplier=1).then_inc(cdone, 1)
            n += 1
            pool.wait_ge(cdone, n)
            g.affine_select(out=lane_mask[:], in_=lane_mask[:], compare_op=ALU.is_ge, fill=0.0, base=LD - 1,
                            pattern=[[LD, LANES]], channel_multiplier=-1).then_inc(cdone, 1)
            n += 1
            for part in range(3):
                v = pair_sel[part * E0:(part + 1) * E0]
                pool.wait_ge(cdone, n)
                g.affine_select(out=v, in_=v, compare_op=ALU.not_equal, fill=1.0, base=0,
                                pattern=[[-1, E0], [0, I0]], channel_multiplier=1).then_inc(cdone, 1)
                n += 1
            assert n == CONSTS
            pool.wait_ge(cdone, n)

            def rsqrt(out, in_, count, done):
                g.tensor_tensor(out, in_, minus_half[:, 0:count], ALU.pow).then_inc(done, 1)

            pool.wait_ge(s("polar_sum_cp"), 1)
            rsqrt(polar_r[:], polar_sum[:], 1, s("polar_r_done"))
            for b in range(B):
                pool.wait_ge(s("ln_var_done"), b + 1)
                rsqrt(ln_rstd[:, b * TB:(b + 1) * TB], ln_var[:, b * TB:(b + 1) * TB], TB, s("ln_pow"))
            for b in range(B):
                pool.wait_ge(s("at_var"), b + 1)
                rsqrt(ln_rstd[:, b * TB:(b + 1) * TB], ln_var[:, b * TB:(b + 1) * TB], TB, s("at_pow"))
            for b in range(B):
                pool.wait_ge(s("l1_var"), b + 1)
                rsqrt(ln_rstd[:, b * TB:(b + 1) * TB], ln_var[:, b * TB:(b + 1) * TB], TB, s("l1_pow"))
            pool.wait_ge(s("ld_small"), LD_SMALL)
            for b in range(B):
                g.tensor_scalar(xT[:, b, 0:PAD], ones[:, 0:1].broadcast_to([P, PAD]), cols[:, 3:4], 1.0,
                                ALU.mult, ALU.mult).then_inc(s("pad_done"), 1)

            def combine_inputs(k, b):
                pool.wait_ge(s("left_cp"), k + 1)
                g.tensor_tensor(prod[:, b % 2, 0], leftT[:, b], xT[:, b, PAD:PAD + N],
                                ALU.mult).then_inc(s("right_prod"), 1)
                g.tensor_tensor(sumT[:, b], leftT[:, b], xT[:, b, PAD:PAD + N],
                                ALU.add).then_inc(s("sum_done"), 1)

            def halve_mix(k, b):
                pool.wait_ge(s("mix_done"), k + 1)
                g.tensor_tensor(mix2[:, b % 2].rearrange("p j l m d -> p (j l) (m d)"),
                                mix[:, b % 2, :, :, 0:2].rearrange("p j l m d -> p (j l) (m d)"),
                                mix[:, b % 2, :, :, 2:4].rearrange("p j l m d -> p (j l) (m d)"),
                                ALU.add).then_inc(s("mix2_done"), 1)

            def rms_factor(k, b):
                pool.wait_ge(s("zms_done"), k + 1)
                g.tensor_tensor(z_rs[:, b % 2], z_ms[:, b % 2],
                                minus_half[:].rearrange("p (a b) -> p a b", a=TB), ALU.pow).then_inc(s("zpow_done"), 1)
                pool.wait_ge(s("zpow_done"), k + 1)
                g.tensor_tensor(z_r[:, b % 2], z_rs[:, b % 2], inv_lane[:], ALU.mult).then_inc(s("zr_done"), 1)

            def slot(k, b, first=True, second=True, third=True):
                if first:
                    combine_inputs(k, b)
                if third:
                    rms_factor(k - 2, (b - 2) % B)
                if second:
                    halve_mix(k - 1, (b - 1) % B)

            slot(0, 0, second=False, third=False)
            slot(1, 1, third=False)
            with pool.Fori(0, LEVELS - 1) as lev:
                for j in range(B):
                    slot(lev * B + (j + 2), (j + 2) % B)
            last = (LEVELS - 1) * B
            slot(last + 2, 2)
            slot(last + 3, 3)
            slot(last + 4, 0, first=False)
            slot(last + 5, 1, first=False, second=False)

        @block.tensor
        def _(pe):
            def mm(out, lhsT, rhs, start=True, stop=True):
                return nc.tensor.matmul(out, lhsT, rhs, start=start, stop=stop)

            def tr(out, in_, idm=None):
                return nc.tensor.transpose(out, in_, ident[:] if idm is None else idm)

            pe.wait_ge(s("const"), CONSTS)
            pe.wait_ge(s("polar_sq_done"), 1)
            mm(bank[7][:, 0:1], ones[:], polar_col[:]).then_inc(s("polar_sum_mm"), 1)

            for b in range(B):
                pe.wait_ge(s("ln_norm"), b + 1)
                if b == 3:
                    pe.wait_ge(s("polar_sum_cp"), 1)
                for j in range(TB):
                    last = tr(bank[4 + b][:, j * P:(j + 1) * P], xn[:, b * TB + j, 0:P])
                last.then_inc(s("xnT_mm"), 1)
            pe.wait_ge(s("ld_small"), LD_SMALL)
            pe.wait_ge(s("xnT_cp"), B)
            for t in range(NT):
                last = mm(bank[4][:, t * E0:(t + 1) * E0], xnT[:, t * P:(t + 1) * P], gate0_w[:])
            last.then_inc(s("logit_mm"), 1)

            for b in range(B):
                for j in range(TB):
                    mm(bank[b][:, 0:P + 1], xn[:, b * TB + j, 0:P], xn[:, b * TB + j, :], j == 0, j == TB - 1)
                for j in range(TB):
                    last = mm(bank[b][0:1, 256:256 + P], ones[:, 0:1], xn[:, b * TB + j, 0:P], j == 0, j == TB - 1)
                last.then_inc(s("gram_mm"), 1)
            pe.wait_ge(s("wfold"), 1)
            pe.wait_ge(s("sig_done"), 1)
            wv = attn_w[:, 3:5].rearrange("p k c -> p (k c)")
            for b in range(B):
                pe.wait_ge(s("gram_cp"), b + 1)
                mm(bank[4 + b][:, 0:256], gram[:, b, 0:P], wv, True, False)
                mm(bank[4 + b][:, 0:256], srow[:, b], rows[:, 256:512], False, True)
                mm(bank[4 + b][0:1, 256:512], gram[:, b, P:P + 1], wv, True, False)
                last = mm(bank[4 + b][0:1, 256:512], tokens_n[:], rows[:, 256:512], False, True)
                last.then_inc(s("m1_mm"), 1)
            for b in range(B):
                pe.wait_ge(s("m1_cp"), b + 1)
                for k in range(2):
                    mm(bank[b][:, k * P:(k + 1) * P], attn_w[:, 1 + k], m1[:, b, k * P:(k + 1) * P], True, False)
                    last = mm(bank[b][:, k * P:(k + 1) * P], rows[:, k * P:(k + 1) * P],
                              m1row[:, b, k * P:(k + 1) * P], False, True)
                last.then_inc(s("st_mm"), 1)
            for b in range(B):
                pe.wait_ge(s("st_cp"), b + 1)
                mm(bank[4 + b][:, 0:P], attn_w[:, 0], state[:, b])
                mm(bank[4 + b][0:1, P:2 * P], cols[:, 0:1], state[:, b]).then_inc(s("mq_mm"), 1)
            for b in range(B):
                pe.wait_ge(s("mq_cp"), b + 1)
                for j in range(TB):
                    mm(bank[b][:, j * P:(j + 1) * P], xnT[:, (b * TB + j) * P:(b * TB + j + 1) * P], mq[:, b],
                       True, False)
                    last = mm(bank[b][:, j * P:(j + 1) * P], ones[0:1, :], mqrow[:, b], False, True)
                last.then_inc(s("at_mm"), 1)
            pe.wait_ge(s("mq_cp"), B)
            mm(bank[4][0:1, 0:P], cols[:, 2:3], attn_w[:, 5]).then_inc(s("borow_mm"), 1)
            pe.wait_ge(s("borow_cp"), 1)
            for b in range(B):
                pe.wait_ge(s("parts_done"), 1)
                pe.wait_ge(s("wog_done"), 2)
                for j in range(TB):
                    t = b * TB + j
                    last = tr(bank[4 + b][:].bitcast(BF16)[0:3 * E0, j * P:(j + 1) * P],
                              gate0_parts[:, t].rearrange("p a e -> p (a e)"), ident_bf[:])
                last.then_inc(s("g0T_mm"), 1)
            for b in range(B):
                pe.wait_ge(s("at_norm"), b + 1)
                pe.wait_ge(s("g0T_cp"), b + 1)
                for j in range(TB):
                    last = tr(bank[4 + b][:, j * P:(j + 1) * P], attn_n[:, b * TB + j])
                last.then_inc(s("atT_mm"), 1)
            pe.wait_ge(s("wog_done"), 1)
            for b in range(B):
                pe.wait_ge(s("atT_cp"), b + 1)
                for j in range(TB):
                    t = b * TB + j
                    mm(bank[b][:, j * P:(j + 1) * P], attn_nT[:, t * P:(t + 1) * P], wo_g[:], True, False)
                    last = mm(bank[b][:, j * P:(j + 1) * P], ones[0:1, :], borow[:], False, True)
                last.then_inc(s("so_mm"), 1)

            pe.wait_ge(s("ld_moe"), LD_MOE)
            pe.wait_ge(s("polar_x0"), 1)
            pe.wait_ge(s("so_cp"), B)
            pe.wait_ge(s("atT_cp"), B)
            UNITS = PAIRS + 1
            with pe.Fori(0, B) as i:
                xin = xnT[:, bass.ds(i * N, N)]
                gin = gate0T[:, bass.ds(i * N, N)]

                def down(u):
                    pe.wait_ge(s("h0_done"), i * UNITS + (u + 1))
                    mm(bank[6][:], wd[:, u], h0[:, u % 2], u == 0, u == UNITS - 1).then_inc(s("dn_mm"), 1)

                def polar_products(q):
                    r, stage = divmod(q - 1, 5)
                    if q < 1 or r >= POLAR_PER_BATCH:
                        return
                    n = i * POLAR_PER_BATCH + r
                    if stage == 0:
                        if r > 0:
                            pe.wait_ge(s("polar_x_cp"), n)
                        mm(bank[7][:, 0:P], polar_x[:], polar_x[:])
                        tr(bank[7][:, P:2 * P], polar_x[:]).then_inc(s("polar_a_mm"), 1)
                    elif stage == 1:
                        pe.wait_ge(s("polar_ab_done"), n + 1)
                        mm(bank[7][:, 0:P], polar_gx[:, 0:P], polar_gx[:, 0:P]).then_inc(s("polar_a2_mm"), 1)
                    elif stage == 2:
                        pe.wait_ge(s("polar_b_done"), n + 1)
                        mm(bank[7][:, 0:P], polar_gx[:, P:2 * P], polar_b[:]).then_inc(s("polar_x_mm"), 1)

                for u in range(UNITS):
                    k = u % 2
                    if u >= 2:
                        pe.wait_ge(s("silu_done"), i * UNITS + (u - 1))
                    mm(bank[k][:], wg[:, u], xin).then_inc(s("g_mm"), 1)
                    if u >= 2:
                        pe.wait_ge(s("h0_done"), i * UNITS + (u - 1))
                    mm(bank[2 + k][:], wu[:, u], xin).then_inc(s("u_mm"), 1)
                    if u >= 1:
                        sel = pair_sel[:, 2 * (u - 1):2 * u].rearrange("p e i -> p (e i)")
                        mm(bank[4 + k][:], sel, gin).then_inc(s("gb_mm"), 1)
                        down(u - 1)
                    polar_products(u)
                down(UNITS - 1)
                pe.wait_ge(s("y0_silu"), i + 1)
                pe.wait_ge(s("polar_x_cp"), (i + 1) * POLAR_PER_BATCH)
                for j in range(TB):
                    last = tr(bank[7][:, j * P:(j + 1) * P], gl0T[:, j * P:(j + 1) * P])
                last.then_inc(s("y0T_mm"), 1)
                pe.wait_ge(s("sg_done"), i + 1)

            for b in range(B):
                pe.wait_ge(s("l1_norm"), b + 1)
                for j in range(TB):
                    last = tr(bank[4 + b][:, j * P:(j + 1) * P], xn[:, b * TB + j, 0:P])
                last.then_inc(s("x1T_mm"), 1)
            pe.wait_ge(s("ld_l1"), LD_L1)
            pe.wait_ge(s("x1T_cp"), B)
            for t in range(NT):
                last = mm(bank[0][:, t * E1:(t + 1) * E1], xnT[:, t * P:(t + 1) * P], gate1_w[:])
            last.then_inc(s("log1_mm"), 1)
            for b in range(B):
                mm(bank[4 + b][:], l1_w[:, 0], xnT[:, b * N:(b + 1) * N]).then_inc(s("up_mm"), 1)
            for b in range(B):
                if b == 3:
                    pe.wait_ge(s("dup_done"), 1)
                for j in range(TB):
                    t = b * TB + j
                    last = mm(bank[1 + b % 3][:, j * P:(j + 1) * P], xnT[:, t * P:(t + 1) * P], l1_w[:, 0])
                last.then_inc(s("uptok_mm"), 1)
            for b in range(B):
                pe.wait_ge(s("gate1_done"), 1)
                pe.wait_ge(s("up_cp"), b + 1)
                for j in range(TB):
                    last = tr(bank[4 + b][0:E1, j * P:(j + 1) * P], gate1[:, b * TB + j])
                last.then_inc(s("g1T_mm"), 1)
            pe.wait_ge(s("dup_done"), B)
            pe.wait_ge(s("log1_cp"), 1)
            for b in range(B):
                pe.wait_ge(s("g1T_cp"), b + 1)
                for j in range(TB):
                    t = b * TB + j
                    last = mm(bank[b][:, j * P:(j + 1) * P], gate1T[:, t * P:(t + 1) * P], b2[:])
                last.then_inc(s("acc_mm"), 1)

            pe.wait_ge(s("acc_cp"), B)

            def rotation(k, b, r):
                if r == 0:
                    pe.wait_ge(s("xtok_done"), k + 1)
                    pe.wait_ge(s("dup_done"), k + 1)
                    after(pe, s("rot_prod"), 3 * k - 1)
                elif r == 1:
                    after(pe, s("rot_prod"), 3 * k)
                elif r == 2:
                    pe.wait_ge(s("xT_cp"), k + 1)
                else:
                    pe.wait_ge(s("rot_prod"), 3 * k + 1)
                for j in range(TB):
                    last = tr(bank[r % 2][:, j * P:(j + 1) * P], x_tok[:, b, j, r * LD:r * LD + P])
                last.then_inc(s("rot_mm"), 1)

            def scores(k, b):
                pe.wait_ge(s("rot_prod"), 3 * k + 3)
                pe.wait_ge(s("right_prod"), k + 1)
                after(pe, s("ssub_done"), k)
                for j in range(TB):
                    for r in range(LANES):
                        last = mm(bank[3][:, j * 16:(j + 1) * 16], prod[:, b % 2, r, j * P:(j + 1) * P],
                                  lane_sel[:, r], r == 0, r == LANES - 1)
                last.then_inc(s("score_mm"), 1)

            def values(k, b):
                pe.wait_ge(s("sum_done"), k + 1)
                after(pe, s("mix_done"), k)
                for j in range(TB):
                    last = mm(bank[4][:, j * P:(j + 1) * P], sumT[:, b, j * P:(j + 1) * P], polar_x[:])
                last.then_inc(s("v_mm"), 1)

            def left_tokens(k, b):
                after(pe, s("xtok_done"), k + B)
                pe.wait_ge(s("left_cp"), k + 1)
                for j in range(TB):
                    last = tr(bank[2][:, j * P:(j + 1) * P], leftT[:, b, j * P:(j + 1) * P])
                last.then_inc(s("left_mm"), 1)

            def expert_up(e, blk, c):
                n = (e * B + blk) * HC + c
                if blk == 0:
                    pe.wait_ge(s(f"ld_w1_{c}"), e * 16 + 16)
                if c >= 2:
                    pe.wait_ge(s("ffn_relu"), n - 1)
                mm(bank[5 + c % 2][:], w1[:, c], xnT[:, blk * N:(blk + 1) * N]).then_inc(s("ffn_up"), 1)

            def expert_down(e, blk):
                n = e * B + blk
                pe.wait_ge(s("ffn_relu"), (n + 1) * HC)
                for j in range(TB):
                    for c in range(HC):
                        last = mm(bank[7][:, j * P:(j + 1) * P], hT[:, c, j * P:(j + 1) * P],
                                  w2[:, bass.ds(e, 1), c].rearrange("p e o -> p (e o)"), c == 0, c == HC - 1)
                last.then_inc(s("ffn_down"), 1)

            def slot(k, b, first=True, third=True, ahead=True, expert=None):
                if first:
                    rotation(k, b, 3)
                if expert:
                    expert_up(*expert, 0)
                    expert_up(*expert, 1)
                if first:
                    scores(k, b)
                if expert:
                    expert_up(*expert, 2)
                    expert_up(*expert, 3)
                if third:
                    left_tokens(k - 2, (b - 2) % B)
                if ahead:
                    rotation(k + 1, (b + 1) % B, 0)
                if expert:
                    expert_down(*expert)
                if ahead:
                    rotation(k + 1, (b + 1) % B, 1)
                    rotation(k + 1, (b + 1) % B, 2)
                if first:
                    values(k, b)

            for r in range(3):
                rotation(0, 0, r)
            slot(0, 0, third=False)
            slot(1, 1, third=False)
            with pe.Fori(0, LEVELS - 1) as lev:
                for j in range(B):
                    slot(lev * B + (j + 2), (j + 2) % B, expert=(lev, j))
            last_k = (LEVELS - 1) * B
            slot(last_k + 2, 2)
            slot(last_k + 3, 3, ahead=False)
            slot(last_k + 4, 0, first=False, ahead=False)
            slot(last_k + 5, 1, first=False, ahead=False)

            pe.wait_ge(s("mix_done"), LEVELS * B)
            pe.wait_ge(s("ffn_acc"), E1 * B * TB)
            pe.wait_ge(s("ssub_done"), LEVELS * B)
            pe.wait_ge(s("rot_prod"), 3 * LEVELS * B)
            pe.wait_ge(s("xtok_done"), (LEVELS + 1) * B)
            for b in range(B):
                for j in range(TB):
                    last = tr(bank[b][:, j * P:(j + 1) * P], x_tok[:, b, j, 0:P])
                last.then_inc(s("rot_mm"), 1)
                mm(bank[4 + b][:], l1_w[:, 1], xnT[:, b * N:(b + 1) * N]).then_inc(s("v1_mm"), 1)
            for b in range(B):
                pe.wait_ge(s("qv_done"), b + 1)
                for j in range(TB):
                    last = mm(bank[b][:, j * P:(j + 1) * P], qvT[:, b, j * P:(j + 1) * P], l1_w[:, 2])
                last.then_inc(s("yp_mm"), 1)

        @block.scalar
        def _(act):
            a = nc.scalar
            act.wait_ge(s("ld_scan"), 16)
            a.activation(polar_sq[:], polar_x[:], ACT.Square, accum_out=polar_col[:]).then_inc(s("polar_sq_done"), 1)
            act.wait_ge(s("polar_sum_mm"), 1)
            a.copy(polar_sum[:], bank[7][:, 0:1]).then_inc(s("polar_sum_cp"), 1)
            for b in range(B):
                act.wait_ge(s("xnT_mm"), b + 1)
                a.copy(xnT[:, b * N:(b + 1) * N], bank[4 + b][:]).then_inc(s("xnT_cp"), 1)
            act.wait_ge(s("logit_mm"), 1)
            a.activation(scores0[:].rearrange("p t e -> p (t e)"), bank[4][:], ACT.Sigmoid).then_inc(s("sig_done"), 1)
            for b in range(B):
                act.wait_ge(s("gram_mm"), b + 1)
                a.copy(gram[:, b], bank[b][:, 0:P + 1])
                a.copy(srow[:, b], bank[b][0:1, 256:256 + P]).then_inc(s("gram_cp"), 1)
            for b in range(B):
                act.wait_ge(s("mq_mm"), b + 1)
                a.copy(mq[:, b], bank[4 + b][:, 0:P])
                a.copy(mqrow[:, b], bank[4 + b][0:1, P:2 * P]).then_inc(s("mq_cp"), 1)
            for b in range(B):
                act.wait_ge(s("g0T_mm"), b + 1)
                a.copy(gate0T[:, b * N:(b + 1) * N], bank[4 + b][:].bitcast(BF16)[0:3 * E0, 0:N]).then_inc(s("g0T_cp"), 1)
            for b in range(B):
                act.wait_ge(s("atT_mm"), b + 1)
                a.copy(attn_nT[:, b * N:(b + 1) * N], bank[4 + b][:]).then_inc(s("atT_cp"), 1)
            for b in range(B):
                act.wait_ge(s("so_mm"), b + 1)
                a.copy(s_tok[:, b * TB:(b + 1) * TB].rearrange("p j c -> p (j c)"), bank[b][:]).then_inc(s("so_cp"), 1)

            UNITS = PAIRS + 1
            with act.Fori(0, B) as i:
                for u in range(UNITS):
                    act.wait_ge(s("g_mm"), i * UNITS + (u + 1))
                    if u == 2:
                        act.wait_ge(s("h0_done"), i * UNITS + 1)
                    elif u > 2:
                        act.wait_ge(s("gu_done"), i * PAIRS + (u - 2))
                    a.activation(silu_g[:, u % 2], bank[u % 2][:], ACT.Silu).then_inc(s("silu_done"), 1)
                act.wait_ge(s("dn_mm"), (i + 1) * UNITS)
                a.activation(gl0T[:], bank[6][:], ACT.Silu).then_inc(s("y0_silu"), 1)

            for b in range(B):
                act.wait_ge(s("x1T_mm"), b + 1)
                a.copy(xnT[:, b * N:(b + 1) * N], bank[4 + b][:]).then_inc(s("x1T_cp"), 1)
            act.wait_ge(s("lsub_done"), 1)
            a.activation(lexp[:], lsub[:], ACT.Exp).then_inc(s("lexp_done"), 1)
            for b in range(B):
                act.wait_ge(s("up_mm"), b + 1)
                a.copy(xT[:, b, PAD:PAD + N], bank[4 + b][:]).then_inc(s("up_cp"), 1)
            for b in range(B):
                act.wait_ge(s("uptok_mm"), b + 1)
                src = bank[1 + b % 3][:].rearrange("p (j c) -> p j c", j=TB)
                a.copy(x_tok[:, b, :, 0:P], src).then_inc(s("xtok_done"), 1)
                a.copy(x_tok[:, b, :, P:P + 3 * LD], src[:, :, 0:3 * LD]).then_inc(s("dup_done"), 1)
            for b in range(B):
                act.wait_ge(s("g1T_mm"), b + 1)
                a.copy(gate1T[:, b * N:(b + 1) * N], bank[4 + b][0:E1, :]).then_inc(s("g1T_cp"), 1)
            for b in range(B):
                act.wait_ge(s("acc_mm"), b + 1)
                a.copy(acc[:, b * TB:(b + 1) * TB].rearrange("p j c -> p (j c)"), bank[b][:]).then_inc(s("acc_cp"), 1)

            act.wait_ge(s("pad_done"), B)

            def state_in(k, b, lev):
                after(act, s("rot_mm"), 4 * k + 1)
                a.copy(xT[:, b, PAD:PAD + N], bank[0][:]).then_inc(s("xT_cp"), 1)
                act.wait_ge(s("xT_cp"), k + 1)
                a.copy(leftT[:, b], xT[:, b, bass.ds(PAD - (1 << lev), N)]).then_inc(s("left_cp"), 1)

            def expo(k, b):
                act.wait_ge(s("ssub_done"), k + 1)
                a.activation(sexp[:, b % 2], ssub[:, b % 2], ACT.Exp, scale=float(LD) ** -0.5).then_inc(s("sexp_done"), 1)

            def square(k, b):
                act.wait_ge(s("z_done"), k + 1)
                a.activation(z_sq[:, b % 2], z[:, b % 2], ACT.Square).then_inc(s("zsq_done"), 1)

            def relu(e, blk, c):
                n = (e * B + blk) * HC + c
                act.wait_ge(s("ffn_up"), n + 1)
                a.activation(hT[:, c], bank[5 + c % 2][:], ACT.Relu, bias=b1_now[:, c:c + 1]).then_inc(s("ffn_relu"), 1)

            def dup(k, b):
                act.wait_ge(s("xtok_done"), B + k + 1)
                a.copy(x_tok[:, b, :, P:P + 3 * LD], x_tok[:, b, :, 0:3 * LD]).then_inc(s("dup_done"), 1)

            def slot(k, b, lev_next, second=True, third=True, ahead=True, expert=None):
                if expert:
                    if expert[1] == 0:
                        a.copy(b1_now[:], b1[:, bass.ds(expert[0], 1)].rearrange("p e c -> p (e c)")).then_inc(s("b1_now_done"), 1)
                        act.wait_ge(s("b1_now_done"), expert[0] + 1)
                    relu(*expert, 0)
                if third:
                    square(k - 2, (b - 2) % B)
                if expert:
                    relu(*expert, 1)
                if second:
                    expo(k - 1, (b - 1) % B)
                if expert:
                    relu(*expert, 2)
                    relu(*expert, 3)
                if ahead:
                    state_in(k + 1, (b + 1) % B, lev_next)
                if third:
                    dup(k - 2, (b - 2) % B)

            state_in(0, 0, 0)
            slot(0, 0, 0, second=False, third=False)
            slot(1, 1, 0, third=False)
            with act.Fori(0, LEVELS - 1) as lev:
                for j in range(B):
                    slot(lev * B + (j + 2), (j + 2) % B, lev if j == 0 else lev + 1, expert=(lev, j))
            top = LEVELS - 1
            slot(top * B + 2, 2, top)
            slot(top * B + 3, 3, top, ahead=False)
            slot(top * B + 4, 0, top, ahead=False)
            slot(top * B + 5, 1, top, second=False, ahead=False)

            for b in range(B):
                act.wait_ge(s("v1_mm"), b + 1)
                a.copy(sumT[:, b], bank[4 + b][:]).then_inc(s("v1_cp"), 1)
            act.wait_ge(s("ffn_acc"), E1 * B * TB)
            for b in range(B):
                a.activation(acc[:, b * TB:(b + 1) * TB], acc[:, b * TB:(b + 1) * TB], ACT.Silu).then_inc(s("gl1_done"), 1)

        @block.vector
        def _(dve):
            v = nc.vector
            tt, ts, stt = v.tensor_tensor, v.tensor_scalar, v.scalar_tensor_tensor

            def layer_norm(b, src_tile, out_tile, stat, var, pow_, norm):
                t0 = b * TB
                for j in range(TB):
                    last = v.bn_stats(ln_stats[:, t0 + j], src_tile(t0 + j))
                last.then_inc(s(stat), 1)
                dve.wait_ge(s(stat), 2 * b + 1)
                for j in range(TB):
                    last = v.bn_aggr(ln_mv[:, t0 + j], ln_stats[:, t0 + j])
                last.then_inc(s(stat), 1)
                dve.wait_ge(s(stat), 2 * b + 2)
                ts(ln_var[:, t0:t0 + TB], ln_mv[:, t0:t0 + TB, 1], LN_EPS, None, ALU.add).then_inc(s(var), 1)

            def normalise(b, src_tile, out_tile, pow_, norm):
                t0 = b * TB
                dve.wait_ge(s(pow_), b + 1)
                for j in range(TB):
                    last = ts(out_tile(t0 + j), src_tile(t0 + j), ln_mv[:, t0 + j, 0:1], ln_rstd[:, t0 + j:t0 + j + 1],
                              ALU.subtract, ALU.mult)
                last.then_inc(s(norm), 1)

            for b in range(B):
                dve.wait_ge(s(f"ld_x{b}"), 16)
                layer_norm(b, lambda t: x[:, t], None, "ln_stat", "ln_var_done", None, None)
                if b >= 1:
                    normalise(b - 1, lambda t: x[:, t], lambda t: xn[:, t, 0:P], "ln_pow", "ln_norm")
            normalise(B - 1, lambda t: x[:, t], lambda t: xn[:, t, 0:P], "ln_pow", "ln_norm")
            dve.wait_ge(s("const"), CONSTS)
            dve.wait_ge(s("ld_small"), LD_SMALL)
            tt(attn_w[:, 0:5], attn_w[:, 0:5], ident[:].unsqueeze(1).broadcast_to([P, 5, P]), ALU.add).then_inc(s("wfold"), 1)
            ts(wo_g[:], attn_w[:, 5], cols[:, 1:2], None, ALU.mult).then_inc(s("wog_done"), 1)
            for r in range(LANES):
                split = LANES - r
                v.tensor_copy(lane_sel[:, r, r:r + 5 * (split - 1) + 1:5], lane_mask[:, 0:split])
                if r:
                    v.tensor_copy(lane_sel[:, r, 5 * split + r - 4:5 * 3 + r - 4 + 1:5], lane_mask[:, split:])
            v.tensor_copy(ident_bf[:], ident[:]).then_inc(s("wog_done"), 1)
            dve.wait_ge(s("polar_r_done"), 1)
            ts(polar_x[:], polar_x[:], polar_r[:], None, ALU.mult).then_inc(s("polar_x0"), 1)

            def m1_out(b):
                dve.wait_ge(s("m1_mm"), b + 1)
                v.tensor_copy(m1[:, b], bank[4 + b][:, 0:256])
                v.tensor_copy(m1row[:, b], bank[4 + b][0:1, 256:512]).then_inc(s("m1_cp"), 1)

            def state_out(b):
                dve.wait_ge(s("st_mm"), b + 1)
                stt(state0[:, b], bank[b][:, 0:P], 1.0 / (N * N), head_mask[:], ALU.mult, ALU.mult).then_inc(s("st0_cp"), 1)

            def state_out2(b):
                dve.wait_ge(s("st0_cp"), b + 1)
                tt(state[:, b], state0[:, b], bank[b][:, P:2 * P], ALU.mult).then_inc(s("st_cp"), 1)

            for b in range(B):
                m1_out(b)
            for b in range(B):
                state_out(b)
                state_out2(b)

            dve.wait_ge(s("sig_done"), 1)
            tt(choice[:], scores0[:], gate0_bias[:].unsqueeze(1).broadcast_to([P, NT, E0]), ALU.add).then_inc(s("choice_done"), 1)
            dve.wait_ge(s("choice_done"), 1)
            for t in range(NT):
                for gr in range(GROUPS):
                    last = v.max(top8[:, t, gr], choice[:, t, gr * GE:(gr + 1) * GE])
            last.then_inc(s("gtop"), 1)
            dve.wait_ge(s("gtop"), 1)
            tt(gscore[:], top8[:, :, :, 0], top8[:, :, :, 1], ALU.add).then_inc(s("gsum"), 1)
            dve.wait_ge(s("gsum"), 1)
            for g_ in range(GROUPS):
                me = gscore[:, :, g_:g_ + 1]
                if g_ > 0:
                    last = tt(gcmp[:, :, g_, 0:g_], gscore[:, :, 0:g_], me.broadcast_to([P, NT, g_]), ALU.is_ge)
                if g_ < GROUPS - 1:
                    last = tt(gcmp[:, :, g_, g_ + 1:], gscore[:, :, g_ + 1:], me.broadcast_to([P, NT, GROUPS - 1 - g_]), ALU.is_gt)
            last.then_inc(s("gcmp_done"), 1)
            dve.wait_ge(s("gcmp_done"), 1)
            v.tensor_reduce(grank[:], gcmp[:], AX_X, ALU.add).then_inc(s("grank_done"), 1)
            dve.wait_ge(s("grank_done"), 1)
            ts(gmask[:], grank[:], 2.0, None, ALU.is_lt).then_inc(s("gmask_done"), 1)
            dve.wait_ge(s("gmask_done"), 1)
            tt(masked[:].rearrange("p t (g e) -> p t g e", g=GROUPS), choice[:].rearrange("p t (g e) -> p t g e", g=GROUPS),
               gmask[:].unsqueeze(3).broadcast_to([P, NT, GROUPS, GE]), ALU.mult).then_inc(s("masked_done"), 1)
            dve.wait_ge(s("masked_done"), 1)
            for t in range(NT):
                last = v.max(best8[:, t], masked[:, t])
            last.then_inc(s("best_done"), 1)
            dve.wait_ge(s("best_done"), 1)
            for t in range(NT):
                last = v.match_replace(replaced[:, t], best8[:, t], masked[:, t], FAR)
            last.then_inc(s("repl_done"), 1)
            dve.wait_ge(s("repl_done"), 1)
            ts(taken[:], replaced[:], FAR, None, ALU.is_equal).then_inc(s("taken_done"), 1)
            dve.wait_ge(s("taken_done"), 1)
            tt(gate0[:], taken[:], scores0[:], ALU.mult).then_inc(s("wraw_done"), 1)
            dve.wait_ge(s("wraw_done"), 1)
            v.tensor_reduce(wsum[:], gate0[:], AX_X, ALU.add).then_inc(s("wsum_done"), 1)
            dve.wait_ge(s("wsum_done"), 1)
            ts(wsum_eps[:], wsum[:], 1e-20, None, ALU.add).then_inc(s("wsume_done"), 1)
            dve.wait_ge(s("wsume_done"), 1)
            v.reciprocal(wrec[:], wsum_eps[:]).then_inc(s("wrec_done"), 1)
            dve.wait_ge(s("wrec_done"), 1)
            stt(gate0_rest[:], gate0[:], ROUTED, wrec[:].unsqueeze(2).broadcast_to([P, NT, E0]), ALU.mult, ALU.mult).then_inc(s("gate0_done"), 1)
            dve.wait_ge(s("gate0_done"), 1)
            v.tensor_copy(gate0_parts[:, :, 0], gate0_rest[:]).then_inc(s("hi_done"), 1)
            dve.wait_ge(s("hi_done"), 1)
            tt(gate0_rest2[:], gate0_rest[:], gate0_parts[:, :, 0], ALU.subtract).then_inc(s("rest_done"), 1)
            dve.wait_ge(s("rest_done"), 1)
            v.tensor_copy(gate0_parts[:, :, 1], gate0_rest2[:]).then_inc(s("mid_done"), 1)
            dve.wait_ge(s("mid_done"), 1)
            tt(gate0_parts[:, :, 2], gate0_rest2[:], gate0_parts[:, :, 1], ALU.subtract).then_inc(s("parts_done"), 1)

            attn_tile = lambda t: bank[t // TB][:, (t % TB) * P:(t % TB + 1) * P]
            for b in range(B):
                dve.wait_ge(s("at_mm"), b + 1)
                layer_norm(b, attn_tile, None, "at_stat", "at_var", None, None)
                if b >= 1:
                    normalise(b - 1, attn_tile, lambda t: attn_n[:, t], "at_pow", "at_norm")
            normalise(B - 1, attn_tile, lambda t: attn_n[:, t], "at_pow", "at_norm")
            dve.wait_ge(s("borow_mm"), 1)
            tt(borow[:], bank[4][0:1, 0:P], rows[:, 4 * P:5 * P], ALU.add).then_inc(s("borow_cp"), 1)

            UNITS = PAIRS + 1
            dve.wait_ge(s("polar_const"), 3 * len(POLAR))
            dve.wait_ge(s("polar_x0"), 1)
            with dve.Fori(0, B) as i:
                def polar_step(q):
                    r, stage = divmod(q - 1, 5)
                    if q < 1 or r >= POLAR_PER_BATCH:
                        return
                    n = i * POLAR_PER_BATCH + r

                    def co(m):
                        return coef[:, bass.ds(n * 3 + m, 1)]
                    if stage == 0:
                        ts(polar_ai[:], ident[:], co(0), None, ALU.mult).then_inc(s("polar_ai_done"), 1)
                        dve.wait_ge(s("polar_a_mm"), n + 1)
                        v.tensor_copy(polar_gx[:], bank[7][:, 0:256]).then_inc(s("polar_gx_cp"), 1)
                        dve.wait_ge(s("polar_gx_cp"), n + 1)
                        stt(polar_ab[:], polar_gx[:, 0:P], co(1), polar_ai[:], ALU.mult, ALU.add).then_inc(s("polar_ab_done"), 1)
                    elif stage == 1:
                        dve.wait_ge(s("polar_a2_mm"), n + 1)
                        dve.wait_ge(s("polar_ab_done"), n + 1)
                        stt(polar_b[:], bank[7][:, 0:P], co(2), polar_ab[:], ALU.mult, ALU.add).then_inc(s("polar_b_done"), 1)
                    elif stage == 2:
                        dve.wait_ge(s("polar_x_mm"), n + 1)
                        v.tensor_copy(polar_x[:], bank[7][:, 0:P]).then_inc(s("polar_x_cp"), 1)

                for u in range(UNITS):
                    k = u % 2
                    dve.wait_ge(s("silu_done"), i * UNITS + (u + 1))
                    dve.wait_ge(s("u_mm"), i * UNITS + (u + 1))
                    if u >= 2:
                        dve.wait_ge(s("dn_mm"), i * UNITS + (u - 1))
                    if u == 0:
                        tt(h0[:, k], silu_g[:, k], bank[2 + k][:], ALU.mult).then_inc(s("h0_done"), 1)
                    else:
                        tt(silu_gu[:, k], silu_g[:, k], bank[2 + k][:], ALU.mult).then_inc(s("gu_done"), 1)
                        dve.wait_ge(s("gu_done"), i * PAIRS + u)
                        dve.wait_ge(s("gb_mm"), i * PAIRS + u)
                        tt(h0[:, k], silu_gu[:, k], bank[4 + k][:], ALU.mult).then_inc(s("h0_done"), 1)
                    polar_step(u)
                dve.wait_ge(s("y0T_mm"), i + 1)
                tt(sg[:], s_tok[:, bass.ds(i * TB, TB)].rearrange("p j c -> p (j c)"), bank[7][:], ALU.mult).then_inc(s("sg_done"), 1)
                dve.wait_ge(s("sg_done"), i + 1)
                xi = x[:, bass.ds(i * TB, TB)].rearrange("p j c -> p (j c)")
                tt(xi, xi, sg[:], ALU.add).then_inc(s("x1_done"), 1)

            dve.wait_ge(s("x1_done"), B)
            for b in range(B):
                layer_norm(b, lambda t: x[:, t], None, "l1_stat", "l1_var", None, None)
                if b >= 1:
                    normalise(b - 1, lambda t: x[:, t], lambda t: xn[:, t, 0:P], "l1_pow", "l1_norm")
            normalise(B - 1, lambda t: x[:, t], lambda t: xn[:, t, 0:P], "l1_pow", "l1_norm")
            dve.wait_ge(s("log1_mm"), 1)
            tt(logits1[:], bank[0][:, 0:NT * E1].rearrange("p (t e) -> p t e", t=NT),
               gate1_bias[:].unsqueeze(1).broadcast_to([P, NT, E1]), ALU.add).then_inc(s("log1_cp"), 1)
            dve.wait_ge(s("log1_cp"), 1)
            v.tensor_reduce(lmax[:], logits1[:], AX_X, ALU.max).then_inc(s("lmax_done"), 1)
            dve.wait_ge(s("lmax_done"), 1)
            tt(lsub[:], logits1[:], lmax[:].unsqueeze(2).broadcast_to([P, NT, E1]), ALU.subtract).then_inc(s("lsub_done"), 1)
            v.memset(ecmp[:], 0.0).then_inc(s("ecmp0"), 1)
            dve.wait_ge(s("ecmp0"), 1)
            for e in range(E1):
                me = logits1[:, :, e:e + 1]
                if e > 0:
                    last = tt(ecmp[:, :, e, 0:e], logits1[:, :, 0:e], me.broadcast_to([P, NT, e]), ALU.is_ge)
                if e < E1 - 1:
                    last = tt(ecmp[:, :, e, e + 1:], logits1[:, :, e + 1:], me.broadcast_to([P, NT, E1 - 1 - e]), ALU.is_gt)
            last.then_inc(s("ecmp_done"), 1)
            dve.wait_ge(s("ecmp_done"), 1)
            v.tensor_reduce(erank[:], ecmp[:], AX_X, ALU.add).then_inc(s("erank_done"), 1)
            dve.wait_ge(s("lexp_done"), 1)
            v.tensor_reduce(lsum[:], lexp[:], AX_X, ALU.add).then_inc(s("lsum_done"), 1)
            dve.wait_ge(s("erank_done"), 1)
            ts(emask[:], erank[:], 2.0, None, ALU.is_lt).then_inc(s("emask_done"), 1)
            dve.wait_ge(s("lsum_done"), 1)
            v.reciprocal(lrec[:], lsum[:]).then_inc(s("lrec_done"), 1)
            dve.wait_ge(s("lrec_done"), 1)
            tt(probs1[:], lexp[:], lrec[:].unsqueeze(2).broadcast_to([P, NT, E1]), ALU.mult).then_inc(s("probs_done"), 1)
            dve.wait_ge(s("probs_done"), 1)
            dve.wait_ge(s("emask_done"), 1)
            tt(gate1[:], probs1[:], emask[:], ALU.mult).then_inc(s("gate1_done"), 1)
            dve.wait_ge(s("gate1_done"), 1)
            dve.wait_ge(s("acc_cp"), B)

            def products(k, b):
                dve.wait_ge(s("left_cp"), k + 1)
                for r in range(1, LANES):
                    dve.wait_ge(s("rot_mm"), 4 * k + r + 1)
                    tt(prod[:, b % 2, r], leftT[:, b], bank[r % 2][:], ALU.mult).then_inc(s("rot_prod"), 1)

            def add_lanes(k, b):
                dve.wait_ge(s("mix2_done"), k + 1)
                m = mix2[:, b % 2].rearrange("p j l m d -> p (j l) m d")
                tt(z[:, b % 2].rearrange("p j (l d) -> p (j l) d", l=LANES), m[:, :, 0], m[:, :, 1],
                   ALU.add).then_inc(s("z_done"), 1)

            def softmax_shift(k, b):
                dve.wait_ge(s("score_mm"), k + 1)
                sc = bank[3][:, 0:TB * 16].rearrange("p (j l m) -> p j l m", j=TB, l=LANES)
                v.tensor_reduce(smax[:, b % 2], sc, AX_X, ALU.max).then_inc(s("smax_done"), 1)
                dve.wait_ge(s("smax_done"), k + 1)
                tt(ssub[:, b % 2], sc, smax[:, b % 2].unsqueeze(3).broadcast_to([P, TB, LANES, LANES]),
                   ALU.subtract).then_inc(s("ssub_done"), 1)

            def mean_square(k, b):
                dve.wait_ge(s("zsq_done"), k + 1)
                v.tensor_reduce(z_ss[:, b % 2], z_sq[:, b % 2].rearrange("p j (l d) -> p j l d", l=LANES), AX_X,
                                ALU.add).then_inc(s("zss_done"), 1)
                stt(eps_ss[:, b % 2], ssum[:, b % 2], RMS_EPS, ssum[:, b % 2], ALU.mult, ALU.mult).then_inc(s("epsss_done"), 1)
                dve.wait_ge(s("epsss_done"), k + 1)
                dve.wait_ge(s("zss_done"), k + 1)
                stt(z_ms[:, b % 2], z_ss[:, b % 2], 1.0 / LD, eps_ss[:, b % 2], ALU.mult, ALU.add).then_inc(s("zms_done"), 1)

            def mix_values(k, b):
                dve.wait_ge(s("sexp_done"), k + 1)
                v.tensor_reduce(ssum[:, b % 2], sexp[:, b % 2], AX_X, ALU.add).then_inc(s("ssum_done"), 1)
                dve.wait_ge(s("v_mm"), k + 1)
                tt(mix[:, b % 2], sexp[:, b % 2].unsqueeze(4).broadcast_to([P, TB, LANES, LANES, LD]),
                   bank[4][:].rearrange("p (j m d) -> p j m d", j=TB, m=LANES).unsqueeze(2).broadcast_to([P, TB, LANES, LANES, LD]),
                   ALU.mult).then_inc(s("mix_done"), 1)
                dve.wait_ge(s("ssum_done"), k + 1)

            def new_state(k, b):
                dve.wait_ge(s("zr_done"), k + 1)
                after(dve, s("xtok_done"), B + k)
                tt(zn[:].rearrange("p j (l d) -> p j l d", l=LANES), z[:, b % 2].rearrange("p j (l d) -> p j l d", l=LANES),
                   z_r[:, b % 2].unsqueeze(3).broadcast_to([P, TB, LANES, LD]), ALU.mult).then_inc(s("zn_done"), 1)
                dve.wait_ge(s("zn_done"), k + 1)
                dve.wait_ge(s("left_mm"), k + 1)
                dve.wait_ge(s("rot_mm"), 4 * k + 4)
                tt(x_tok[:, b, :, 0:P], zn[:], bank[2][:].rearrange("p (j c) -> p j c", j=TB),
                   ALU.add).then_inc(s("xtok_done"), 1)

            def expert_sum(e, blk):
                n = e * B + blk
                dve.wait_ge(s("ffn_down"), n + 1)
                if blk == 0:
                    v.tensor_copy(gate1_now[:], gate1[:, :, bass.ds(e, 1)].rearrange("p t e -> p (t e)")).then_inc(s("gate_now_done"), 1)
                    dve.wait_ge(s("gate_now_done"), e + 1)
                for j in range(TB):
                    t = blk * TB + j
                    stt(acc[:, t], bank[7][:, j * P:(j + 1) * P], gate1_now[:, t:t + 1], acc[:, t],
                        ALU.mult, ALU.add).then_inc(s("ffn_acc"), 1)

            def slot(k, b, first=True, second=True, third=True, expert=None):
                if first:
                    products(k, b)
                if third:
                    add_lanes(k - 2, (b - 2) % B)
                if second:
                    softmax_shift(k - 1, (b - 1) % B)
                if third:
                    mean_square(k - 2, (b - 2) % B)
                if second:
                    mix_values(k - 1, (b - 1) % B)
                if third:
                    new_state(k - 2, (b - 2) % B)
                if expert:
                    expert_sum(*expert)

            slot(0, 0, second=False, third=False)
            slot(1, 1, third=False)
            with dve.Fori(0, LEVELS - 1) as lev:
                for j in range(B):
                    slot(lev * B + (j + 2), (j + 2) % B, expert=(lev, j))
            top = (LEVELS - 1) * B
            slot(top + 2, 2)
            slot(top + 3, 3)
            slot(top + 4, 0, first=False)
            slot(top + 5, 1, first=False, second=False)

            for b in range(B):
                dve.wait_ge(s("v1_cp"), b + 1)
                dve.wait_ge(s("rot_mm"), 4 * LEVELS * B + b + 1)
                tt(qvT[:, b], sumT[:, b], bank[b][:], ALU.mult).then_inc(s("qv_done"), 1)
            for b in range(B):
                dve.wait_ge(s("yp_mm"), b + 1)
                dve.wait_ge(s("gl1_done"), b + 1)
                gb = acc[:, b * TB:(b + 1) * TB].rearrange("p j c -> p (j c)")
                tt(gb, bank[b][:], gb, ALU.mult).then_inc(s("o_mul"), 1)
                dve.wait_ge(s("o_mul"), b + 1)
                xb = x[:, b * TB:(b + 1) * TB].rearrange("p j c -> p (j c)")
                tt(xb, xb, gb, ALU.add).then_inc(s("o_done"), 1)


_OUT_SHAPE = (B, N, P)


def kernel(**inputs):
    import numpy as np
    import concourse.bacc as bacc
    from concourse.bass_utils import run_bass_kernel_spmd as run

    w = {k: np.asarray(v) for k, v in inputs.items()}
    swap = lambda m: np.swapaxes(m, -1, -2)

    def experts_in(shared, experts):
        rows = np.concatenate([shared, experts.reshape(E0 * I0, P)]).reshape(PAIRS + 1, P, P)
        return rows.transpose(2, 0, 1)

    down = np.concatenate([swap(w["L0_ffn_shared_down"])[None],
                           swap(w["L0_ffn_expert_down"]).reshape(PAIRS, P, P)])
    arrays = {
        "x": w["L0_attn_x"],
        "cols": np.stack([w["L0_attn_bq"], w["L0_attn_ln_g"], w["L0_attn_ln_b"], w["L1_attn_identity"]], 1),
        "rows": np.concatenate([w["L0_attn_bk"].reshape(-1), w["L0_attn_bv"].reshape(-1), w["L0_attn_bo"]])[None],
        "gate0_bias": w["L0_ffn_gate_bias"],
        "gate1_bias": w["L1_ffn_gate_b"],
        "attn_w": np.stack([swap(w["L0_attn_Wq"]), *w["L0_attn_Wk"], *w["L0_attn_Wv"], w["L0_attn_Wo"]], 1),
        "gate0": swap(w["L0_ffn_gate_w"]),
        "wg": experts_in(w["L0_ffn_shared_gate"], w["L0_ffn_expert_gate"]),
        "wu": experts_in(w["L0_ffn_shared_up"], w["L0_ffn_expert_up"]),
        "wd": down.transpose(1, 0, 2),
        "scan_raw": w["L1_attn_W_scan_raw"],
        "l1_w": np.stack([swap(w["L1_attn_W_up"]), swap(w["L1_attn_W_v"]), swap(w["L1_attn_W_proj"])], 1),
        "gate1": swap(w["L1_ffn_gate_w"]),
        "w1": w["L1_ffn_w1"].reshape(E1, P, HC, P),
        "b1": w["L1_ffn_b1"].reshape(E1, HC, P).transpose(2, 0, 1),
        "w2": w["L1_ffn_w2"].reshape(E1, HC, P, P).transpose(2, 0, 1, 3),
        "b2": w["L1_ffn_b2"],
    }
    nc = bacc.Bacc("TRN2", target_bir_lowering=False, num_devices=1)
    feed, args = {}, []
    for name, value in arrays.items():
        value = np.ascontiguousarray(value)
        feed[f"in_{name}"] = value
        args.append(nc.dram_tensor(f"in_{name}", value.shape, mybir.dt.from_np(value.dtype), kind="ExternalInput").ap())
    args.append(nc.dram_tensor("out", _OUT_SHAPE, F32, kind="ExternalOutput").ap())
    build(nc, *args)
    return run(nc, [feed], core_ids=[0]).results[0]["out"]
```

```python
from contextlib import ExitStack

import numpy as np
import concourse.bass as bass
from concourse import mybir

F32 = mybir.dt.float32
BF16 = mybir.dt.bfloat16
ALU = mybir.AluOpType
ACT = mybir.ActivationFunctionType
AX_X = mybir.AxisListType.X

P = 128
B, N = 4, 512
TB = N // P
NT = B * TB
E0, I0 = 32, 64
PAIRS = E0 * I0 // P
GROUPS, GE = 4, 8
TOP0 = 8
E1, H1 = 8, 512
HC = H1 // P
HEADS, HD = 16, 8
LANES, LD = 4, 32
LEVELS = 9
PAD = N // 2
LN_EPS = 1e-5
RMS_EPS = 1e-8
ROUTED = 2.5
FAR = -2.0 ** 127
SHARED = 30 * 1024
CONSTS = 17

POLAR = [(8.51425808, -25.281576, 18.7673094), (4.2570752, -3.16016629, 0.586476766),
         (4.25682787, -3.15999522, 0.586457253), (4.25577537, -3.15926721, 0.586374211),
         (4.25130191, -3.15617245, 0.586021201), (4.23238747, -3.14307812, 0.584527605),
         (4.15415638, -3.08875796, 0.578332236), (3.85835916, -2.88082531, 0.554631634),
         (3.0495984, -2.2849888, 0.487060827), (2.11205594, -1.49383647, 0.400102503),
         (1.87838366, -1.2537545, 0.375375648), (1.87500002, -1.25000002, 0.375000005)]
POLAR_PER_BATCH = len(POLAR) // B


def after(engine, semaphore, value):
    if not isinstance(value, int) or value > 0:
        engine.wait_ge(semaphore, value)


def build(nc, x_d, cols_d, rows_d, gate0_bias_d, gate1_bias_d, attn_w_d, gate0_d, wg_d, wu_d, wd_d,
          scan_raw_d, l1_w_d, gate1_d, w1_d, b1_d, w2_d, b2_d, out_d):
    ctx = ExitStack()
    with ctx:
        def sb(name, shape, dt=F32):
            return ctx.enter_context(nc.sbuf_tensor(name, shape, dt))

        def sem(name):
            return ctx.enter_context(nc.semaphore(name))

        shared = sb("shared", [P, SHARED])
        used = {0: 0, 1: 0}

        def carve(layer, shape):
            size = int(np.prod(shape[1:]))
            v = shared[:, used[layer]:used[layer] + size]
            used[layer] += size
            assert used[layer] <= SHARED, used
            dims = "abcdef"[:len(shape) - 1]
            if len(dims) > 1:
                v = v.rearrange(f"p ({' '.join(dims)}) -> p {' '.join(dims)}", **dict(zip(dims, shape[1:])))
            return v

        bank = [ctx.enter_context(nc.psum_tensor(f"bank{k}", [P, 512], F32)) for k in range(8)]

        cols = sb("cols", [P, 4])
        rows = sb("rows", [1, 5 * P])
        gate0_bias = sb("gate0_bias", [P, E0])
        gate1_bias = sb("gate1_bias", [P, E1])
        attn_w = carve(0, [P, 6, P])
        gate0_w = sb("gate0_w", [P, E0])
        wg = carve(0, [P, PAIRS + 1, P])
        wu = carve(0, [P, PAIRS + 1, P])
        wd = carve(0, [P, PAIRS + 1, P])
        polar_x = sb("polar_x", [P, P])
        l1_w = sb("l1_w", [P, 3, P])
        gate1_w = sb("gate1_w", [P, E1])
        w1 = sb("w1", [P, HC, P])
        b1 = sb("b1", [P, E1, HC])
        w2 = sb("w2", [P, E1, HC, P])
        b2 = sb("b2", [E1, P])

        ident = sb("ident", [P, P])
        ident_bf = sb("ident_bf", [P, P], BF16)
        ones = sb("ones", [P, P])
        tokens_n = sb("tokens_n", [1, 1])
        head_mask = sb("head_mask", [P, P])
        inv_lane = sb("inv_lane", [P, TB, LANES])
        pair_sel = sb("pair_sel", [3 * E0, E0, I0], BF16)
        coef = sb("coef", [P, 3 * len(POLAR)])

        x = sb("x", [P, NT, P])
        xn = sb("xn", [P, NT, P + 1])
        xnT = sb("xnT", [P, B * N])
        s_tok = carve(0, [P, NT, P])
        ln_stats = sb("ln_stats", [P, NT, 6])
        ln_mv = sb("ln_mv", [P, NT, 2])
        ln_var = sb("ln_var", [P, NT])
        ln_rstd = sb("ln_rstd", [P, NT])
        ln_log = sb("ln_log", [P, 3 * NT + 1])

        gram = carve(0, [P, B, P + 1])
        srow = sb("srow", [1, B, P])
        m1 = carve(0, [P, B, 2 * P])
        m1row = sb("m1row", [1, B, 2 * P])
        state0 = carve(0, [P, B, P])
        state = carve(0, [P, B, P])
        mq = carve(0, [P, B, P])
        mqrow = sb("mqrow", [1, B, P])
        attn_n = carve(0, [P, NT, P])
        attn_nT = carve(0, [P, B * N])
        wo_g = carve(0, [P, P])
        borow = sb("borow", [1, P])

        scores0 = carve(0, [P, NT, E0])
        choice = carve(0, [P, NT, E0])
        top8 = carve(0, [P, NT, GROUPS, 8])
        gscore = carve(0, [P, NT, GROUPS])
        gcmp = carve(0, [P, NT, GROUPS, GROUPS])
        grank = carve(0, [P, NT, GROUPS])
        gmask = carve(0, [P, NT, GROUPS])
        masked = carve(0, [P, NT, E0])
        best8 = carve(0, [P, NT, 8])
        replaced = carve(0, [P, NT, E0])
        taken = carve(0, [P, NT, E0])
        wsum = sb("wsum", [P, NT])
        wsum_eps = sb("wsum_eps", [P, NT])
        wrec = sb("wrec", [P, NT])
        gate0 = carve(0, [P, NT, E0])
        gate0_rest = carve(0, [P, NT, E0])
        gate0_rest2 = carve(0, [P, NT, E0])
        gate0_parts = sb("gate0_parts", [P, NT, 3, E0], BF16)
        gate0T = sb("gate0T", [3 * E0, B * N], BF16)

        silu_g = carve(0, [P, 2, N])
        silu_gu = carve(0, [P, 2, N])
        h0 = carve(0, [P, 2, N])
        gl0T = carve(0, [P, N])
        sg = carve(0, [P, N])
        polar_gx = sb("polar_gx", [P, 2 * P])
        polar_ai = carve(0, [P, P])
        polar_ab = carve(0, [P, P])
        polar_b = carve(0, [P, P])
        polar_sq = carve(0, [P, P])
        polar_col = sb("polar_col", [P, 1])
        polar_sum = sb("polar_sum", [P, 1])
        polar_r = sb("polar_r", [P, 1])

        logits1 = sb("logits1", [P, NT, E1])
        lmax = sb("lmax", [P, NT])
        lsub = sb("lsub", [P, NT, E1])
        lexp = sb("lexp", [P, NT, E1])
        lsum = sb("lsum", [P, NT])
        lrec = sb("lrec", [P, NT])
        ecmp = carve(1, [P, NT, E1, E1])
        erank = sb("erank", [P, NT, E1])
        emask = sb("emask", [P, NT, E1])
        probs1 = sb("probs1", [P, NT, E1])
        gate1 = sb("gate1", [P, NT, E1])
        gate1T = sb("gate1T", [E1, B * N])

        xT = carve(1, [P, B, PAD + N])
        x_tok = carve(1, [P, B, TB, P])
        left_tok = carve(1, [P, B, TB, P])
        leftT = carve(1, [P, B, N])
        sumT = carve(1, [P, B, N])
        prod = carve(1, [P, 2, TB, LANES, LANES, LD])
        score = carve(1, [P, 2, TB, LANES, LANES])
        v_last = carve(1, [P, 2, TB, LD])
        smax = sb("smax", [P, 2, TB, LANES])
        ssub = carve(1, [P, 2, TB, LANES, LANES])
        sexp = carve(1, [P, 2, TB, LANES, LANES])
        ssum = sb("ssum", [P, 2, TB, LANES])
        mix = carve(1, [P, 2, TB, LANES, LANES, LD])
        mix2 = carve(1, [P, 2, TB, LANES, 2, LD])
        z = carve(1, [P, 2, TB, P])
        z_sq = carve(1, [P, 2, TB, P])
        z_ss = sb("z_ss", [P, 2, TB, LANES])
        eps_ss = sb("eps_ss", [P, 2, TB, LANES])
        z_ms = sb("z_ms", [P, 2, TB, LANES])
        z_ln = sb("z_ln", [P, 2, TB, LANES])
        z_rs = sb("z_rs", [P, 2, TB, LANES])
        z_r = sb("z_r", [P, 2, TB, LANES])
        zn = carve(1, [P, TB, P])
        hT = carve(1, [P, HC, N])
        b1_now = sb("b1_now", [P, HC])
        gate1_now = sb("gate1_now", [P, NT])
        acc = carve(1, [P, NT, P])
        qvT = leftT
        gl1 = z_sq

        S = {}

        def s(name):
            if name not in S:
                S[name] = sem(name)
            return S[name]

        for name in (
            "ld_x0 ld_x1 ld_x2 ld_x3 ld_w1_0 ld_w1_1 ld_w1_2 ld_w1_3 ld_scan ld_small ld_moe ld_l1 st_out const "
            "polar_const polar_sq_done polar_sum_mm polar_sum_cp polar_r_done polar_x0 ln_stat ln_var_done "
            "ln_pow ln_norm xnT_mm xnT_cp wfold wog_done borow_mm borow_cp gram_mm gram_cp m1_mm m1_cp st_mm "
            "st0_cp st_cp mq_mm mq_cp at_mm at_stat at_var at_pow at_norm atT_mm atT_cp so_mm so_cp logit_mm "
            "sig_done parts_done g0T_mm g0T_cp g_mm u_mm gb_mm silu_done gu_done h0_done dn_mm y0_silu y0T_mm "
            "sg_done x1_done polar_ai_done polar_a_mm polar_gx_cp polar_ab_done polar_a2_mm polar_b_done "
            "polar_x_mm polar_x_cp l1_stat l1_var l1_pow l1_norm x1T_mm x1T_cp log1_mm log1_cp lsub_done "
            "lexp_done gate1_done g1T_mm g1T_cp acc_mm acc_cp up_mm up_cp uptok_mm pad_done state_mm xT_cp "
            "leftT_cp left_mm left_tok_cp sum_done prod_done last_prod score_done smax_done ssub_done sexp_done "
            "ssum_done v_mm v_last_cp mix_done last_mix mix2_done z_done zsq_done zss_done epsss_done zms_done "
            "zln_done zrs_done zr_done zn_done xtok_done ffn_up ffn_relu ffn_down ffn_acc qT_mm b1_now_done "
            "gate_now_done v1_mm v1_cp qv_done yp_mm gl1_done o_mul o_done ln_var route0_step route1_step "
        ).split():
            s(name)

        block = ctx.enter_context(nc.Block())

        @block.sync
        def _(sp):
            xv = x_d.rearrange("b (j p) c -> p b j c", p=P)
            for b in range(B):
                sp.dma_start(x[:, b * TB:(b + 1) * TB, :], xv[:, b]).then_inc(s(f"ld_x{b}"), 16)
            sp.dma_start(polar_x[:], scan_raw_d).then_inc(s("ld_scan"), 16)
            sp.dma_start(attn_w[:], attn_w_d).then_inc(s("ld_small"), 16)
            sp.dma_start(cols[:], cols_d).then_inc(s("ld_small"), 16)
            sp.dma_start(rows[:], rows_d).then_inc(s("ld_small"), 16)
            sp.dma_start(gate0_w[:], gate0_d).then_inc(s("ld_small"), 16)
            sp.dma_start(gate0_bias[:], gate0_bias_d.partition_broadcast(P)).then_inc(s("ld_small"), 16)
            sp.dma_start(wg[:], wg_d).then_inc(s("ld_moe"), 16)
            sp.dma_start(wu[:], wu_d).then_inc(s("ld_moe"), 16)
            sp.dma_start(wd[:], wd_d).then_inc(s("ld_moe"), 16)
            sp.dma_start(l1_w[:], l1_w_d).then_inc(s("ld_l1"), 16)
            sp.dma_start(gate1_w[:], gate1_d).then_inc(s("ld_l1"), 16)
            sp.dma_start(gate1_bias[:], gate1_bias_d.partition_broadcast(P)).then_inc(s("ld_l1"), 16)
            sp.dma_start(b1[:], b1_d).then_inc(s("ld_l1"), 16)
            sp.dma_start(b2[:], b2_d).then_inc(s("ld_l1"), 16)
            sp.dma_start(w2[:], w2_d).then_inc(s("ld_l1"), 16)
            for c in range(HC):
                sp.dma_start(w1[:, c], w1_d[0, :, c]).then_inc(s(f"ld_w1_{c}"), 16)
            with sp.Fori(0, E1 - 1) as e:
                for c in range(HC):
                    sp.wait_ge(s("ffn_up"), e * (B * HC) + (B - 1) * HC + c + 1)
                    sp.dma_start(w1[:, c], w1_d[bass.ds(e + 1, 1), :, c].rearrange("e p h -> (e p) h")).then_inc(s(f"ld_w1_{c}"), 16)
            ov = out_d.rearrange("b (j p) c -> p b j c", p=P)
            for b in range(B):
                sp.wait_ge(s("o_done"), b + 1)
                sp.dma_start(ov[:, b], x[:, b * TB:(b + 1) * TB, :]).then_inc(s("st_out"), 16)
            sp.wait_ge(s("st_out"), 16 * B)

        LD_SMALL, LD_MOE, LD_L1 = 16 * 5, 16 * 3, 16 * 6

        @block.gpsimd
        def _(pool):
            g = nc.gpsimd
            cdone = s("const")
            n = 0
            for k, abc in enumerate(POLAR):
                for m, v in enumerate(abc):
                    g.memset(coef[:, 3 * k + m:3 * k + m + 1], float(v)).then_inc(s("polar_const"), 1)
            g.memset(ones[:], 1.0).then_inc(cdone, 1)
            g.memset(ident[:], 0.0).then_inc(cdone, 1)
            g.memset(tokens_n[:], float(N)).then_inc(cdone, 1)
            g.memset(xn[:, :, P:P + 1], 1.0).then_inc(cdone, 1)
            g.memset(head_mask[:], 1.0).then_inc(cdone, 1)
            g.memset(pair_sel[:], 0.0).then_inc(cdone, 1)
            n = 6
            for lane in range(LANES):
                g.memset(inv_lane[:, :, lane:lane + 1], 1.0 / (1 + lane)).then_inc(cdone, 1)
                n += 1
            g.memset(gcmp[:], 0.0).then_inc(cdone, 1)
            n += 1
            pool.wait_ge(cdone, n)
            g.affine_select(out=ident[:], in_=ident[:], compare_op=ALU.not_equal, fill=1.0, base=0,
                            pattern=[[-1, P]], channel_multiplier=1).then_inc(cdone, 1)
            n += 1
            hm = head_mask[:].rearrange("p (h d) -> p h d", h=HEADS)
            g.affine_select(out=hm, in_=hm, compare_op=ALU.is_ge, fill=0.0, base=0,
                            pattern=[[-HD, HEADS], [0, HD]], channel_multiplier=1).then_inc(cdone, 1)
            n += 1
            pool.wait_ge(cdone, n)
            g.affine_select(out=hm, in_=hm, compare_op=ALU.is_ge, fill=0.0, base=HD - 1,
                            pattern=[[HD, HEADS], [0, HD]], channel_multiplier=-1).then_inc(cdone, 1)
            n += 1
            for part in range(3):
                v = pair_sel[part * E0:(part + 1) * E0]
                pool.wait_ge(cdone, n)
                g.affine_select(out=v, in_=v, compare_op=ALU.not_equal, fill=1.0, base=0,
                                pattern=[[-1, E0], [0, I0]], channel_multiplier=1).then_inc(cdone, 1)
                n += 1
            assert n == CONSTS

            pool.wait_ge(s("ld_small"), LD_SMALL)
            pool.wait_ge(cdone, n)
            pool.wait_ge(s("x1_done"), B)
            for b in range(B):
                g.tensor_scalar(xT[:, b, 0:PAD], ones[:, 0:1].broadcast_to([P, PAD]), cols[:, 3:4], 1.0,
                                ALU.mult, ALU.mult).then_inc(s("pad_done"), 1)

            def sum_inputs(k, b):
                pool.wait_ge(s("leftT_cp"), k + 1)
                g.tensor_tensor(sumT[:, b], leftT[:, b], xT[:, b, PAD:PAD + N],
                                ALU.add).then_inc(s("sum_done"), 1)

            def last_product(k, b):
                pool.wait_ge(s("left_tok_cp"), k + 1)
                pool.wait_ge(s("xtok_done"), k + 1)
                g.tensor_tensor(prod[:, b % 2, :, :, LANES - 1],
                                left_tok[:, b].rearrange("p j (l d) -> p j l d", l=LANES),
                                x_tok[:, b, :, (LANES - 1) * LD:].unsqueeze(2).broadcast_to([P, TB, LANES, LD]),
                                ALU.mult).then_inc(s("last_prod"), 1)

            def last_mix(k, b):
                pool.wait_ge(s("sexp_done"), k + 1)
                pool.wait_ge(s("v_last_cp"), k + 1)
                g.tensor_tensor(mix[:, b % 2, :, :, LANES - 1],
                                sexp[:, b % 2, :, :, LANES - 1].unsqueeze(3).broadcast_to([P, TB, LANES, LD]),
                                v_last[:, b % 2].unsqueeze(2).broadcast_to([P, TB, LANES, LD]),
                                ALU.mult).then_inc(s("last_mix"), 1)

            def halve_mix(k, b):
                pool.wait_ge(s("mix_done"), k + 1)
                pool.wait_ge(s("last_mix"), k + 1)
                g.tensor_tensor(mix2[:, b % 2].rearrange("p j l m d -> p (j l) (m d)"),
                                mix[:, b % 2, :, :, 0:2].rearrange("p j l m d -> p (j l) (m d)"),
                                mix[:, b % 2, :, :, 2:4].rearrange("p j l m d -> p (j l) (m d)"),
                                ALU.add).then_inc(s("mix2_done"), 1)

            def rms_factor(k, b):
                pool.wait_ge(s("zrs_done"), k + 1)
                g.tensor_tensor(z_r[:, b % 2], z_rs[:, b % 2], inv_lane[:], ALU.mult).then_inc(s("zr_done"), 1)

            def new_state(k, b):
                pool.wait_ge(s("zn_done"), k + 1)
                g.tensor_tensor(x_tok[:, b], zn[:], left_tok[:, b], ALU.add).then_inc(s("xtok_done"), 1)

            def slot(k, b, this=True, before=True, ahead=True):
                if ahead:
                    sum_inputs(k + 1, (b + 1) % B)
                if this:
                    last_mix(k, b)
                if before:
                    rms_factor(k - 1, (b - 1) % B)
                if ahead:
                    last_product(k + 1, (b + 1) % B)
                if this:
                    halve_mix(k, b)
                if before:
                    new_state(k - 1, (b - 1) % B)

            pool.wait_ge(s("const"), CONSTS)
            sum_inputs(0, 0)
            last_product(0, 0)
            slot(0, 0, before=False)
            with pool.Fori(0, LEVELS - 1) as lev:
                for j in range(B):
                    slot(lev * B + (j + 1), (j + 1) % B)
            top = LEVELS - 1
            slot(top * B + 1, 1)
            slot(top * B + 2, 2)
            slot(top * B + 3, 3, ahead=False)
            slot(top * B + 4, 0, this=False, ahead=False)

        @block.tensor
        def _(pe):
            def mm(out, lhsT, rhs, start=True, stop=True):
                return nc.tensor.matmul(out, lhsT, rhs, start=start, stop=stop)

            def tr(out, in_, idm=None):
                return nc.tensor.transpose(out, in_, ident[:] if idm is None else idm)

            pe.wait_ge(s("const"), CONSTS)
            pe.wait_ge(s("polar_sq_done"), 1)
            mm(bank[7][:, 0:1], ones[:], polar_col[:]).then_inc(s("polar_sum_mm"), 1)

            for b in range(B):
                pe.wait_ge(s("ln_norm"), b + 1)
                if b == 3:
                    pe.wait_ge(s("polar_sum_cp"), 1)
                for j in range(TB):
                    last = tr(bank[4 + b][:, j * P:(j + 1) * P], xn[:, b * TB + j, 0:P])
                last.then_inc(s("xnT_mm"), 1)
            pe.wait_ge(s("ld_small"), LD_SMALL)
            pe.wait_ge(s("xnT_cp"), B)
            for t in range(NT):
                last = mm(bank[4][:, t * E0:(t + 1) * E0], xnT[:, t * P:(t + 1) * P], gate0_w[:])
            last.then_inc(s("logit_mm"), 1)

            for b in range(B):
                for j in range(TB):
                    mm(bank[b][:, 0:P + 1], xn[:, b * TB + j, 0:P], xn[:, b * TB + j, :], j == 0, j == TB - 1)
                for j in range(TB):
                    last = mm(bank[b][0:1, 256:256 + P], ones[:, 0:1], xn[:, b * TB + j, 0:P], j == 0, j == TB - 1)
                last.then_inc(s("gram_mm"), 1)
            pe.wait_ge(s("wfold"), 1)
            pe.wait_ge(s("sig_done"), 1)
            wv = attn_w[:, 3:5].rearrange("p k c -> p (k c)")
            for b in range(B):
                pe.wait_ge(s("gram_cp"), b + 1)
                mm(bank[4 + b][:, 0:256], gram[:, b, 0:P], wv, True, False)
                mm(bank[4 + b][:, 0:256], srow[:, b], rows[:, 256:512], False, True)
                mm(bank[4 + b][0:1, 256:512], gram[:, b, P:P + 1], wv, True, False)
                last = mm(bank[4 + b][0:1, 256:512], tokens_n[:], rows[:, 256:512], False, True)
                last.then_inc(s("m1_mm"), 1)
            for b in range(B):
                pe.wait_ge(s("m1_cp"), b + 1)
                for k in range(2):
                    mm(bank[b][:, k * P:(k + 1) * P], attn_w[:, 1 + k], m1[:, b, k * P:(k + 1) * P], True, False)
                    last = mm(bank[b][:, k * P:(k + 1) * P], rows[:, k * P:(k + 1) * P],
                              m1row[:, b, k * P:(k + 1) * P], False, True)
                last.then_inc(s("st_mm"), 1)
            for b in range(B):
                pe.wait_ge(s("st_cp"), b + 1)
                mm(bank[4 + b][:, 0:P], attn_w[:, 0], state[:, b])
                mm(bank[4 + b][0:1, P:2 * P], cols[:, 0:1], state[:, b]).then_inc(s("mq_mm"), 1)
            for b in range(B):
                pe.wait_ge(s("mq_cp"), b + 1)
                for j in range(TB):
                    mm(bank[b][:, j * P:(j + 1) * P], xnT[:, (b * TB + j) * P:(b * TB + j + 1) * P], mq[:, b],
                       True, False)
                    last = mm(bank[b][:, j * P:(j + 1) * P], ones[0:1, :], mqrow[:, b], False, True)
                last.then_inc(s("at_mm"), 1)
            pe.wait_ge(s("mq_cp"), B)
            mm(bank[4][0:1, 0:P], cols[:, 2:3], attn_w[:, 5]).then_inc(s("borow_mm"), 1)
            pe.wait_ge(s("borow_cp"), 1)
            for b in range(B):
                pe.wait_ge(s("parts_done"), 1)
                pe.wait_ge(s("wog_done"), 2)
                for j in range(TB):
                    t = b * TB + j
                    last = tr(bank[4 + b][:].bitcast(BF16)[0:3 * E0, j * P:(j + 1) * P],
                              gate0_parts[:, t].rearrange("p a e -> p (a e)"), ident_bf[:])
                last.then_inc(s("g0T_mm"), 1)
            for b in range(B):
                pe.wait_ge(s("at_norm"), b + 1)
                pe.wait_ge(s("g0T_cp"), b + 1)
                for j in range(TB):
                    last = tr(bank[4 + b][:, j * P:(j + 1) * P], attn_n[:, b * TB + j])
                last.then_inc(s("atT_mm"), 1)
            pe.wait_ge(s("wog_done"), 1)
            for b in range(B):
                pe.wait_ge(s("atT_cp"), b + 1)
                for j in range(TB):
                    t = b * TB + j
                    mm(bank[b][:, j * P:(j + 1) * P], attn_nT[:, t * P:(t + 1) * P], wo_g[:], True, False)
                    last = mm(bank[b][:, j * P:(j + 1) * P], ones[0:1, :], borow[:], False, True)
                last.then_inc(s("so_mm"), 1)

            pe.wait_ge(s("ld_moe"), LD_MOE)
            pe.wait_ge(s("polar_x0"), 1)
            pe.wait_ge(s("so_cp"), B)
            pe.wait_ge(s("atT_cp"), B)
            UNITS = PAIRS + 1
            with pe.Fori(0, B) as i:
                xin = xnT[:, bass.ds(i * N, N)]
                gin = gate0T[:, bass.ds(i * N, N)]

                def down(u):
                    pe.wait_ge(s("h0_done"), i * UNITS + (u + 1))
                    mm(bank[6][:], wd[:, u], h0[:, u % 2], u == 0, u == UNITS - 1).then_inc(s("dn_mm"), 1)

                def polar_products(q):
                    r, stage = divmod(q - 1, 5)
                    if q < 1 or r >= POLAR_PER_BATCH:
                        return
                    n = i * POLAR_PER_BATCH + r
                    if stage == 0:
                        if r > 0:
                            pe.wait_ge(s("polar_x_cp"), n)
                        mm(bank[7][:, 0:P], polar_x[:], polar_x[:])
                        tr(bank[7][:, P:2 * P], polar_x[:]).then_inc(s("polar_a_mm"), 1)
                    elif stage == 1:
                        pe.wait_ge(s("polar_ab_done"), n + 1)
                        mm(bank[7][:, 0:P], polar_gx[:, 0:P], polar_gx[:, 0:P]).then_inc(s("polar_a2_mm"), 1)
                    elif stage == 2:
                        pe.wait_ge(s("polar_b_done"), n + 1)
                        mm(bank[7][:, 0:P], polar_gx[:, P:2 * P], polar_b[:]).then_inc(s("polar_x_mm"), 1)

                for u in range(UNITS):
                    k = u % 2
                    if u >= 2:
                        pe.wait_ge(s("silu_done"), i * UNITS + (u - 1))
                    mm(bank[k][:], wg[:, u], xin).then_inc(s("g_mm"), 1)
                    if u >= 2:
                        pe.wait_ge(s("h0_done"), i * UNITS + (u - 1))
                    mm(bank[2 + k][:], wu[:, u], xin).then_inc(s("u_mm"), 1)
                    if u >= 1:
                        sel = pair_sel[:, 2 * (u - 1):2 * u].rearrange("p e i -> p (e i)")
                        mm(bank[4 + k][:], sel, gin).then_inc(s("gb_mm"), 1)
                        down(u - 1)
                    polar_products(u)
                down(UNITS - 1)
                pe.wait_ge(s("y0_silu"), i + 1)
                pe.wait_ge(s("polar_x_cp"), (i + 1) * POLAR_PER_BATCH)
                for j in range(TB):
                    last = tr(bank[7][:, j * P:(j + 1) * P], gl0T[:, j * P:(j + 1) * P])
                last.then_inc(s("y0T_mm"), 1)
                pe.wait_ge(s("sg_done"), i + 1)

            for b in range(B):
                pe.wait_ge(s("l1_norm"), b + 1)
                for j in range(TB):
                    last = tr(bank[4 + b][:, j * P:(j + 1) * P], xn[:, b * TB + j, 0:P])
                last.then_inc(s("x1T_mm"), 1)
            pe.wait_ge(s("ld_l1"), LD_L1)
            pe.wait_ge(s("x1T_cp"), B)
            for t in range(NT):
                last = mm(bank[0][:, t * E1:(t + 1) * E1], xnT[:, t * P:(t + 1) * P], gate1_w[:])
            last.then_inc(s("log1_mm"), 1)
            for b in range(B):
                mm(bank[4 + b][:], l1_w[:, 0], xnT[:, b * N:(b + 1) * N]).then_inc(s("up_mm"), 1)
            for b in range(B):
                if b == 3:
                    pe.wait_ge(s("xtok_done"), 1)
                for j in range(TB):
                    t = b * TB + j
                    last = mm(bank[1 + b % 3][:, j * P:(j + 1) * P], xnT[:, t * P:(t + 1) * P], l1_w[:, 0])
                last.then_inc(s("uptok_mm"), 1)
            for b in range(B):
                pe.wait_ge(s("gate1_done"), 1)
                pe.wait_ge(s("up_cp"), b + 1)
                for j in range(TB):
                    last = tr(bank[4 + b][0:E1, j * P:(j + 1) * P], gate1[:, b * TB + j])
                last.then_inc(s("g1T_mm"), 1)
            pe.wait_ge(s("xtok_done"), B)
            pe.wait_ge(s("log1_cp"), 1)
            for b in range(B):
                pe.wait_ge(s("g1T_cp"), b + 1)
                for j in range(TB):
                    t = b * TB + j
                    last = mm(bank[b][:, j * P:(j + 1) * P], gate1T[:, t * P:(t + 1) * P], b2[:])
                last.then_inc(s("acc_mm"), 1)

            pe.wait_ge(s("acc_cp"), B)

            def state_channels(k, b):
                pe.wait_ge(s("xtok_done"), k + 1)
                after(pe, s("xT_cp"), k)
                for j in range(TB):
                    last = tr(bank[0][:, j * P:(j + 1) * P], x_tok[:, b, j])
                last.then_inc(s("state_mm"), 1)

            def left_tokens(k, b):
                pe.wait_ge(s("leftT_cp"), k + 1)
                after(pe, s("prod_done"), k)
                for j in range(TB):
                    last = tr(bank[1][:, j * P:(j + 1) * P], leftT[:, b, j * P:(j + 1) * P])
                last.then_inc(s("left_mm"), 1)

            def values(k, b):
                pe.wait_ge(s("sum_done"), k + 1)
                after(pe, s("mix_done"), k)
                for j in range(TB):
                    last = mm(bank[2][:, j * P:(j + 1) * P], sumT[:, b, j * P:(j + 1) * P], polar_x[:])
                last.then_inc(s("v_mm"), 1)

            def expert_up(e, blk, c):
                if blk == 0:
                    pe.wait_ge(s(f"ld_w1_{c}"), e * 16 + 16)
                mm(bank[3 + c][:], w1[:, c], xnT[:, blk * N:(blk + 1) * N]).then_inc(s("ffn_up"), 1)

            def expert_down(e, blk):
                n = e * B + blk
                pe.wait_ge(s("ffn_relu"), (n + 1) * HC)
                for j in range(TB):
                    for c in range(HC):
                        last = mm(bank[7][:, j * P:(j + 1) * P], hT[:, c, j * P:(j + 1) * P],
                                  w2[:, bass.ds(e, 1), c].rearrange("p e o -> p (e o)"), c == 0, c == HC - 1)
                last.then_inc(s("ffn_down"), 1)

            def slot(k, b, expert=None):
                state_channels(k + 1, (b + 1) % B)
                if expert:
                    expert_up(*expert, 0)
                    expert_up(*expert, 1)
                left_tokens(k + 1, (b + 1) % B)
                if expert:
                    expert_up(*expert, 2)
                    expert_up(*expert, 3)
                    expert_down(*expert)
                values(k + 1, (b + 1) % B)

            slot(-1, B - 1)
            slot(0, 0)
            with pe.Fori(0, LEVELS - 1) as lev:
                for j in range(B):
                    slot(lev * B + (j + 1), (j + 1) % B, expert=(lev, j))
            slot((LEVELS - 1) * B + 1, 1)
            slot((LEVELS - 1) * B + 2, 2)

            pe.wait_ge(s("mix_done"), LEVELS * B)
            pe.wait_ge(s("ffn_acc"), E1 * B * TB)
            for b in range(B):
                mm(bank[4 + b][:], l1_w[:, 1], xnT[:, b * N:(b + 1) * N]).then_inc(s("v1_mm"), 1)
            for b in range(B):
                pe.wait_ge(s("xtok_done"), LEVELS * B + b + 1)
                for j in range(TB):
                    last = tr(bank[b][:, j * P:(j + 1) * P], x_tok[:, b, j])
                last.then_inc(s("qT_mm"), 1)
            for b in range(B):
                pe.wait_ge(s("qv_done"), b + 1)
                for j in range(TB):
                    last = mm(bank[b][:, j * P:(j + 1) * P], qvT[:, b, j * P:(j + 1) * P], l1_w[:, 2])
                last.then_inc(s("yp_mm"), 1)

        @block.scalar
        def _(act):
            a = nc.scalar
            def root(out, in_, done, n, slot):
                log = ln_log[:, slot:slot + in_.shape[1]]
                a.activation(log, in_, ACT.Ln).then_inc(s(done), 1)
                act.wait_ge(s(done), 2 * n + 1)
                a.activation(out, log, ACT.Exp, scale=-0.5).then_inc(s(done), 1)

            def norm_roots(var, done, b, which):
                act.wait_ge(s(var), b + 1)
                root(ln_rstd[:, b * TB:(b + 1) * TB], ln_var[:, b * TB:(b + 1) * TB], done, b, which * NT + b * TB)

            act.wait_ge(s("ld_scan"), 16)
            a.activation(polar_sq[:], polar_x[:], ACT.Square, accum_out=polar_col[:]).then_inc(s("polar_sq_done"), 1)
            act.wait_ge(s("polar_sum_mm"), 1)
            a.copy(polar_sum[:], bank[7][:, 0:1]).then_inc(s("polar_sum_cp"), 1)
            act.wait_ge(s("polar_sum_cp"), 1)
            root(polar_r[:], polar_sum[:], "polar_r_done", 0, 3 * NT)
            for b in range(B):
                norm_roots("ln_var_done", "ln_pow", b, 0)
            for b in range(B):
                act.wait_ge(s("xnT_mm"), b + 1)
                a.copy(xnT[:, b * N:(b + 1) * N], bank[4 + b][:]).then_inc(s("xnT_cp"), 1)
            act.wait_ge(s("logit_mm"), 1)
            a.activation(scores0[:].rearrange("p t e -> p (t e)"), bank[4][:], ACT.Sigmoid).then_inc(s("sig_done"), 1)
            for b in range(B):
                act.wait_ge(s("gram_mm"), b + 1)
                a.copy(gram[:, b], bank[b][:, 0:P + 1])
                a.copy(srow[:, b], bank[b][0:1, 256:256 + P]).then_inc(s("gram_cp"), 1)
            for b in range(B):
                act.wait_ge(s("mq_mm"), b + 1)
                a.copy(mq[:, b], bank[4 + b][:, 0:P])
                a.copy(mqrow[:, b], bank[4 + b][0:1, P:2 * P]).then_inc(s("mq_cp"), 1)
            for b in range(B):
                norm_roots("at_var", "at_pow", b, 1)
            for b in range(B):
                act.wait_ge(s("g0T_mm"), b + 1)
                a.copy(gate0T[:, b * N:(b + 1) * N], bank[4 + b][:].bitcast(BF16)[0:3 * E0, 0:N]).then_inc(s("g0T_cp"), 1)
            for b in range(B):
                act.wait_ge(s("atT_mm"), b + 1)
                a.copy(attn_nT[:, b * N:(b + 1) * N], bank[4 + b][:]).then_inc(s("atT_cp"), 1)
            for b in range(B):
                act.wait_ge(s("so_mm"), b + 1)
                a.copy(s_tok[:, b * TB:(b + 1) * TB].rearrange("p j c -> p (j c)"), bank[b][:]).then_inc(s("so_cp"), 1)

            UNITS = PAIRS + 1
            with act.Fori(0, B) as i:
                for u in range(UNITS):
                    act.wait_ge(s("g_mm"), i * UNITS + (u + 1))
                    if u == 2:
                        act.wait_ge(s("h0_done"), i * UNITS + 1)
                    elif u > 2:
                        act.wait_ge(s("gu_done"), i * PAIRS + (u - 2))
                    a.activation(silu_g[:, u % 2], bank[u % 2][:], ACT.Silu).then_inc(s("silu_done"), 1)
                act.wait_ge(s("dn_mm"), (i + 1) * UNITS)
                a.activation(gl0T[:], bank[6][:], ACT.Silu).then_inc(s("y0_silu"), 1)

            for b in range(B):
                norm_roots("l1_var", "l1_pow", b, 2)
            for b in range(B):
                act.wait_ge(s("x1T_mm"), b + 1)
                a.copy(xnT[:, b * N:(b + 1) * N], bank[4 + b][:]).then_inc(s("x1T_cp"), 1)
            act.wait_ge(s("lsub_done"), 1)
            a.activation(lexp[:], lsub[:], ACT.Exp).then_inc(s("lexp_done"), 1)
            for b in range(B):
                act.wait_ge(s("up_mm"), b + 1)
                a.copy(xT[:, b, PAD:PAD + N], bank[4 + b][:]).then_inc(s("up_cp"), 1)
            for b in range(B):
                act.wait_ge(s("uptok_mm"), b + 1)
                a.copy(x_tok[:, b].rearrange("p j c -> p (j c)"), bank[1 + b % 3][:]).then_inc(s("xtok_done"), 1)
            for b in range(B):
                act.wait_ge(s("g1T_mm"), b + 1)
                a.copy(gate1T[:, b * N:(b + 1) * N], bank[4 + b][0:E1, :]).then_inc(s("g1T_cp"), 1)
            for b in range(B):
                act.wait_ge(s("acc_mm"), b + 1)
                a.copy(acc[:, b * TB:(b + 1) * TB].rearrange("p j c -> p (j c)"), bank[b][:]).then_inc(s("acc_cp"), 1)

            act.wait_ge(s("pad_done"), B)

            def state_in(k, b, lev):
                act.wait_ge(s("state_mm"), k + 1)
                a.copy(xT[:, b, PAD:PAD + N], bank[0][:]).then_inc(s("xT_cp"), 1)
                act.wait_ge(s("xT_cp"), k + 1)
                a.copy(leftT[:, b], xT[:, b, bass.ds(PAD - (1 << lev), N)]).then_inc(s("leftT_cp"), 1)

            def left_out(k, b):
                act.wait_ge(s("left_mm"), k + 1)
                a.copy(left_tok[:, b].rearrange("p j c -> p (j c)"), bank[1][:]).then_inc(s("left_tok_cp"), 1)

            def last_values_out(k, b):
                act.wait_ge(s("v_mm"), k + 1)
                a.copy(v_last[:, b % 2], bank[2][:].rearrange("p (j c) -> p j c", j=TB)[:, :, (LANES - 1) * LD:])\
                 .then_inc(s("v_last_cp"), 1)

            def expo(k, b):
                act.wait_ge(s("ssub_done"), k + 1)
                a.activation(sexp[:, b % 2], ssub[:, b % 2], ACT.Exp, scale=float(LD) ** -0.5).then_inc(s("sexp_done"), 1)

            def square(k, b):
                act.wait_ge(s("z_done"), k + 1)
                a.activation(z_sq[:, b % 2], z[:, b % 2], ACT.Square).then_inc(s("zsq_done"), 1)

            def rsqrt(k, b):
                act.wait_ge(s("zms_done"), k + 1)
                a.activation(z_ln[:, b % 2], z_ms[:, b % 2], ACT.Ln).then_inc(s("zln_done"), 1)
                act.wait_ge(s("zln_done"), k + 1)
                a.activation(z_rs[:, b % 2], z_ln[:, b % 2], ACT.Exp, scale=-0.5).then_inc(s("zrs_done"), 1)

            def relu(e, blk, c):
                act.wait_ge(s("ffn_up"), (e * B + blk) * HC + c + 1)
                a.activation(hT[:, c], bank[3 + c][:], ACT.Relu, bias=b1_now[:, c:c + 1]).then_inc(s("ffn_relu"), 1)

            def slot(k, b, lev_next, this=True, before=True, ahead=True, expert=None):
                if ahead:
                    state_in(k + 1, (b + 1) % B, lev_next)
                if expert:
                    if expert[1] == 0:
                        a.copy(b1_now[:], b1[:, bass.ds(expert[0], 1)].rearrange("p e c -> p (e c)")).then_inc(s("b1_now_done"), 1)
                        act.wait_ge(s("b1_now_done"), expert[0] + 1)
                    relu(*expert, 0)
                if before:
                    square(k - 1, (b - 1) % B)
                if expert:
                    relu(*expert, 1)
                if ahead:
                    left_out(k + 1, (b + 1) % B)
                if expert:
                    relu(*expert, 2)
                    relu(*expert, 3)
                if this:
                    expo(k, b)
                if before:
                    rsqrt(k - 1, (b - 1) % B)
                if ahead:
                    last_values_out(k + 1, (b + 1) % B)

            slot(-1, B - 1, 0, this=False, before=False)
            slot(0, 0, 0, before=False)
            with act.Fori(0, LEVELS - 1) as lev:
                for j in range(B):
                    slot(lev * B + (j + 1), (j + 1) % B, lev if j < 2 else lev + 1, expert=(lev, j))
            top = LEVELS - 1
            slot(top * B + 1, 1, top)
            slot(top * B + 2, 2, top)
            slot(top * B + 3, 3, top, ahead=False)
            slot(top * B + 4, 0, top, this=False, ahead=False)

            for b in range(B):
                act.wait_ge(s("v1_mm"), b + 1)
                a.copy(sumT[:, b], bank[4 + b][:]).then_inc(s("v1_cp"), 1)
            act.wait_ge(s("ffn_acc"), E1 * B * TB)
            for b in range(B):
                a.activation(acc[:, b * TB:(b + 1) * TB], acc[:, b * TB:(b + 1) * TB], ACT.Silu).then_inc(s("gl1_done"), 1)

        @block.vector
        def _(dve):
            v = nc.vector
            tt, ts, stt = v.tensor_tensor, v.tensor_scalar, v.scalar_tensor_tensor

            def layer_norm(b, src_tile, out_tile, stat, var, pow_, norm):
                t0 = b * TB
                for j in range(TB):
                    last = v.bn_stats(ln_stats[:, t0 + j], src_tile(t0 + j))
                last.then_inc(s(stat), 1)
                dve.wait_ge(s(stat), 2 * b + 1)
                for j in range(TB):
                    last = v.bn_aggr(ln_mv[:, t0 + j], ln_stats[:, t0 + j])
                last.then_inc(s(stat), 1)
                dve.wait_ge(s(stat), 2 * b + 2)
                ts(ln_var[:, t0:t0 + TB], ln_mv[:, t0:t0 + TB, 1], LN_EPS, None, ALU.add).then_inc(s(var), 1)

            def normalise(b, src_tile, out_tile, pow_, norm):
                t0 = b * TB
                dve.wait_ge(s(pow_), 2 * b + 2)
                for j in range(TB):
                    last = ts(out_tile(t0 + j), src_tile(t0 + j), ln_mv[:, t0 + j, 0:1], ln_rstd[:, t0 + j:t0 + j + 1],
                              ALU.subtract, ALU.mult)
                last.then_inc(s(norm), 1)

            for b in range(B):
                dve.wait_ge(s(f"ld_x{b}"), 16)
                layer_norm(b, lambda t: x[:, t], None, "ln_stat", "ln_var_done", None, None)
                if b >= 1:
                    normalise(b - 1, lambda t: x[:, t], lambda t: xn[:, t, 0:P], "ln_pow", "ln_norm")
            normalise(B - 1, lambda t: x[:, t], lambda t: xn[:, t, 0:P], "ln_pow", "ln_norm")
            dve.wait_ge(s("const"), CONSTS)
            dve.wait_ge(s("ld_small"), LD_SMALL)
            tt(attn_w[:, 0:5], attn_w[:, 0:5], ident[:].unsqueeze(1).broadcast_to([P, 5, P]), ALU.add).then_inc(s("wfold"), 1)
            ts(wo_g[:], attn_w[:, 5], cols[:, 1:2], None, ALU.mult).then_inc(s("wog_done"), 1)
            v.tensor_copy(ident_bf[:], ident[:]).then_inc(s("wog_done"), 1)
            dve.wait_ge(s("polar_r_done"), 2)
            ts(polar_x[:], polar_x[:], polar_r[:], None, ALU.mult).then_inc(s("polar_x0"), 1)

            def m1_out(b):
                dve.wait_ge(s("m1_mm"), b + 1)
                v.tensor_copy(m1[:, b], bank[4 + b][:, 0:256])
                v.tensor_copy(m1row[:, b], bank[4 + b][0:1, 256:512]).then_inc(s("m1_cp"), 1)

            def state_out(b):
                dve.wait_ge(s("st_mm"), b + 1)
                stt(state0[:, b], bank[b][:, 0:P], 1.0 / (N * N), head_mask[:], ALU.mult, ALU.mult).then_inc(s("st0_cp"), 1)

            def state_out2(b):
                dve.wait_ge(s("st0_cp"), b + 1)
                tt(state[:, b], state0[:, b], bank[b][:, P:2 * P], ALU.mult).then_inc(s("st_cp"), 1)

            for b in range(B):
                m1_out(b)
            for b in range(B):
                state_out(b)
                state_out2(b)

            dve.wait_ge(s("sig_done"), 1)
            tt(choice[:], scores0[:], gate0_bias[:].unsqueeze(1).broadcast_to([P, NT, E0]), ALU.add).then_inc(s("route0_step"), 1)
            dve.wait_ge(s("route0_step"), 1)
            for t in range(NT):
                for gr in range(GROUPS):
                    last = v.max(top8[:, t, gr], choice[:, t, gr * GE:(gr + 1) * GE])
            last.then_inc(s("route0_step"), 1)
            dve.wait_ge(s("route0_step"), 2)
            tt(gscore[:], top8[:, :, :, 0], top8[:, :, :, 1], ALU.add).then_inc(s("route0_step"), 1)
            dve.wait_ge(s("route0_step"), 3)
            for g_ in range(GROUPS):
                me = gscore[:, :, g_:g_ + 1]
                if g_ > 0:
                    last = tt(gcmp[:, :, g_, 0:g_], gscore[:, :, 0:g_], me.broadcast_to([P, NT, g_]), ALU.is_ge)
                if g_ < GROUPS - 1:
                    last = tt(gcmp[:, :, g_, g_ + 1:], gscore[:, :, g_ + 1:], me.broadcast_to([P, NT, GROUPS - 1 - g_]), ALU.is_gt)
            last.then_inc(s("route0_step"), 1)
            dve.wait_ge(s("route0_step"), 4)
            v.tensor_reduce(grank[:], gcmp[:], AX_X, ALU.add).then_inc(s("route0_step"), 1)
            dve.wait_ge(s("route0_step"), 5)
            ts(gmask[:], grank[:], 2.0, None, ALU.is_lt).then_inc(s("route0_step"), 1)
            dve.wait_ge(s("route0_step"), 6)
            tt(masked[:].rearrange("p t (g e) -> p t g e", g=GROUPS), choice[:].rearrange("p t (g e) -> p t g e", g=GROUPS),
               gmask[:].unsqueeze(3).broadcast_to([P, NT, GROUPS, GE]), ALU.mult).then_inc(s("route0_step"), 1)
            dve.wait_ge(s("route0_step"), 7)
            for t in range(NT):
                last = v.max(best8[:, t], masked[:, t])
            last.then_inc(s("route0_step"), 1)
            dve.wait_ge(s("route0_step"), 8)
            for t in range(NT):
                last = v.match_replace(replaced[:, t], best8[:, t], masked[:, t], FAR)
            last.then_inc(s("route0_step"), 1)
            dve.wait_ge(s("route0_step"), 9)
            ts(taken[:], replaced[:], FAR, None, ALU.is_equal).then_inc(s("route0_step"), 1)
            dve.wait_ge(s("route0_step"), 10)
            tt(gate0[:], taken[:], scores0[:], ALU.mult).then_inc(s("route0_step"), 1)
            dve.wait_ge(s("route0_step"), 11)
            v.tensor_reduce(wsum[:], gate0[:], AX_X, ALU.add).then_inc(s("route0_step"), 1)
            dve.wait_ge(s("route0_step"), 12)
            ts(wsum_eps[:], wsum[:], 1e-20, None, ALU.add).then_inc(s("route0_step"), 1)
            dve.wait_ge(s("route0_step"), 13)
            v.reciprocal(wrec[:], wsum_eps[:]).then_inc(s("route0_step"), 1)
            dve.wait_ge(s("route0_step"), 14)
            stt(gate0_rest[:], gate0[:], ROUTED, wrec[:].unsqueeze(2).broadcast_to([P, NT, E0]), ALU.mult, ALU.mult).then_inc(s("route0_step"), 1)
            dve.wait_ge(s("route0_step"), 15)
            v.tensor_copy(gate0_parts[:, :, 0], gate0_rest[:]).then_inc(s("route0_step"), 1)
            dve.wait_ge(s("route0_step"), 16)
            tt(gate0_rest2[:], gate0_rest[:], gate0_parts[:, :, 0], ALU.subtract).then_inc(s("route0_step"), 1)
            dve.wait_ge(s("route0_step"), 17)
            v.tensor_copy(gate0_parts[:, :, 1], gate0_rest2[:]).then_inc(s("route0_step"), 1)
            dve.wait_ge(s("route0_step"), 18)
            tt(gate0_parts[:, :, 2], gate0_rest2[:], gate0_parts[:, :, 1], ALU.subtract).then_inc(s("parts_done"), 1)

            attn_tile = lambda t: bank[t // TB][:, (t % TB) * P:(t % TB + 1) * P]
            for b in range(B):
                dve.wait_ge(s("at_mm"), b + 1)
                layer_norm(b, attn_tile, None, "at_stat", "at_var", None, None)
                if b >= 1:
                    normalise(b - 1, attn_tile, lambda t: attn_n[:, t], "at_pow", "at_norm")
            normalise(B - 1, attn_tile, lambda t: attn_n[:, t], "at_pow", "at_norm")
            dve.wait_ge(s("borow_mm"), 1)
            tt(borow[:], bank[4][0:1, 0:P], rows[:, 4 * P:5 * P], ALU.add).then_inc(s("borow_cp"), 1)

            UNITS = PAIRS + 1
            dve.wait_ge(s("polar_const"), 3 * len(POLAR))
            dve.wait_ge(s("polar_x0"), 1)
            with dve.Fori(0, B) as i:
                def polar_step(q):
                    r, stage = divmod(q - 1, 5)
                    if q < 1 or r >= POLAR_PER_BATCH:
                        return
                    n = i * POLAR_PER_BATCH + r

                    def co(m):
                        return coef[:, bass.ds(n * 3 + m, 1)]
                    if stage == 0:
                        ts(polar_ai[:], ident[:], co(0), None, ALU.mult).then_inc(s("polar_ai_done"), 1)
                        dve.wait_ge(s("polar_a_mm"), n + 1)
                        v.tensor_copy(polar_gx[:], bank[7][:, 0:256]).then_inc(s("polar_gx_cp"), 1)
                        dve.wait_ge(s("polar_gx_cp"), n + 1)
                        stt(polar_ab[:], polar_gx[:, 0:P], co(1), polar_ai[:], ALU.mult, ALU.add).then_inc(s("polar_ab_done"), 1)
                    elif stage == 1:
                        dve.wait_ge(s("polar_a2_mm"), n + 1)
                        dve.wait_ge(s("polar_ab_done"), n + 1)
                        stt(polar_b[:], bank[7][:, 0:P], co(2), polar_ab[:], ALU.mult, ALU.add).then_inc(s("polar_b_done"), 1)
                    elif stage == 2:
                        dve.wait_ge(s("polar_x_mm"), n + 1)
                        v.tensor_copy(polar_x[:], bank[7][:, 0:P]).then_inc(s("polar_x_cp"), 1)

                for u in range(UNITS):
                    k = u % 2
                    dve.wait_ge(s("silu_done"), i * UNITS + (u + 1))
                    dve.wait_ge(s("u_mm"), i * UNITS + (u + 1))
                    if u >= 2:
                        dve.wait_ge(s("dn_mm"), i * UNITS + (u - 1))
                    if u == 0:
                        tt(h0[:, k], silu_g[:, k], bank[2 + k][:], ALU.mult).then_inc(s("h0_done"), 1)
                    else:
                        tt(silu_gu[:, k], silu_g[:, k], bank[2 + k][:], ALU.mult).then_inc(s("gu_done"), 1)
                        dve.wait_ge(s("gu_done"), i * PAIRS + u)
                        dve.wait_ge(s("gb_mm"), i * PAIRS + u)
                        tt(h0[:, k], silu_gu[:, k], bank[4 + k][:], ALU.mult).then_inc(s("h0_done"), 1)
                    polar_step(u)
                dve.wait_ge(s("y0T_mm"), i + 1)
                tt(sg[:], s_tok[:, bass.ds(i * TB, TB)].rearrange("p j c -> p (j c)"), bank[7][:], ALU.mult).then_inc(s("sg_done"), 1)
                dve.wait_ge(s("sg_done"), i + 1)
                xi = x[:, bass.ds(i * TB, TB)].rearrange("p j c -> p (j c)")
                tt(xi, xi, sg[:], ALU.add).then_inc(s("x1_done"), 1)

            dve.wait_ge(s("x1_done"), B)
            for b in range(B):
                layer_norm(b, lambda t: x[:, t], None, "l1_stat", "l1_var", None, None)
                if b >= 1:
                    normalise(b - 1, lambda t: x[:, t], lambda t: xn[:, t, 0:P], "l1_pow", "l1_norm")
            normalise(B - 1, lambda t: x[:, t], lambda t: xn[:, t, 0:P], "l1_pow", "l1_norm")
            dve.wait_ge(s("log1_mm"), 1)
            tt(logits1[:], bank[0][:, 0:NT * E1].rearrange("p (t e) -> p t e", t=NT),
               gate1_bias[:].unsqueeze(1).broadcast_to([P, NT, E1]), ALU.add).then_inc(s("log1_cp"), 1)
            dve.wait_ge(s("log1_cp"), 1)
            v.tensor_reduce(lmax[:], logits1[:], AX_X, ALU.max).then_inc(s("route1_step"), 1)
            dve.wait_ge(s("route1_step"), 1)
            tt(lsub[:], logits1[:], lmax[:].unsqueeze(2).broadcast_to([P, NT, E1]), ALU.subtract).then_inc(s("lsub_done"), 1)
            v.memset(ecmp[:], 0.0).then_inc(s("route1_step"), 1)
            dve.wait_ge(s("route1_step"), 2)
            for e in range(E1):
                me = logits1[:, :, e:e + 1]
                if e > 0:
                    last = tt(ecmp[:, :, e, 0:e], logits1[:, :, 0:e], me.broadcast_to([P, NT, e]), ALU.is_ge)
                if e < E1 - 1:
                    last = tt(ecmp[:, :, e, e + 1:], logits1[:, :, e + 1:], me.broadcast_to([P, NT, E1 - 1 - e]), ALU.is_gt)
            last.then_inc(s("route1_step"), 1)
            dve.wait_ge(s("route1_step"), 3)
            v.tensor_reduce(erank[:], ecmp[:], AX_X, ALU.add).then_inc(s("route1_step"), 1)
            dve.wait_ge(s("lexp_done"), 1)
            v.tensor_reduce(lsum[:], lexp[:], AX_X, ALU.add).then_inc(s("route1_step"), 1)
            dve.wait_ge(s("route1_step"), 4)
            ts(emask[:], erank[:], 2.0, None, ALU.is_lt).then_inc(s("route1_step"), 1)
            dve.wait_ge(s("route1_step"), 5)
            v.reciprocal(lrec[:], lsum[:]).then_inc(s("route1_step"), 1)
            dve.wait_ge(s("route1_step"), 7)
            tt(probs1[:], lexp[:], lrec[:].unsqueeze(2).broadcast_to([P, NT, E1]), ALU.mult).then_inc(s("route1_step"), 1)
            dve.wait_ge(s("route1_step"), 8)
            dve.wait_ge(s("route1_step"), 6)
            tt(gate1[:], probs1[:], emask[:], ALU.mult).then_inc(s("gate1_done"), 1)
            dve.wait_ge(s("gate1_done"), 1)
            dve.wait_ge(s("acc_cp"), B)

            def products(k, b):
                dve.wait_ge(s("left_tok_cp"), k + 1)
                left = bank[1][:].rearrange("p (j l d) -> p j l d", j=TB, l=LANES).unsqueeze(3)
                right = x_tok[:, b].rearrange("p j (m d) -> p j m d", m=LANES)[:, :, 0:LANES - 1].unsqueeze(2)
                tt(prod[:, b % 2, :, :, 0:LANES - 1], left.broadcast_to([P, TB, LANES, LANES - 1, LD]),
                   right.broadcast_to([P, TB, LANES, LANES - 1, LD]), ALU.mult).then_inc(s("prod_done"), 1)

            def add_lanes(k, b):
                dve.wait_ge(s("mix2_done"), k + 1)
                m = mix2[:, b % 2].rearrange("p j l m d -> p (j l) m d")
                tt(z[:, b % 2].rearrange("p j (l d) -> p (j l) d", l=LANES), m[:, :, 0], m[:, :, 1],
                   ALU.add).then_inc(s("z_done"), 1)

            def softmax_shift(k, b):
                dve.wait_ge(s("prod_done"), k + 1)
                dve.wait_ge(s("last_prod"), k + 1)
                v.tensor_reduce(score[:, b % 2], prod[:, b % 2], AX_X, ALU.add).then_inc(s("score_done"), 1)
                dve.wait_ge(s("score_done"), k + 1)
                v.tensor_reduce(smax[:, b % 2], score[:, b % 2], AX_X, ALU.max).then_inc(s("smax_done"), 1)
                dve.wait_ge(s("smax_done"), k + 1)
                tt(ssub[:, b % 2], score[:, b % 2], smax[:, b % 2].unsqueeze(3).broadcast_to([P, TB, LANES, LANES]),
                   ALU.subtract).then_inc(s("ssub_done"), 1)

            def mean_square(k, b):
                stt(eps_ss[:, b % 2], ssum[:, b % 2], RMS_EPS, ssum[:, b % 2], ALU.mult, ALU.mult).then_inc(s("epsss_done"), 1)
                dve.wait_ge(s("zsq_done"), k + 1)
                v.tensor_reduce(z_ss[:, b % 2], z_sq[:, b % 2].rearrange("p j (l d) -> p j l d", l=LANES), AX_X,
                                ALU.add).then_inc(s("zss_done"), 1)
                dve.wait_ge(s("epsss_done"), k + 1)
                dve.wait_ge(s("zss_done"), k + 1)
                stt(z_ms[:, b % 2], z_ss[:, b % 2], 1.0 / LD, eps_ss[:, b % 2], ALU.mult, ALU.add).then_inc(s("zms_done"), 1)

            def mix_values(k, b):
                dve.wait_ge(s("sexp_done"), k + 1)
                v.tensor_reduce(ssum[:, b % 2], sexp[:, b % 2], AX_X, ALU.add).then_inc(s("ssum_done"), 1)
                dve.wait_ge(s("v_last_cp"), k + 1)
                values = bank[2][:].rearrange("p (j m d) -> p j m d", j=TB, m=LANES)[:, :, 0:LANES - 1].unsqueeze(2)
                tt(mix[:, b % 2, :, :, 0:LANES - 1],
                   sexp[:, b % 2, :, :, 0:LANES - 1].unsqueeze(4).broadcast_to([P, TB, LANES, LANES - 1, LD]),
                   values.broadcast_to([P, TB, LANES, LANES - 1, LD]), ALU.mult).then_inc(s("mix_done"), 1)
                dve.wait_ge(s("ssum_done"), k + 1)

            def scale_z(k, b):
                dve.wait_ge(s("zr_done"), k + 1)
                tt(zn[:].rearrange("p j (l d) -> p j l d", l=LANES), z[:, b % 2].rearrange("p j (l d) -> p j l d", l=LANES),
                   z_r[:, b % 2].unsqueeze(3).broadcast_to([P, TB, LANES, LD]), ALU.mult).then_inc(s("zn_done"), 1)

            def expert_sum(e, blk):
                n = e * B + blk
                if blk == 0:
                    v.tensor_copy(gate1_now[:], gate1[:, :, bass.ds(e, 1)].rearrange("p t e -> p (t e)")).then_inc(s("gate_now_done"), 1)
                    dve.wait_ge(s("gate_now_done"), e + 1)
                dve.wait_ge(s("ffn_down"), n + 1)
                for j in range(TB):
                    t = blk * TB + j
                    stt(acc[:, t], bank[7][:, j * P:(j + 1) * P], gate1_now[:, t:t + 1], acc[:, t],
                        ALU.mult, ALU.add).then_inc(s("ffn_acc"), 1)

            def slot(k, b, this=True, before=True, expert=None):
                if this:
                    products(k, b)
                if before:
                    add_lanes(k - 1, (b - 1) % B)
                if this:
                    softmax_shift(k, b)
                if before:
                    mean_square(k - 1, (b - 1) % B)
                if this:
                    mix_values(k, b)
                if before:
                    scale_z(k - 1, (b - 1) % B)
                if expert:
                    expert_sum(*expert)

            slot(0, 0, before=False)
            with dve.Fori(0, LEVELS - 1) as lev:
                for j in range(B):
                    slot(lev * B + (j + 1), (j + 1) % B, expert=(lev, j))
            for k in range(1, B):
                slot((LEVELS - 1) * B + k, k)
            slot(LEVELS * B, 0, this=False)

            for b in range(B):
                dve.wait_ge(s("v1_cp"), b + 1)
                dve.wait_ge(s("qT_mm"), b + 1)
                tt(qvT[:, b], sumT[:, b], bank[b][:], ALU.mult).then_inc(s("qv_done"), 1)
            for b in range(B):
                dve.wait_ge(s("yp_mm"), b + 1)
                dve.wait_ge(s("gl1_done"), b + 1)
                gb = acc[:, b * TB:(b + 1) * TB].rearrange("p j c -> p (j c)")
                tt(gb, bank[b][:], gb, ALU.mult).then_inc(s("o_mul"), 1)
                dve.wait_ge(s("o_mul"), b + 1)
                xb = x[:, b * TB:(b + 1) * TB].rearrange("p j c -> p (j c)")
                tt(xb, xb, gb, ALU.add).then_inc(s("o_done"), 1)


_OUT_SHAPE = (B, N, P)


def kernel(**inputs):
    import numpy as np
    import concourse.bacc as bacc
    from concourse.bass_utils import run_bass_kernel_spmd as run

    w = {k: np.asarray(v) for k, v in inputs.items()}
    swap = lambda m: np.swapaxes(m, -1, -2)

    def experts_in(shared, experts):
        rows = np.concatenate([shared, experts.reshape(E0 * I0, P)]).reshape(PAIRS + 1, P, P)
        return rows.transpose(2, 0, 1)

    down = np.concatenate([swap(w["L0_ffn_shared_down"])[None],
                           swap(w["L0_ffn_expert_down"]).reshape(PAIRS, P, P)])
    arrays = {
        "x": w["L0_attn_x"],
        "cols": np.stack([w["L0_attn_bq"], w["L0_attn_ln_g"], w["L0_attn_ln_b"], w["L1_attn_identity"]], 1),
        "rows": np.concatenate([w["L0_attn_bk"].reshape(-1), w["L0_attn_bv"].reshape(-1), w["L0_attn_bo"]])[None],
        "gate0_bias": w["L0_ffn_gate_bias"],
        "gate1_bias": w["L1_ffn_gate_b"],
        "attn_w": np.stack([swap(w["L0_attn_Wq"]), *w["L0_attn_Wk"], *w["L0_attn_Wv"], w["L0_attn_Wo"]], 1),
        "gate0": swap(w["L0_ffn_gate_w"]),
        "wg": experts_in(w["L0_ffn_shared_gate"], w["L0_ffn_expert_gate"]),
        "wu": experts_in(w["L0_ffn_shared_up"], w["L0_ffn_expert_up"]),
        "wd": down.transpose(1, 0, 2),
        "scan_raw": w["L1_attn_W_scan_raw"],
        "l1_w": np.stack([swap(w["L1_attn_W_up"]), swap(w["L1_attn_W_v"]), swap(w["L1_attn_W_proj"])], 1),
        "gate1": swap(w["L1_ffn_gate_w"]),
        "w1": w["L1_ffn_w1"].reshape(E1, P, HC, P),
        "b1": w["L1_ffn_b1"].reshape(E1, HC, P).transpose(2, 0, 1),
        "w2": w["L1_ffn_w2"].reshape(E1, HC, P, P).transpose(2, 0, 1, 3),
        "b2": w["L1_ffn_b2"],
    }
    nc = bacc.Bacc("TRN2", target_bir_lowering=False, num_devices=1)
    feed, args = {}, []
    for name, value in arrays.items():
        value = np.ascontiguousarray(value)
        feed[f"in_{name}"] = value
        args.append(nc.dram_tensor(f"in_{name}", value.shape, mybir.dt.from_np(value.dtype), kind="ExternalInput").ap())
    args.append(nc.dram_tensor("out", _OUT_SHAPE, F32, kind="ExternalOutput").ap())
    build(nc, *args)
    return run(nc, [feed], core_ids=[0]).results[0]["out"]
```

```python
from contextlib import ExitStack

import numpy as np
import concourse.bass as bass
from concourse import mybir

F32 = mybir.dt.float32
BF16 = mybir.dt.bfloat16
F32R = mybir.dt.float32r
ALU = mybir.AluOpType
ACT = mybir.ActivationFunctionType
AX_X = mybir.AxisListType.X

P = 128
B, N = 4, 512
TB = N // P
NT = B * TB
E0, I0 = 32, 64
PAIRS = E0 * I0 // P
GROUPS, GE = 4, 8
TOP0 = 8
E1, H1 = 8, 512
HC = H1 // P
HEADS, HD = 16, 8
LANES, LD = 4, 32
LEVELS = 9
PAD = N // 2
LN_EPS = 1e-5
RMS_EPS = 1e-8
ROUTED = 2.5
FAR = -2.0 ** 127
EXP_LN = "natural_log_exp_and_others"
SHARED = 29 * 1024
CONSTS = 17
IDENT_READY = 3

POLAR = [(8.51425808, -25.281576, 18.7673094), (4.2570752, -3.16016629, 0.586476766),
         (4.25682787, -3.15999522, 0.586457253), (4.25577537, -3.15926721, 0.586374211),
         (4.25130191, -3.15617245, 0.586021201), (4.23238747, -3.14307812, 0.584527605),
         (4.15415638, -3.08875796, 0.578332236), (3.85835916, -2.88082531, 0.554631634),
         (3.0495984, -2.2849888, 0.487060827), (2.11205594, -1.49383647, 0.400102503),
         (1.87838366, -1.2537545, 0.375375648), (1.87500002, -1.25000002, 0.375000005)]
POLAR_PER_BATCH = len(POLAR) // B

UNITS = PAIRS + 1
HEAD = 6


def is_turn(i, peeled):
    return isinstance(i, int) and i == peeled


def turn_positions(i):
    return range(UNITS - HEAD if is_turn(i, -1) else 0, UNITS - HEAD if is_turn(i, B - 1) else UNITS)


def unit_at(i, p):
    u = (p + HEAD) % UNITS
    gated = i * PAIRS + (p + HEAD if p + HEAD < UNITS else p + HEAD - 1)
    return i * UNITS + (p + HEAD), u, gated


def pair_user(n, p):
    return n if p == 0 else n - 2 if p == 1 else n - 1


def ring_user(n, p):
    return n - 1 if p < 2 else n - 4 if p == 2 else n - 2


def after(engine, semaphore, value):
    if not isinstance(value, int) or value > 0:
        engine.wait_ge(semaphore, value)


def build(nc, x_d, cols_d, rows_d, gate0_bias_d, gate1_bias_d, attn_w_d, gate0_d, wg_d, wu_d, wd_d,
          scan_raw_d, l1_w_d, gate1_d, w1_d, b1_d, w2_d, b2_d, out_d):
    ctx = ExitStack()
    with ctx:
        def sb(name, shape, dt=F32):
            return ctx.enter_context(nc.sbuf_tensor(name, shape, dt))

        def sem(name):
            return ctx.enter_context(nc.semaphore(name))

        shared = sb("shared", [P, SHARED])
        used = {0: 0, 1: 0}

        def carve(layer, shape):
            size = int(np.prod(shape[1:]))
            v = shared[:, used[layer]:used[layer] + size]
            used[layer] += size
            assert used[layer] <= SHARED
            dims = "abcdef"[:len(shape) - 1]
            if len(dims) > 1:
                v = v.rearrange(f"p ({' '.join(dims)}) -> p {' '.join(dims)}", **dict(zip(dims, shape[1:])))
            return v

        bank = [ctx.enter_context(nc.psum_tensor(f"bank{k}", [P, 512], F32)) for k in range(8)]

        cols = sb("cols", [P, 4])
        rows = carve(0, [P, 5 * P])[0:1]
        gate0_bias = sb("gate0_bias", [P, E0])
        gate1_bias = sb("gate1_bias", [P, E1])
        attn_w = carve(0, [P, 6, P])
        gate0_w = sb("gate0_w", [P, E0])
        wg = carve(0, [P, PAIRS + 1, P])
        wu = carve(0, [P, PAIRS + 1, P])
        wd = carve(0, [P, PAIRS + 1, P])
        polar_x = sb("polar_x", [P, P])
        l1_w = sb("l1_w", [P, 3, P])
        gate1_w = sb("gate1_w", [P, E1])
        w1 = sb("w1", [P, HC, P])
        b1 = sb("b1", [P, E1, HC])
        w2 = sb("w2", [P, HC, P])
        b2 = sb("b2", [E1, P])

        ident = sb("ident", [P, P])
        ident_bf = sb("ident_bf", [P, P], BF16)
        ones = sb("ones", [P, P])
        tokens_n = sb("tokens_n", [1, 1])
        head_mask = sb("head_mask", [P, P])
        inv_lane = sb("inv_lane", [P, TB, LANES])
        pair_sel = sb("pair_sel", [3 * E0, E0, I0], BF16)
        coef = sb("coef", [P, 3 * len(POLAR)])

        x = sb("x", [P, NT, P])
        xn = carve(0, [P, NT, P + 1])
        xnT = sb("xnT", [P, B * N])
        xnT_hi = sb("xnT_hi", [P, B * N], F32R)
        xnT_lo = sb("xnT_lo", [P, B * N], F32R)
        wgu_hi = sb("wgu_hi", [P, 2, PAIRS + 1, P], F32R)
        wgu_lo = sb("wgu_lo", [P, 2, PAIRS + 1, P], F32R)
        s_tok = carve(0, [P, NT, P])
        ln_stats = sb("ln_stats", [P, NT, 6])
        ln_mv = sb("ln_mv", [P, NT, 2])
        ln_var = sb("ln_var", [P, NT])
        ln_rstd = sb("ln_rstd", [P, NT])
        ln_log = sb("ln_log", [P, 3 * NT + 1])

        mq = carve(0, [P, B, P])
        attn_n = carve(0, [P, NT, P])
        xn1 = attn_n
        attn_nT = carve(0, [P, B * N])
        wo_g = carve(0, [P, P])
        borow = sb("borow", [1, P])

        scores0 = carve(0, [P, NT, E0])
        choice = carve(0, [P, NT, E0])
        top8 = carve(0, [P, NT, GROUPS, 8])
        gscore = carve(0, [P, NT, GROUPS])
        gcmp = carve(0, [P, NT, GROUPS, GROUPS])
        grank = carve(0, [P, NT, GROUPS])
        gmask = carve(0, [P, NT, GROUPS])
        masked = carve(0, [P, NT, E0])
        best8 = carve(0, [P, NT, 8])
        replaced = carve(0, [P, NT, E0])
        taken = carve(0, [P, NT, E0])
        wsum = sb("wsum", [P, NT])
        wsum_eps = sb("wsum_eps", [P, NT])
        wrec = sb("wrec", [P, NT])
        gate0 = carve(0, [P, NT, E0])
        gate0_rest = carve(0, [P, NT, E0])
        gate0_rest2 = carve(0, [P, NT, E0])
        gate0_parts = sb("gate0_parts", [P, NT, 3, E0], BF16)
        gate0T = sb("gate0T", [3 * E0, B * N], BF16)

        mark = used[0]
        gram = carve(0, [P, B, P + 1])
        srow = carve(0, [P, B, P])[0:1]
        m1 = carve(0, [P, B, 2 * P])
        m1row = carve(0, [P, B, 2 * P])[0:1]
        state0 = carve(0, [P, B, P])
        state = carve(0, [P, B, P])
        mqrow = carve(0, [P, B, P])[0:1]
        used[0] = mark
        silu_g = carve(0, [P, 2, N])
        silu_gu = carve(0, [P, 2, N])
        h0 = carve(0, [P, 3, N])
        gl0T = carve(0, [P, N])
        sg = carve(0, [P, N])
        polar_gx = sb("polar_gx", [P, 2 * P])
        polar_ai = carve(0, [P, P])
        polar_ab = carve(0, [P, P])
        polar_b = carve(0, [P, P])
        polar_sq = carve(0, [P, P])
        polar_col = sb("polar_col", [P, 1])
        polar_sum = sb("polar_sum", [P, 1])
        polar_r = sb("polar_r", [P, 1])

        logits1 = sb("logits1", [P, NT, E1])
        lmax = sb("lmax", [P, NT])
        lsum = sb("lsum", [P, NT])
        lrec = sb("lrec", [P, NT])
        gate1 = sb("gate1", [P, NT, E1])

        xT = carve(1, [P, B, PAD + N])
        x_tok = carve(1, [P, B, TB, P])
        left_tok = carve(1, [P, B, TB, P])
        leftT = carve(1, [P, B, N])
        sumT = carve(1, [P, B, N])
        prod = carve(1, [P, 2, TB, LANES, LANES, LD])
        score = carve(1, [P, 2, TB, LANES, LANES])
        v_tok = carve(1, [P, 2, TB, P])
        smax = sb("smax", [P, 2, TB, LANES])
        ssub = carve(1, [P, 2, TB, LANES, LANES])
        sexp = carve(1, [P, 2, TB, LANES, LANES])
        ssum = sb("ssum", [P, 2, TB, LANES])
        mark = used[1]
        used[1] += 2048
        ecmp = carve(1, [P, NT, E1, E1])
        lsub = carve(1, [P, NT, E1])
        lexp = carve(1, [P, NT, E1])
        erank = carve(1, [P, NT, E1])
        emask = carve(1, [P, NT, E1])
        probs1 = carve(1, [P, NT, E1])
        used[1] = mark
        mix = carve(1, [P, 2, TB, LANES, LANES, LD])
        mix2 = carve(1, [P, 2, TB, LANES, 2, LD])
        z = carve(1, [P, 2, TB, P])
        z_sq = carve(1, [P, 2, TB, P])
        z_ss = sb("z_ss", [P, 2, TB, LANES])
        eps_ss = sb("eps_ss", [P, 2, TB, LANES])
        z_ms = sb("z_ms", [P, 2, TB, LANES])
        z_ln = sb("z_ln", [P, 2, TB, LANES])
        z_rs = sb("z_rs", [P, 2, TB, LANES])
        z_r = sb("z_r", [P, 2, TB, LANES])
        zn = carve(1, [P, TB, P])
        mark = used[1]
        gate1T = carve(1, [P, B * N])[0:E1]
        used[1] = mark
        hT = carve(1, [P, HC, N])
        b1_now = sb("b1_now", [P, HC])
        gate1_now = sb("gate1_now", [P, NT])
        acc = carve(1, [P, NT, P])
        qvT = leftT

        S = {}

        def s(name):
            if name not in S:
                S[name] = sem(name)
            return S[name]

        for name in (
            "ld_x0 ld_x1 ld_x2 ld_x3 ld_w1_0 ld_w1_1 ld_w1_2 ld_w1_3 ld_scan ld_small ld_l1 st_out const "
            "polar_const polar_sq_done polar_sum_mm polar_sum_cp polar_r_done polar_x0 ln_stat ln_var_done "
            "ln_pow ln_norm xnT_mm xnT_cp wfold wog_done borow_mm borow_cp gram_mm gram_cp m1_mm m1_cp st_mm "
            "st0_cp st_cp mq_mm mq_cp at_mm at_stat at_var at_pow at_norm atT_mm atT_cp so_mm so_cp logit_mm "
            "sig_done parts_done g0T_mm g0T_cp g_mm u_mm gb_mm silu_done gu_done h0_done dn_mm y0_silu y0T_mm "
            "sg_done x1_done polar_ai_done polar_a_mm polar_gx_cp polar_ab_done polar_a2_mm polar_b_done "
            "polar_x_mm polar_x_cp l1_stat l1_var l1_pow l1_norm x1T_mm x1T_cp log1_mm log1_cp lsub_done "
            "lexp_done gate1_done g1T_mm g1T_cp acc_mm uptok_mm pad_done state_mm xT_cp leftT_cp left_mm "
            "left_tok_cp sum_done prod_done last_prod score_done smax_done ssub_done sexp_done ssum_done v_mm "
            "v_cp mix_done last_mix mix2_done z_done zsq_done zss_done epsss_done zms_done zln_done zrs_done "
            "zr_done zn_done xtok_done ffn_up ffn_relu ffn_down ffn_acc qT_mm b1_now_done gate_now_done v1_mm "
            "v1_cp qv_done yp_mm gl1_done o_mul o_done route0_step route1_step ld_wd ld_wg ld_wu "
            "w_hi_done w_lo_done xnT_lo_done ld_w2 acc_done acc_zero ecmp_zero xnT_hi_cp "
        ).split():
            s(name)

        block = ctx.enter_context(nc.Block())

        @block.sync
        def _(sp):
            xv = x_d.rearrange("b (j p) c -> p b j c", p=P)
            for b in range(B):
                sp.dma_start(x[:, b * TB:(b + 1) * TB, :], xv[:, b]).then_inc(s(f"ld_x{b}"), 16)
            sp.dma_start(polar_x[:], scan_raw_d).then_inc(s("ld_scan"), 16)
            sp.dma_start(attn_w[:], attn_w_d).then_inc(s("ld_small"), 16)
            sp.dma_start(cols[:], cols_d).then_inc(s("ld_small"), 16)
            sp.dma_start(rows[:], rows_d).then_inc(s("ld_small"), 16)
            sp.dma_start(gate0_w[:], gate0_d).then_inc(s("ld_small"), 16)
            sp.dma_start(gate0_bias[:], gate0_bias_d.partition_broadcast(P)).then_inc(s("ld_small"), 16)
            sp.dma_start(wg[:], wg_d).then_inc(s("ld_wg"), 16)
            sp.dma_start(wu[:], wu_d).then_inc(s("ld_wu"), 16)
            sp.dma_start(wd[:], wd_d).then_inc(s("ld_wd"), 16)
            sp.dma_start(l1_w[:], l1_w_d).then_inc(s("ld_l1"), 16)
            sp.dma_start(gate1_w[:], gate1_d).then_inc(s("ld_l1"), 16)
            sp.dma_start(gate1_bias[:], gate1_bias_d.partition_broadcast(P)).then_inc(s("ld_l1"), 16)
            sp.dma_start(b1[:], b1_d).then_inc(s("ld_l1"), 16)
            sp.dma_start(b2[:], b2_d).then_inc(s("ld_l1"), 16)
            for c in range(HC):
                sp.dma_start(w1[:, c], w1_d[0, :, c]).then_inc(s(f"ld_w1_{c}"), 16)
            sp.dma_start(w2[:], w2_d[:, 0]).then_inc(s("ld_w2"), 16)
            with sp.Fori(0, E1 - 1) as e:
                for c in range(HC):
                    sp.wait_ge(s("ffn_up"), e * (B * HC) + (B - 1) * HC + c + 1)
                    sp.dma_start(w1[:, c], w1_d[bass.ds(e + 1, 1), :, c].rearrange("e p h -> (e p) h")).then_inc(s(f"ld_w1_{c}"), 16)
                sp.wait_ge(s("ffn_down"), (e + 1) * B)
                sp.dma_start(w2[:], w2_d[:, bass.ds(e + 1, 1)].rearrange("p e c o -> p (e c) o")).then_inc(s("ld_w2"), 16)
            ov = out_d.rearrange("b (j p) c -> p b j c", p=P)
            for b in range(B):
                sp.wait_ge(s("o_done"), b + 1)
                sp.dma_start(ov[:, b], x[:, b * TB:(b + 1) * TB, :]).then_inc(s("st_out"), 16)
            sp.wait_ge(s("st_out"), 16 * B)

        LD_SMALL, LD_L1 = 16 * 5, 16 * 5

        @block.gpsimd
        def _(pool):
            g = nc.gpsimd
            cdone = s("const")
            g.memset(ones[:], 1.0).then_inc(cdone, 1)
            g.memset(ident[:], 0.0).then_inc(cdone, 1)
            n = 2
            pool.wait_ge(cdone, n)
            g.affine_select(out=ident[:], in_=ident[:], compare_op=ALU.not_equal, fill=1.0, base=0,
                            pattern=[[-1, P]], channel_multiplier=1).then_inc(cdone, 1)
            n += 1
            assert n == IDENT_READY
            g.memset(tokens_n[:], float(N)).then_inc(cdone, 1)
            g.memset(xn[:, :, P:P + 1], 1.0).then_inc(cdone, 1)
            g.memset(head_mask[:], 1.0).then_inc(cdone, 1)
            g.memset(pair_sel[:], 0.0).then_inc(cdone, 1)
            n += 4
            for lane in range(LANES):
                g.memset(inv_lane[:, :, lane:lane + 1], 1.0 / (1 + lane)).then_inc(cdone, 1)
                n += 1
            g.memset(gcmp[:], 0.0).then_inc(cdone, 1)
            n += 1
            pool.wait_ge(cdone, n)
            hm = head_mask[:].rearrange("p (h d) -> p h d", h=HEADS)
            g.affine_select(out=hm, in_=hm, compare_op=ALU.is_ge, fill=0.0, base=0,
                            pattern=[[-HD, HEADS], [0, HD]], channel_multiplier=1).then_inc(cdone, 1)
            n += 1
            pool.wait_ge(cdone, n)
            g.affine_select(out=hm, in_=hm, compare_op=ALU.is_ge, fill=0.0, base=HD - 1,
                            pattern=[[HD, HEADS], [0, HD]], channel_multiplier=-1).then_inc(cdone, 1)
            n += 1
            for part in range(3):
                v = pair_sel[part * E0:(part + 1) * E0]
                pool.wait_ge(cdone, n)
                g.affine_select(out=v, in_=v, compare_op=ALU.not_equal, fill=1.0, base=0,
                                pattern=[[-1, E0], [0, I0]], channel_multiplier=1).then_inc(cdone, 1)
                n += 1
            assert n == CONSTS
            pool.wait_ge(cdone, n)
            for k, abc in enumerate(POLAR):
                for m, v in enumerate(abc):
                    g.memset(coef[:, 3 * k + m:3 * k + m + 1], float(v)).then_inc(s("polar_const"), 1)

            for b in range(B):
                pool.wait_ge(s("xnT_hi_cp"), b + 1)
                part = slice(b * N, (b + 1) * N)
                g.tensor_tensor(xnT_lo[:, part], xnT[:, part], xnT_hi[:, part], ALU.subtract).then_inc(s("xnT_lo_done"), 1)
            for m, (w, loaded) in enumerate(((wg, "ld_wg"), (wu, "ld_wu"))):
                pool.wait_ge(s(loaded), 16)
                g.tensor_copy(wgu_hi[:, m], w[:]).then_inc(s("w_hi_done"), 1)
                pool.wait_ge(s("w_hi_done"), m + 1)
                g.tensor_tensor(wgu_lo[:, m], w[:], wgu_hi[:, m], ALU.subtract).then_inc(s("w_lo_done"), 1)

            pool.wait_ge(s("ld_small"), LD_SMALL)
            pool.wait_ge(cdone, n)
            pool.wait_ge(s("x1_done"), B)
            for b in range(B):
                g.tensor_scalar(xT[:, b, 0:PAD], ones[:, 0:1].broadcast_to([P, PAD]), cols[:, 3:4], 1.0,
                                ALU.mult, ALU.mult).then_inc(s("pad_done"), 1)
            g.memset(ecmp[:], 0.0).then_inc(s("ecmp_zero"), 1)
            g.memset(acc[:], 0.0).then_inc(s("acc_zero"), 1)

            def sum_inputs(k, b):
                pool.wait_ge(s("leftT_cp"), k + 1)
                g.tensor_tensor(sumT[:, b], leftT[:, b], xT[:, b, PAD:PAD + N],
                                ALU.add).then_inc(s("sum_done"), 1)

            def last_product(k, b):
                pool.wait_ge(s("left_tok_cp"), k + 1)
                pool.wait_ge(s("xtok_done"), k + 1)
                g.tensor_tensor(prod[:, b % 2, :, :, LANES - 1],
                                left_tok[:, b].rearrange("p j (l d) -> p j l d", l=LANES),
                                x_tok[:, b, :, (LANES - 1) * LD:].unsqueeze(2).broadcast_to([P, TB, LANES, LD]),
                                ALU.mult).then_inc(s("last_prod"), 1)

            def last_mix(k, b):
                pool.wait_ge(s("sexp_done"), k + 1)
                pool.wait_ge(s("v_cp"), k + 1)
                g.tensor_tensor(mix[:, b % 2, :, :, LANES - 1],
                                sexp[:, b % 2, :, :, LANES - 1].unsqueeze(3).broadcast_to([P, TB, LANES, LD]),
                                v_tok[:, b % 2, :, (LANES - 1) * LD:].unsqueeze(2).broadcast_to([P, TB, LANES, LD]),
                                ALU.mult).then_inc(s("last_mix"), 1)

            def halve_mix(k, b):
                pool.wait_ge(s("mix_done"), k + 1)
                pool.wait_ge(s("last_mix"), k + 1)
                g.tensor_tensor(mix2[:, b % 2].rearrange("p j l m d -> p (j l) (m d)"),
                                mix[:, b % 2, :, :, 0:2].rearrange("p j l m d -> p (j l) (m d)"),
                                mix[:, b % 2, :, :, 2:4].rearrange("p j l m d -> p (j l) (m d)"),
                                ALU.add).then_inc(s("mix2_done"), 1)

            def rms_factor(k, b):
                pool.wait_ge(s("zrs_done"), k + 1)
                g.tensor_tensor(z_r[:, b % 2], z_rs[:, b % 2], inv_lane[:], ALU.mult).then_inc(s("zr_done"), 1)

            def scale_z(k, b):
                pool.wait_ge(s("zr_done"), k + 1)
                g.tensor_tensor(zn[:].rearrange("p j (l d) -> p j l d", l=LANES),
                                z[:, b % 2].rearrange("p j (l d) -> p j l d", l=LANES),
                                z_r[:, b % 2].unsqueeze(3).broadcast_to([P, TB, LANES, LD]), ALU.mult).then_inc(s("zn_done"), 1)

            def new_state(k, b):
                pool.wait_ge(s("zn_done"), k + 1)
                g.tensor_tensor(x_tok[:, b], zn[:], left_tok[:, b], ALU.add).then_inc(s("xtok_done"), 1)

            def slot(k, b, this=True, before=True, before2=True, ahead=True):
                if before:
                    halve_mix(k - 1, (b - 1) % B)
                if before2:
                    rms_factor(k - 2, (b - 2) % B)
                    scale_z(k - 2, (b - 2) % B)
                    new_state(k - 2, (b - 2) % B)
                if ahead:
                    sum_inputs(k + 1, (b + 1) % B)
                    last_product(k + 1, (b + 1) % B)
                if this:
                    last_mix(k, b)

            def level(lev, first=False):
                for j in range(B):
                    slot(lev * B + (j + 1), (j + 1) % B, before2=not (first and j == 0))

            pool.wait_ge(s("const"), CONSTS)
            sum_inputs(0, 0)
            last_product(0, 0)
            slot(0, 0, before=False, before2=False)
            level(0, first=True)
            with pool.Fori(1, LEVELS - 1) as lev:
                level(lev)
            top = LEVELS - 1
            slot(top * B + 1, 1)
            slot(top * B + 2, 2)
            slot(top * B + 3, 3, ahead=False)
            slot(top * B + 4, 0, this=False, ahead=False)
            slot(top * B + 5, 1, this=False, before=False, ahead=False)

        @block.tensor
        def _(pe):
            def mm(out, lhsT, rhs, start=True, stop=True):
                return nc.tensor.matmul(out, lhsT, rhs, start=start, stop=stop)

            def tr(out, in_, idm=None):
                return nc.tensor.transpose(out, in_, ident[:] if idm is None else idm)

            pe.wait_ge(s("const"), IDENT_READY)
            pe.wait_ge(s("polar_sq_done"), 1)
            mm(bank[7][:, 0:1], ones[:], polar_col[:]).then_inc(s("polar_sum_mm"), 1)

            def tokens_to_channels0(b):
                pe.wait_ge(s("ln_norm"), b + 1)
                if b == 3:
                    pe.wait_ge(s("polar_sum_cp"), 1)
                for j in range(TB):
                    last = tr(bank[4 + b][:, j * P:(j + 1) * P], xn[:, b * TB + j, 0:P])
                last.then_inc(s("xnT_mm"), 1)

            def router_logits0(b):
                pe.wait_ge(s("xnT_cp"), b + 1)
                for t in range(b * TB, (b + 1) * TB):
                    last = mm(bank[3][:, t * E0:(t + 1) * E0], xnT[:, t * P:(t + 1) * P], gate0_w[:])
                last.then_inc(s("logit_mm"), 1)

            tokens_to_channels0(0)
            pe.wait_ge(s("ld_small"), LD_SMALL)
            for b in range(1, B):
                tokens_to_channels0(b)
                router_logits0(b - 1)
            router_logits0(B - 1)

            pe.wait_ge(s("const"), CONSTS)
            for b in range(B):
                if b == 3:
                    pe.wait_ge(s("sig_done"), 1)
                for j in range(TB):
                    mm(bank[b][:, 0:P + 1], xn[:, b * TB + j, 0:P], xn[:, b * TB + j, :], j == 0, j == TB - 1)
                for j in range(TB):
                    last = mm(bank[b][0:1, 256:256 + P], ones[:, 0:1], xn[:, b * TB + j, 0:P], j == 0, j == TB - 1)
                last.then_inc(s("gram_mm"), 1)
            pe.wait_ge(s("wfold"), 1)
            wv = attn_w[:, 3:5].rearrange("p k c -> p (k c)")
            for b in range(B):
                pe.wait_ge(s("gram_cp"), b + 1)
                mm(bank[4 + b][:, 0:256], gram[:, b, 0:P], wv, True, False)
                mm(bank[4 + b][:, 0:256], srow[:, b], rows[:, 256:512], False, True)
                mm(bank[4 + b][0:1, 256:512], gram[:, b, P:P + 1], wv, True, False)
                last = mm(bank[4 + b][0:1, 256:512], tokens_n[:], rows[:, 256:512], False, True)
                last.then_inc(s("m1_mm"), 1)
            for b in range(B):
                pe.wait_ge(s("m1_cp"), b + 1)
                for k in range(2):
                    mm(bank[b][:, k * P:(k + 1) * P], attn_w[:, 1 + k], m1[:, b, k * P:(k + 1) * P], True, False)
                    last = mm(bank[b][:, k * P:(k + 1) * P], rows[:, k * P:(k + 1) * P],
                              m1row[:, b, k * P:(k + 1) * P], False, True)
                last.then_inc(s("st_mm"), 1)
            for b in range(B):
                pe.wait_ge(s("st_cp"), b + 1)
                mm(bank[4 + b][:, 0:P], attn_w[:, 0], state[:, b])
                mm(bank[4 + b][0:1, P:2 * P], cols[:, 0:1], state[:, b]).then_inc(s("mq_mm"), 1)
            for b in range(B):
                pe.wait_ge(s("mq_cp"), b + 1)
                if b == 1:
                    mm(bank[4][0:1, 0:P], cols[:, 2:3], attn_w[:, 5]).then_inc(s("borow_mm"), 1)
                for j in range(TB):
                    mm(bank[b][:, j * P:(j + 1) * P], xnT[:, (b * TB + j) * P:(b * TB + j + 1) * P], mq[:, b],
                       True, False)
                    last = mm(bank[b][:, j * P:(j + 1) * P], ones[0:1, :], mqrow[:, b], False, True)
                last.then_inc(s("at_mm"), 1)
            pe.wait_ge(s("borow_cp"), 1)
            pe.wait_ge(s("parts_done"), 1)
            pe.wait_ge(s("wog_done"), 2)
            for b in range(B):
                for j in range(TB):
                    t = b * TB + j
                    last = tr(bank[4 + b][:].bitcast(BF16)[0:3 * E0, j * P:(j + 1) * P],
                              gate0_parts[:, t].rearrange("p a e -> p (a e)"), ident_bf[:])
                last.then_inc(s("g0T_mm"), 1)

            def attention_to_channels(b):
                pe.wait_ge(s("at_norm"), b + 1)
                pe.wait_ge(s("g0T_cp"), b + 1)
                for j in range(TB):
                    last = tr(bank[4 + b][:, j * P:(j + 1) * P], attn_n[:, b * TB + j])
                last.then_inc(s("atT_mm"), 1)

            def attention_output(b):
                pe.wait_ge(s("atT_cp"), b + 1)
                for j in range(TB):
                    t = b * TB + j
                    mm(bank[b][:, j * P:(j + 1) * P], attn_nT[:, t * P:(t + 1) * P], wo_g[:], True, False)
                    last = mm(bank[b][:, j * P:(j + 1) * P], ones[0:1, :], borow[:], False, True)
                last.then_inc(s("so_mm"), 1)

            attention_to_channels(0)
            for b in range(1, B):
                attention_to_channels(b)
                attention_output(b - 1)
            attention_output(B - 1)

            pe.wait_ge(s("w_lo_done"), 2)
            pe.wait_ge(s("xnT_lo_done"), B)
            pe.wait_ge(s("ld_wd"), 16)
            pe.wait_ge(s("polar_x0"), 1)
            pe.wait_ge(s("so_cp"), B)
            pe.wait_ge(s("atT_cp"), B)

            def split_product(out, m, u, cols_):
                mm(out, wgu_hi[:, m, u], xnT_lo[:, cols_], True, False)
                mm(out, wgu_hi[:, m, u], xnT_hi[:, cols_], False, False)
                return mm(out, wgu_lo[:, m, u], xnT_hi[:, cols_], False, True)

            def down(n, u, third, batch):
                pe.wait_ge(s("h0_done"), n + 1)
                if u == 0:
                    after(pe, s("y0_silu"), batch)
                mm(bank[6][:], wd[:, u], h0[:, third], u == 0, u == UNITS - 1).then_inc(s("dn_mm"), 1)

            def polar_products(i, p):
                r, stage = divmod(p, 4)
                if r >= POLAR_PER_BATCH or is_turn(i, -1):
                    return
                n = i * POLAR_PER_BATCH + r
                if stage == 0:
                    if r > 0:
                        pe.wait_ge(s("polar_x_cp"), n)
                    mm(bank[7][:, 0:P], polar_x[:], polar_x[:])
                    tr(bank[7][:, P:2 * P], polar_x[:]).then_inc(s("polar_a_mm"), 1)
                elif stage == 1:
                    pe.wait_ge(s("polar_ab_done"), n + 1)
                    mm(bank[7][:, 0:P], polar_gx[:, 0:P], polar_gx[:, 0:P]).then_inc(s("polar_a2_mm"), 1)
                elif stage == 2:
                    pe.wait_ge(s("polar_b_done"), n + 1)
                    mm(bank[7][:, 0:P], polar_gx[:, P:2 * P], polar_b[:]).then_inc(s("polar_x_mm"), 1)

            def silu_y_tokens(i):
                pe.wait_ge(s("y0_silu"), i + 1)
                pe.wait_ge(s("polar_x_cp"), (i + 1) * POLAR_PER_BATCH)
                for j in range(TB):
                    last = tr(bank[7][:, j * P:(j + 1) * P], gl0T[:, j * P:(j + 1) * P])
                last.then_inc(s("y0T_mm"), 1)

            def turn(i):
                for p in turn_positions(i):
                    n, u, gated = unit_at(i, p)
                    batch = i if p + HEAD < UNITS else i + 1
                    k = p % 2
                    tokens = bass.ds(batch * N, N)
                    after(pe, s("silu_done"), pair_user(n, p))
                    split_product(bank[k][:], 0, u, tokens).then_inc(s("g_mm"), 1)
                    after(pe, s("h0_done"), pair_user(n, p))
                    split_product(bank[2 + k][:], 1, u, tokens).then_inc(s("u_mm"), 1)
                    if u >= 1:
                        sel = pair_sel[:, 2 * (u - 1):2 * u].rearrange("p e i -> p (e i)")
                        mm(bank[4 + k][:], sel, gate0T[:, tokens]).then_inc(s("gb_mm"), 1)
                    if not is_turn(i, -1) or u >= 2:
                        down(n - 2, (u - 2) % UNITS, (p - 2 if p >= 2 else p - 2 + UNITS) % 3, batch)
                    polar_products(i, p)
                    if p == UNITS - HEAD + 3 and not is_turn(i, -1):
                        silu_y_tokens(i)

            turn(-1)
            with pe.Fori(0, B - 1) as i:
                turn(i)
            turn(B - 1)
            for u in range(UNITS - 2, UNITS):
                down((B - 1) * UNITS + u, u, (u - HEAD) % 3, B - 1)

            def tokens_to_channels(b):
                pe.wait_ge(s("l1_norm"), b + 1)
                for j in range(TB):
                    last = tr(bank[4 + b][:, j * P:(j + 1) * P], xn1[:, b * TB + j])
                last.then_inc(s("x1T_mm"), 1)

            def scan_input(b):
                pe.wait_ge(s("x1T_cp"), b + 1)
                for j in range(TB):
                    t = b * TB + j
                    last = mm(bank[b][:, j * P:(j + 1) * P], xnT[:, t * P:(t + 1) * P], l1_w[:, 0])
                last.then_inc(s("uptok_mm"), 1)

            tokens_to_channels(0)
            tokens_to_channels(1)
            silu_y_tokens(B - 1)
            tokens_to_channels(2)
            pe.wait_ge(s("ld_l1"), LD_L1)
            for b in range(B - 1):
                scan_input(b)
            def router_logits():
                for t in range(NT):
                    last = mm(bank[7][:, t * E1:(t + 1) * E1], xnT[:, t * P:(t + 1) * P], gate1_w[:])
                last.then_inc(s("log1_mm"), 1)

            def gated_biases():
                for b in range(B):
                    for j in range(TB):
                        last = tr(bank[3 + b][0:E1, j * P:(j + 1) * P], gate1[:, b * TB + j])
                    last.then_inc(s("g1T_mm"), 1)
                for b in range(B):
                    pe.wait_ge(s("g1T_cp"), b + 1)
                    for j in range(TB):
                        t = b * TB + j
                        last = mm(bank[3 + b][:, j * P:(j + 1) * P], gate1T[:, t * P:(t + 1) * P], b2[:])
                    last.then_inc(s("acc_mm"), 1)


            def state_channels(k, b):
                pe.wait_ge(s("xtok_done"), k + 1)
                after(pe, s("xT_cp"), k)
                for j in range(TB):
                    last = tr(bank[0][:, j * P:(j + 1) * P], x_tok[:, b, j])
                last.then_inc(s("state_mm"), 1)

            def left_tokens(k, b):
                pe.wait_ge(s("leftT_cp"), k + 1)
                after(pe, s("prod_done"), k)
                for j in range(TB):
                    last = tr(bank[1][:, j * P:(j + 1) * P], leftT[:, b, j * P:(j + 1) * P])
                last.then_inc(s("left_mm"), 1)

            def values(k, b):
                pe.wait_ge(s("sum_done"), k + 1)
                after(pe, s("v_cp"), k)
                for j in range(TB):
                    last = mm(bank[2][:, j * P:(j + 1) * P], sumT[:, b, j * P:(j + 1) * P], polar_x[:])
                last.then_inc(s("v_mm"), 1)

            def expert_up(e, blk, c):
                if blk == 0:
                    pe.wait_ge(s(f"ld_w1_{c}"), e * 16 + 16)
                mm(bank[3 + c][:], w1[:, c], xnT[:, blk * N:(blk + 1) * N]).then_inc(s("ffn_up"), 1)

            def expert_down(e, blk, tiles):
                n = e * B + blk
                if 0 in tiles:
                    pe.wait_ge(s("ffn_relu"), (n + 1) * HC)
                    if blk == 0:
                        pe.wait_ge(s("ld_w2"), e * 16 + 16)
                    after(pe, s("ffn_acc"), n * TB)
                for j in tiles:
                    for c in range(HC):
                        last = mm(bank[7][:, j * P:(j + 1) * P], hT[:, c, j * P:(j + 1) * P],
                                  w2[:, c], c == 0, c == HC - 1)
                if TB - 1 in tiles:
                    last.then_inc(s("ffn_down"), 1)

            def slot(k, b, this=True, ahead=True, up=None, down=None, then=None):
                if ahead:
                    state_channels(k + 1, (b + 1) % B)
                if this:
                    values(k, b)
                if down:
                    expert_down(*down, range(0, TB // 2))
                if ahead:
                    left_tokens(k + 1, (b + 1) % B)
                if down:
                    expert_down(*down, range(TB // 2, TB))
                if then:
                    then()
                if up:
                    for c in range(HC):
                        expert_up(*up, c)

            def level(lev, last=False):
                for j in range(B):
                    up = (lev, j + 1) if j < B - 1 else None if last else (lev + 1, 0)
                    slot(lev * B + (j + 1), (j + 1) % B, up=up, down=(lev, j))

            state_channels(0, 0)
            pe.wait_ge(s("sg_done"), B)
            tokens_to_channels(B - 1)
            left_tokens(0, 0)
            scan_input(B - 1)
            router_logits()
            slot(0, 0, up=(0, 0))
            with pe.Fori(0, LEVELS - 2) as lev:
                level(lev)
            level(LEVELS - 2, last=True)
            slot((LEVELS - 1) * B + 1, 1, then=gated_biases)
            slot((LEVELS - 1) * B + 2, 2)
            slot((LEVELS - 1) * B + 3, 3, ahead=False)

            pe.wait_ge(s("ffn_acc"), E1 * B * TB)
            pe.wait_ge(s("acc_done"), B)
            for b in range(B):
                mm(bank[4 + b][:], l1_w[:, 1], xnT[:, b * N:(b + 1) * N]).then_inc(s("v1_mm"), 1)
            pe.wait_ge(s("v_cp"), LEVELS * B)
            pe.wait_ge(s("prod_done"), LEVELS * B)

            def final_state(b):
                pe.wait_ge(s("xtok_done"), LEVELS * B + b + 1)
                for j in range(TB):
                    last = tr(bank[b][:, j * P:(j + 1) * P], x_tok[:, b, j])
                last.then_inc(s("qT_mm"), 1)

            def project(b):
                pe.wait_ge(s("qv_done"), b + 1)
                for j in range(TB):
                    last = mm(bank[b][:, j * P:(j + 1) * P], qvT[:, b, j * P:(j + 1) * P], l1_w[:, 2])
                last.then_inc(s("yp_mm"), 1)

            final_state(0)
            for b in range(1, B):
                final_state(b)
                project(b - 1)
            project(B - 1)

        @block.scalar
        def _(act):
            a = nc.scalar
            def root(out, in_, done, n, slot):
                log = ln_log[:, slot:slot + in_.shape[1]]
                a.activation(log, in_, ACT.Ln).then_inc(s(done), 1)
                act.wait_ge(s(done), 2 * n + 1)
                a.activation(out, log, ACT.Exp, scale=-0.5).then_inc(s(done), 1)

            def norm_roots(var, done, b, which):
                act.wait_ge(s(var), b + 1)
                root(ln_rstd[:, b * TB:(b + 1) * TB], ln_var[:, b * TB:(b + 1) * TB], done, b, which * NT + b * TB)

            a.preload_act_table_set(EXP_LN)
            act.wait_ge(s("ld_scan"), 16)
            a.activation(polar_sq[:], polar_x[:], ACT.Square, accum_out=polar_col[:]).then_inc(s("polar_sq_done"), 1)
            def channels_out0(b):
                act.wait_ge(s("xnT_mm"), b + 1)
                a.copy(xnT[:, b * N:(b + 1) * N], bank[4 + b][:]).then_inc(s("xnT_cp"), 1)

            norm_roots("ln_var_done", "ln_pow", 0, 0)
            act.wait_ge(s("polar_sum_mm"), 1)
            a.copy(polar_sum[:], bank[7][:, 0:1]).then_inc(s("polar_sum_cp"), 1)
            act.wait_ge(s("polar_sum_cp"), 1)
            root(polar_r[:], polar_sum[:], "polar_r_done", 0, 3 * NT)
            for b in range(1, B):
                norm_roots("ln_var_done", "ln_pow", b, 0)
                channels_out0(b - 1)
            channels_out0(B - 1)
            act.wait_ge(s("xnT_cp"), B)
            for b in range(B):
                a.copy(xnT_hi[:, b * N:(b + 1) * N], xnT[:, b * N:(b + 1) * N]).then_inc(s("xnT_hi_cp"), 1)
            act.wait_ge(s("logit_mm"), B)
            a.activation(scores0[:].rearrange("p t e -> p (t e)"), bank[3][:], ACT.Sigmoid).then_inc(s("sig_done"), 1)
            for b in range(B):
                act.wait_ge(s("gram_mm"), b + 1)
                a.copy(gram[:, b], bank[b][:, 0:P + 1])
                a.copy(srow[:, b], bank[b][0:1, 256:256 + P]).then_inc(s("gram_cp"), 1)
            for b in range(B):
                act.wait_ge(s("m1_mm"), b + 1)
                a.copy(m1[:, b], bank[4 + b][:, 0:256])
                a.copy(m1row[:, b], bank[4 + b][0:1, 256:512]).then_inc(s("m1_cp"), 1)
            for b in range(B):
                act.wait_ge(s("mq_mm"), b + 1)
                a.copy(mq[:, b], bank[4 + b][:, 0:P])
                a.copy(mqrow[:, b], bank[4 + b][0:1, P:2 * P]).then_inc(s("mq_cp"), 1)
            a.preload_act_table_set(EXP_LN)
            def attention_channels_out(b):
                act.wait_ge(s("atT_mm"), b + 1)
                a.copy(attn_nT[:, b * N:(b + 1) * N], bank[4 + b][:]).then_inc(s("atT_cp"), 1)

            def attention_out(b):
                act.wait_ge(s("so_mm"), b + 1)
                a.copy(s_tok[:, b * TB:(b + 1) * TB].rearrange("p j c -> p (j c)"), bank[b][:]).then_inc(s("so_cp"), 1)

            norm_roots("at_var", "at_pow", 0, 1)
            norm_roots("at_var", "at_pow", 1, 1)
            for b in range(B):
                act.wait_ge(s("g0T_mm"), b + 1)
                a.copy(gate0T[:, b * N:(b + 1) * N], bank[4 + b][:].bitcast(BF16)[0:3 * E0, 0:N]).then_inc(s("g0T_cp"), 1)
            for b in range(B):
                attention_channels_out(b)
                if b + 2 < B:
                    norm_roots("at_var", "at_pow", b + 2, 1)
                if b >= 1:
                    attention_out(b - 1)
            attention_out(B - 1)

            def silu_y(b):
                act.wait_ge(s("dn_mm"), (b + 1) * UNITS)
                a.activation(gl0T[:], bank[6][:], ACT.Silu).then_inc(s("y0_silu"), 1)

            def turn(i):
                for p in turn_positions(i):
                    n, u, gated = unit_at(i, p)
                    if p == UNITS - HEAD + 2 and not is_turn(i, -1):
                        silu_y(i)
                    act.wait_ge(s("g_mm"), n + 1)
                    after(act, s("h0_done"), pair_user(n, p))
                    a.activation(silu_g[:, p % 2], bank[p % 2][:], ACT.Silu).then_inc(s("silu_done"), 1)

            turn(-1)
            with act.Fori(0, B - 1) as i:
                turn(i)
            turn(B - 1)
            def channels_out(b):
                act.wait_ge(s("x1T_mm"), b + 1)
                a.copy(xnT[:, b * N:(b + 1) * N], bank[4 + b][:]).then_inc(s("x1T_cp"), 1)

            def scan_input_out(b):
                act.wait_ge(s("uptok_mm"), b + 1)
                a.copy(x_tok[:, b].rearrange("p j c -> p (j c)"), bank[b][:]).then_inc(s("xtok_done"), 1)

            a.preload_act_table_set(EXP_LN)
            for b in range(B - 1):
                norm_roots("l1_var", "l1_pow", b, 2)
            silu_y(B - 1)
            channels_out(0)
            channels_out(1)
            a.preload_act_table_set(EXP_LN)
            channels_out(2)
            scan_input_out(0)
            norm_roots("l1_var", "l1_pow", B - 1, 2)
            scan_input_out(1)
            scan_input_out(2)

            def router_exp():
                act.wait_ge(s("lsub_done"), 1)
                a.activation(lexp[:], lsub[:], ACT.Exp).then_inc(s("lexp_done"), 1)

            def gates_out():
                for b in range(B):
                    act.wait_ge(s("g1T_mm"), b + 1)
                    a.copy(gate1T[:, b * N:(b + 1) * N], bank[3 + b][0:E1, :]).then_inc(s("g1T_cp"), 1)

            act.wait_ge(s("pad_done"), B)

            def state_in(k, b, lev):
                act.wait_ge(s("state_mm"), k + 1)
                a.copy(xT[:, b, PAD:PAD + N], bank[0][:]).then_inc(s("xT_cp"), 1)
                act.wait_ge(s("xT_cp"), k + 1)
                a.copy(leftT[:, b], xT[:, b, bass.ds(PAD - (1 << lev), N)]).then_inc(s("leftT_cp"), 1)

            def left_out(k, b):
                act.wait_ge(s("left_mm"), k + 1)
                a.copy(left_tok[:, b].rearrange("p j c -> p (j c)"), bank[1][:]).then_inc(s("left_tok_cp"), 1)

            def values_out(k, b):
                act.wait_ge(s("v_mm"), k + 1)
                a.copy(v_tok[:, b % 2].rearrange("p j c -> p (j c)"), bank[2][:]).then_inc(s("v_cp"), 1)

            def expo(k, b):
                act.wait_ge(s("ssub_done"), k + 1)
                a.activation(sexp[:, b % 2], ssub[:, b % 2], ACT.Exp, scale=float(LD) ** -0.5).then_inc(s("sexp_done"), 1)

            def square(k, b):
                act.wait_ge(s("z_done"), k + 1)
                a.activation(z_sq[:, b % 2], z[:, b % 2], ACT.Square).then_inc(s("zsq_done"), 1)

            def rsqrt(k, b):
                act.wait_ge(s("zms_done"), k + 1)
                a.activation(z_ln[:, b % 2], z_ms[:, b % 2], ACT.Ln).then_inc(s("zln_done"), 1)
                act.wait_ge(s("zln_done"), k + 1)
                a.activation(z_rs[:, b % 2], z_ln[:, b % 2], ACT.Exp, scale=-0.5).then_inc(s("zrs_done"), 1)

            def relu(e, blk, c):
                act.wait_ge(s("ffn_up"), (e * B + blk) * HC + c + 1)
                after(act, s("ffn_down"), e * B + blk)
                a.activation(hT[:, c], bank[3 + c][:], ACT.Relu, bias=b1_now[:, c:c + 1]).then_inc(s("ffn_relu"), 1)

            def slot(k, b, lev_next, this=True, before=True, ahead=True, up=None, then=None):
                if ahead:
                    state_in(k + 1, (b + 1) % B, lev_next)
                if this:
                    values_out(k, b)
                if ahead:
                    left_out(k + 1, (b + 1) % B)
                if this:
                    expo(k, b)
                if before:
                    square(k - 1, (b - 1) % B)
                if then:
                    then()
                if up:
                    if up[1] == 0:
                        a.copy(b1_now[:], b1[:, bass.ds(up[0], 1)].rearrange("p e c -> p (e c)")).then_inc(s("b1_now_done"), 1)
                        act.wait_ge(s("b1_now_done"), up[0] + 1)
                    relu(*up, 0)
                    relu(*up, 1)
                if before:
                    rsqrt(k - 1, (b - 1) % B)
                if up:
                    relu(*up, 2)
                    relu(*up, 3)

            def level(lev, last=False):
                for j in range(B):
                    up = (lev, j + 1) if j < B - 1 else None if last else (lev + 1, 0)
                    slot(lev * B + (j + 1), (j + 1) % B, lev if j < 2 else lev + 1, up=up)

            state_in(0, 0, 0)
            channels_out(B - 1)
            left_out(0, 0)
            scan_input_out(B - 1)
            slot(0, 0, 0, before=False, up=(0, 0), then=router_exp)
            with act.Fori(0, LEVELS - 2) as lev:
                level(lev)
            level(LEVELS - 2, last=True)
            top = LEVELS - 1
            slot(top * B + 1, 1, top, then=gates_out)
            slot(top * B + 2, 2, top)
            slot(top * B + 3, 3, top, ahead=False)
            for b in range(B):
                act.wait_ge(s("v1_mm"), b + 1)
                a.copy(sumT[:, b], bank[4 + b][:]).then_inc(s("v1_cp"), 1)
            slot(top * B + 4, 0, top, this=False, ahead=False)

            for b in range(B):
                act.wait_ge(s("acc_done"), b + 1)
                a.activation(acc[:, b * TB:(b + 1) * TB], acc[:, b * TB:(b + 1) * TB], ACT.Silu).then_inc(s("gl1_done"), 1)

        @block.vector
        def _(dve):
            v = nc.vector
            tt, ts, stt = v.tensor_tensor, v.tensor_scalar, v.scalar_tensor_tensor

            def layer_norm(b, src_tile, stat, var):
                t0 = b * TB
                for j in range(TB):
                    last = v.bn_stats(ln_stats[:, t0 + j], src_tile(t0 + j))
                last.then_inc(s(stat), 1)
                dve.wait_ge(s(stat), 2 * b + 1)
                for j in range(TB):
                    last = v.bn_aggr(ln_mv[:, t0 + j], ln_stats[:, t0 + j])
                last.then_inc(s(stat), 1)
                dve.wait_ge(s(stat), 2 * b + 2)
                ts(ln_var[:, t0:t0 + TB], ln_mv[:, t0:t0 + TB, 1], LN_EPS, None, ALU.add).then_inc(s(var), 1)

            def normalise(b, src_tile, out_tile, pow_, norm):
                t0 = b * TB
                dve.wait_ge(s(pow_), 2 * b + 2)
                for j in range(TB):
                    last = ts(out_tile(t0 + j), src_tile(t0 + j), ln_mv[:, t0 + j, 0:1], ln_rstd[:, t0 + j:t0 + j + 1],
                              ALU.subtract, ALU.mult)
                last.then_inc(s(norm), 1)

            for b in range(B):
                dve.wait_ge(s(f"ld_x{b}"), 16)
                layer_norm(b, lambda t: x[:, t], "ln_stat", "ln_var_done")
                if b >= 1:
                    normalise(b - 1, lambda t: x[:, t], lambda t: xn[:, t, 0:P], "ln_pow", "ln_norm")
            normalise(B - 1, lambda t: x[:, t], lambda t: xn[:, t, 0:P], "ln_pow", "ln_norm")
            dve.wait_ge(s("const"), IDENT_READY)
            dve.wait_ge(s("ld_small"), LD_SMALL)
            tt(attn_w[:, 0:5], attn_w[:, 0:5], ident[:].unsqueeze(1).broadcast_to([P, 5, P]), ALU.add).then_inc(s("wfold"), 1)
            ts(wo_g[:], attn_w[:, 5], cols[:, 1:2], None, ALU.mult).then_inc(s("wog_done"), 1)
            v.tensor_copy(ident_bf[:], ident[:]).then_inc(s("wog_done"), 1)
            dve.wait_ge(s("polar_r_done"), 2)
            ts(polar_x[:], polar_x[:], polar_r[:], None, ALU.mult).then_inc(s("polar_x0"), 1)

            def state_out(b):
                dve.wait_ge(s("st_mm"), b + 1)
                stt(state0[:, b], bank[b][:, 0:P], 1.0 / (N * N), head_mask[:], ALU.mult, ALU.mult).then_inc(s("st0_cp"), 1)

            def state_out2(b):
                dve.wait_ge(s("st0_cp"), b + 1)
                tt(state[:, b], state0[:, b], bank[b][:, P:2 * P], ALU.mult).then_inc(s("st_cp"), 1)

            dve.wait_ge(s("const"), CONSTS)
            dve.wait_ge(s("sig_done"), 1)
            tt(choice[:], scores0[:], gate0_bias[:].unsqueeze(1).broadcast_to([P, NT, E0]), ALU.add).then_inc(s("route0_step"), 1)
            dve.wait_ge(s("route0_step"), 1)
            for t in range(NT):
                for gr in range(GROUPS):
                    last = v.max(top8[:, t, gr], choice[:, t, gr * GE:(gr + 1) * GE])
            last.then_inc(s("route0_step"), 1)
            dve.wait_ge(s("route0_step"), 2)
            tt(gscore[:], top8[:, :, :, 0], top8[:, :, :, 1], ALU.add).then_inc(s("route0_step"), 1)
            dve.wait_ge(s("route0_step"), 3)
            for g_ in range(GROUPS):
                me = gscore[:, :, g_:g_ + 1]
                if g_ > 0:
                    last = tt(gcmp[:, :, g_, 0:g_], gscore[:, :, 0:g_], me.broadcast_to([P, NT, g_]), ALU.is_ge)
                if g_ < GROUPS - 1:
                    last = tt(gcmp[:, :, g_, g_ + 1:], gscore[:, :, g_ + 1:], me.broadcast_to([P, NT, GROUPS - 1 - g_]), ALU.is_gt)
            last.then_inc(s("route0_step"), 1)
            dve.wait_ge(s("route0_step"), 4)
            v.tensor_reduce(grank[:], gcmp[:], AX_X, ALU.add).then_inc(s("route0_step"), 1)
            dve.wait_ge(s("route0_step"), 5)
            ts(gmask[:], grank[:], 2.0, None, ALU.is_lt).then_inc(s("route0_step"), 1)
            dve.wait_ge(s("route0_step"), 6)
            tt(masked[:].rearrange("p t (g e) -> p t g e", g=GROUPS), choice[:].rearrange("p t (g e) -> p t g e", g=GROUPS),
               gmask[:].unsqueeze(3).broadcast_to([P, NT, GROUPS, GE]), ALU.mult).then_inc(s("route0_step"), 1)
            dve.wait_ge(s("route0_step"), 7)
            for t in range(NT):
                last = v.max(best8[:, t], masked[:, t])
            last.then_inc(s("route0_step"), 1)
            dve.wait_ge(s("route0_step"), 8)
            for t in range(NT):
                last = v.match_replace(replaced[:, t], best8[:, t], masked[:, t], FAR)
            last.then_inc(s("route0_step"), 1)
            dve.wait_ge(s("route0_step"), 9)
            ts(taken[:], replaced[:], FAR, None, ALU.is_equal).then_inc(s("route0_step"), 1)
            dve.wait_ge(s("route0_step"), 10)
            tt(gate0[:], taken[:], scores0[:], ALU.mult).then_inc(s("route0_step"), 1)
            dve.wait_ge(s("route0_step"), 11)
            v.tensor_reduce(wsum[:], gate0[:], AX_X, ALU.add).then_inc(s("route0_step"), 1)
            dve.wait_ge(s("route0_step"), 12)
            ts(wsum_eps[:], wsum[:], 1e-20, None, ALU.add).then_inc(s("route0_step"), 1)
            dve.wait_ge(s("route0_step"), 13)
            v.reciprocal(wrec[:], wsum_eps[:]).then_inc(s("route0_step"), 1)
            dve.wait_ge(s("route0_step"), 14)
            stt(gate0_rest[:], gate0[:], ROUTED, wrec[:].unsqueeze(2).broadcast_to([P, NT, E0]), ALU.mult, ALU.mult).then_inc(s("route0_step"), 1)
            dve.wait_ge(s("route0_step"), 15)
            v.tensor_copy(gate0_parts[:, :, 0], gate0_rest[:]).then_inc(s("route0_step"), 1)
            dve.wait_ge(s("route0_step"), 16)
            tt(gate0_rest2[:], gate0_rest[:], gate0_parts[:, :, 0], ALU.subtract).then_inc(s("route0_step"), 1)
            dve.wait_ge(s("route0_step"), 17)
            v.tensor_copy(gate0_parts[:, :, 1], gate0_rest2[:]).then_inc(s("route0_step"), 1)
            dve.wait_ge(s("route0_step"), 18)
            tt(gate0_parts[:, :, 2], gate0_rest2[:], gate0_parts[:, :, 1], ALU.subtract).then_inc(s("parts_done"), 1)

            for b in range(B):
                state_out(b)
                state_out2(b)

            attn_tile = lambda t: bank[t // TB][:, (t % TB) * P:(t % TB + 1) * P]
            for b in range(B):
                dve.wait_ge(s("at_mm"), b + 1)
                if b == 1:
                    dve.wait_ge(s("borow_mm"), 1)
                    tt(borow[:], bank[4][0:1, 0:P], rows[:, 4 * P:5 * P], ALU.add).then_inc(s("borow_cp"), 1)
                layer_norm(b, attn_tile, "at_stat", "at_var")
                if b >= 1:
                    normalise(b - 1, attn_tile, lambda t: attn_n[:, t], "at_pow", "at_norm")
            normalise(B - 1, attn_tile, lambda t: attn_n[:, t], "at_pow", "at_norm")

            dve.wait_ge(s("polar_const"), 3 * len(POLAR))
            dve.wait_ge(s("polar_x0"), 1)

            def polar_step(i, p):
                r, stage = divmod(p, 4)
                if r >= POLAR_PER_BATCH or is_turn(i, -1):
                    return
                n = i * POLAR_PER_BATCH + r

                def co(m):
                    return coef[:, bass.ds(n * 3 + m, 1)]
                if stage == 0:
                    ts(polar_ai[:], ident[:], co(0), None, ALU.mult).then_inc(s("polar_ai_done"), 1)
                    dve.wait_ge(s("polar_a_mm"), n + 1)
                    v.tensor_copy(polar_gx[:], bank[7][:, 0:256]).then_inc(s("polar_gx_cp"), 1)
                    dve.wait_ge(s("polar_gx_cp"), n + 1)
                    stt(polar_ab[:], polar_gx[:, 0:P], co(1), polar_ai[:], ALU.mult, ALU.add).then_inc(s("polar_ab_done"), 1)
                elif stage == 1:
                    dve.wait_ge(s("polar_a2_mm"), n + 1)
                    dve.wait_ge(s("polar_ab_done"), n + 1)
                    stt(polar_b[:], bank[7][:, 0:P], co(2), polar_ab[:], ALU.mult, ALU.add).then_inc(s("polar_b_done"), 1)
                elif stage == 2:
                    dve.wait_ge(s("polar_x_mm"), n + 1)
                    v.tensor_copy(polar_x[:], bank[7][:, 0:P]).then_inc(s("polar_x_cp"), 1)

            def add_to_x(i):
                dve.wait_ge(s("y0T_mm"), i + 1)
                tt(sg[:], s_tok[:, bass.ds(i * TB, TB)].rearrange("p j c -> p (j c)"), bank[7][:], ALU.mult).then_inc(s("sg_done"), 1)
                dve.wait_ge(s("sg_done"), i + 1)
                xi = x[:, bass.ds(i * TB, TB)].rearrange("p j c -> p (j c)")
                tt(xi, xi, sg[:], ALU.add).then_inc(s("x1_done"), 1)

            def turn(i):
                for p in turn_positions(i):
                    n, u, gated = unit_at(i, p)
                    k = p % 2
                    dve.wait_ge(s("silu_done"), n + 1)
                    dve.wait_ge(s("u_mm"), n + 1)
                    if u == 0:
                        after(dve, s("dn_mm"), ring_user(n, p))
                        tt(h0[:, p % 3], silu_g[:, k], bank[2 + k][:], ALU.mult).then_inc(s("h0_done"), 1)
                    else:
                        tt(silu_gu[:, k], silu_g[:, k], bank[2 + k][:], ALU.mult).then_inc(s("gu_done"), 1)
                        dve.wait_ge(s("gu_done"), gated)
                        dve.wait_ge(s("gb_mm"), gated)
                        after(dve, s("dn_mm"), ring_user(n, p))
                        tt(h0[:, p % 3], silu_gu[:, k], bank[4 + k][:], ALU.mult).then_inc(s("h0_done"), 1)
                    polar_step(i, p)
                    if p == UNITS - HEAD + 4 and not is_turn(i, -1):
                        add_to_x(i)
                    if is_turn(i, B - 1) and p in (1, 3, 5):
                        dve.wait_ge(s("x1_done"), B - 1)
                        layer_norm((p - 1) // 2, lambda t: x[:, t], "l1_stat", "l1_var")

            turn(-1)
            with dve.Fori(0, B - 1) as i:
                turn(i)
            turn(B - 1)
            for b in range(B - 1):
                normalise(b, lambda t: x[:, t], lambda t: xn1[:, t], "l1_pow", "l1_norm")
            add_to_x(B - 1)
            dve.wait_ge(s("x1_done"), B)
            layer_norm(B - 1, lambda t: x[:, t], "l1_stat", "l1_var")
            normalise(B - 1, lambda t: x[:, t], lambda t: xn1[:, t], "l1_pow", "l1_norm")
            def routing1():
                dve.wait_ge(s("log1_mm"), 1)
                tt(logits1[:], bank[7][:, 0:NT * E1].rearrange("p (t e) -> p t e", t=NT),
                   gate1_bias[:].unsqueeze(1).broadcast_to([P, NT, E1]), ALU.add).then_inc(s("log1_cp"), 1)
                dve.wait_ge(s("log1_cp"), 1)
                v.tensor_reduce(lmax[:], logits1[:], AX_X, ALU.max).then_inc(s("route1_step"), 1)
                dve.wait_ge(s("route1_step"), 1)
                tt(lsub[:], logits1[:], lmax[:].unsqueeze(2).broadcast_to([P, NT, E1]), ALU.subtract).then_inc(s("lsub_done"), 1)
                dve.wait_ge(s("ecmp_zero"), 1)
                for e in range(E1):
                    me = logits1[:, :, e:e + 1]
                    if e > 0:
                        last = tt(ecmp[:, :, e, 0:e], logits1[:, :, 0:e], me.broadcast_to([P, NT, e]), ALU.is_ge)
                    if e < E1 - 1:
                        last = tt(ecmp[:, :, e, e + 1:], logits1[:, :, e + 1:], me.broadcast_to([P, NT, E1 - 1 - e]), ALU.is_gt)
                last.then_inc(s("route1_step"), 1)
                dve.wait_ge(s("route1_step"), 2)
                v.tensor_reduce(erank[:], ecmp[:], AX_X, ALU.add).then_inc(s("route1_step"), 1)
                dve.wait_ge(s("lexp_done"), 1)
                v.tensor_reduce(lsum[:], lexp[:], AX_X, ALU.add).then_inc(s("route1_step"), 1)
                dve.wait_ge(s("route1_step"), 3)
                ts(emask[:], erank[:], 2.0, None, ALU.is_lt).then_inc(s("route1_step"), 1)
                dve.wait_ge(s("route1_step"), 4)
                v.reciprocal(lrec[:], lsum[:]).then_inc(s("route1_step"), 1)
                dve.wait_ge(s("route1_step"), 6)
                tt(probs1[:], lexp[:], lrec[:].unsqueeze(2).broadcast_to([P, NT, E1]), ALU.mult).then_inc(s("route1_step"), 1)
                dve.wait_ge(s("route1_step"), 7)
                dve.wait_ge(s("route1_step"), 5)
                tt(gate1[:], probs1[:], emask[:], ALU.mult).then_inc(s("gate1_done"), 1)


            def products(k, b):
                dve.wait_ge(s("left_tok_cp"), k + 1)
                left = bank[1][:].rearrange("p (j l d) -> p j l d", j=TB, l=LANES).unsqueeze(3)
                right = x_tok[:, b].rearrange("p j (m d) -> p j m d", m=LANES)[:, :, 0:LANES - 1].unsqueeze(2)
                tt(prod[:, b % 2, :, :, 0:LANES - 1], left.broadcast_to([P, TB, LANES, LANES - 1, LD]),
                   right.broadcast_to([P, TB, LANES, LANES - 1, LD]), ALU.mult).then_inc(s("prod_done"), 1)

            def add_lanes(k, b):
                dve.wait_ge(s("mix2_done"), k + 1)
                m = mix2[:, b % 2].rearrange("p j l m d -> p (j l) m d")
                tt(z[:, b % 2].rearrange("p j (l d) -> p (j l) d", l=LANES), m[:, :, 0], m[:, :, 1],
                   ALU.add).then_inc(s("z_done"), 1)

            def scores(k, b):
                dve.wait_ge(s("prod_done"), k + 1)
                dve.wait_ge(s("last_prod"), k + 1)
                v.tensor_reduce(score[:, b % 2], prod[:, b % 2], AX_X, ALU.add).then_inc(s("score_done"), 1)

            def score_max(k, b):
                dve.wait_ge(s("score_done"), k + 1)
                v.tensor_reduce(smax[:, b % 2], score[:, b % 2], AX_X, ALU.max).then_inc(s("smax_done"), 1)

            def softmax_shift(k, b):
                dve.wait_ge(s("smax_done"), k + 1)
                tt(ssub[:, b % 2], score[:, b % 2], smax[:, b % 2].unsqueeze(3).broadcast_to([P, TB, LANES, LANES]),
                   ALU.subtract).then_inc(s("ssub_done"), 1)

            def eps_term(k, b):
                dve.wait_ge(s("ssum_done"), k + 1)
                stt(eps_ss[:, b % 2], ssum[:, b % 2], RMS_EPS, ssum[:, b % 2], ALU.mult, ALU.mult).then_inc(s("epsss_done"), 1)

            def square_sum(k, b):
                dve.wait_ge(s("zsq_done"), k + 1)
                v.tensor_reduce(z_ss[:, b % 2], z_sq[:, b % 2].rearrange("p j (l d) -> p j l d", l=LANES), AX_X,
                                ALU.add).then_inc(s("zss_done"), 1)

            def mean_square(k, b):
                dve.wait_ge(s("epsss_done"), k + 1)
                dve.wait_ge(s("zss_done"), k + 1)
                stt(z_ms[:, b % 2], z_ss[:, b % 2], 1.0 / LD, eps_ss[:, b % 2], ALU.mult, ALU.add).then_inc(s("zms_done"), 1)

            def exp_sum(k, b):
                dve.wait_ge(s("sexp_done"), k + 1)
                v.tensor_reduce(ssum[:, b % 2], sexp[:, b % 2], AX_X, ALU.add).then_inc(s("ssum_done"), 1)

            def mix_values(k, b):
                dve.wait_ge(s("v_cp"), k + 1)
                values = v_tok[:, b % 2].rearrange("p j (m d) -> p j m d", m=LANES)[:, :, 0:LANES - 1].unsqueeze(2)
                tt(mix[:, b % 2, :, :, 0:LANES - 1],
                   sexp[:, b % 2, :, :, 0:LANES - 1].unsqueeze(4).broadcast_to([P, TB, LANES, LANES - 1, LD]),
                   values.broadcast_to([P, TB, LANES, LANES - 1, LD]), ALU.mult).then_inc(s("mix_done"), 1)

            def expert_gates(e, blk):
                if blk == 0:
                    v.tensor_copy(gate1_now[:], gate1[:, :, bass.ds(e, 1)].rearrange("p t e -> p (t e)")).then_inc(s("gate_now_done"), 1)
                    dve.wait_ge(s("gate_now_done"), e + 1)

            def expert_sum(e, blk, tiles):
                dve.wait_ge(s("ffn_down"), e * B + blk + 1)
                for j in tiles:
                    t = blk * TB + j
                    stt(acc[:, t], bank[7][:, j * P:(j + 1) * P], gate1_now[:, t:t + 1], acc[:, t],
                        ALU.mult, ALU.add).then_inc(s("ffn_acc"), 1)

            def slot(k, b, this=True, before=True, summed=None):
                prev = (k - 1, (b - 1) % B)
                if this:
                    products(k, b)
                if before:
                    eps_term(*prev)
                if this:
                    scores(k, b)
                if before:
                    add_lanes(*prev)
                if summed:
                    expert_gates(*summed)
                if this:
                    score_max(k, b)
                if summed:
                    expert_sum(*summed, range(0, 1))
                if this:
                    softmax_shift(k, b)
                if summed:
                    expert_sum(*summed, range(1, TB))
                if before:
                    square_sum(*prev)
                if this:
                    exp_sum(k, b)
                if before:
                    mean_square(*prev)
                if this:
                    mix_values(k, b)

            slot(0, 0, before=False)
            routing1()
            dve.wait_ge(s("gate1_done"), 1)
            dve.wait_ge(s("acc_zero"), 1)
            with dve.Fori(0, LEVELS - 1) as lev:
                for j in range(B):
                    slot(lev * B + (j + 1), (j + 1) % B, summed=(lev, j))
            for k in range(1, B):
                slot((LEVELS - 1) * B + k, k)
                if k == 2:
                    dve.wait_ge(s("ffn_acc"), E1 * B * TB)
                    for b in range(B):
                        dve.wait_ge(s("acc_mm"), b + 1)
                        ab = acc[:, b * TB:(b + 1) * TB].rearrange("p j c -> p (j c)")
                        tt(ab, ab, bank[3 + b][:], ALU.add).then_inc(s("acc_done"), 1)

            def gate_state(b):
                dve.wait_ge(s("v1_cp"), b + 1)
                dve.wait_ge(s("qT_mm"), b + 1)
                tt(qvT[:, b], sumT[:, b], bank[b][:], ALU.mult).then_inc(s("qv_done"), 1)

            gate_state(0)
            gate_state(1)
            slot(LEVELS * B, 0, this=False)

            def output(b):
                dve.wait_ge(s("yp_mm"), b + 1)
                dve.wait_ge(s("gl1_done"), b + 1)
                gb = acc[:, b * TB:(b + 1) * TB].rearrange("p j c -> p (j c)")
                tt(gb, bank[b][:], gb, ALU.mult).then_inc(s("o_mul"), 1)
                dve.wait_ge(s("o_mul"), b + 1)
                xb = x[:, b * TB:(b + 1) * TB].rearrange("p j c -> p (j c)")
                tt(xb, xb, gb, ALU.add).then_inc(s("o_done"), 1)

            gate_state(2)
            output(0)
            gate_state(3)
            for b in range(1, B):
                output(b)


_OUT_SHAPE = (B, N, P)


def kernel(**inputs):
    import numpy as np
    import concourse.bacc as bacc
    from concourse.bass_utils import run_bass_kernel_spmd as run

    w = {k: np.asarray(v) for k, v in inputs.items()}
    swap = lambda m: np.swapaxes(m, -1, -2)

    def experts_in(shared, experts):
        rows = np.concatenate([shared, experts.reshape(E0 * I0, P)]).reshape(PAIRS + 1, P, P)
        return rows.transpose(2, 0, 1)

    down = np.concatenate([swap(w["L0_ffn_shared_down"])[None],
                           swap(w["L0_ffn_expert_down"]).reshape(PAIRS, P, P)])
    arrays = {
        "x": w["L0_attn_x"],
        "cols": np.stack([w["L0_attn_bq"], w["L0_attn_ln_g"], w["L0_attn_ln_b"], w["L1_attn_identity"]], 1),
        "rows": np.concatenate([w["L0_attn_bk"].reshape(-1), w["L0_attn_bv"].reshape(-1), w["L0_attn_bo"]])[None],
        "gate0_bias": w["L0_ffn_gate_bias"],
        "gate1_bias": w["L1_ffn_gate_b"],
        "attn_w": np.stack([swap(w["L0_attn_Wq"]), *w["L0_attn_Wk"], *w["L0_attn_Wv"], w["L0_attn_Wo"]], 1),
        "gate0": swap(w["L0_ffn_gate_w"]),
        "wg": experts_in(w["L0_ffn_shared_gate"], w["L0_ffn_expert_gate"]),
        "wu": experts_in(w["L0_ffn_shared_up"], w["L0_ffn_expert_up"]),
        "wd": down.transpose(1, 0, 2),
        "scan_raw": w["L1_attn_W_scan_raw"],
        "l1_w": np.stack([swap(w["L1_attn_W_up"]), swap(w["L1_attn_W_v"]), swap(w["L1_attn_W_proj"])], 1),
        "gate1": swap(w["L1_ffn_gate_w"]),
        "w1": w["L1_ffn_w1"].reshape(E1, P, HC, P),
        "b1": w["L1_ffn_b1"].reshape(E1, HC, P).transpose(2, 0, 1),
        "w2": w["L1_ffn_w2"].reshape(E1, HC, P, P).transpose(2, 0, 1, 3),
        "b2": w["L1_ffn_b2"],
    }
    nc = bacc.Bacc("TRN2", target_bir_lowering=False, num_devices=1)
    feed, args = {}, []
    for name, value in arrays.items():
        value = np.ascontiguousarray(value)
        feed[f"in_{name}"] = value
        args.append(nc.dram_tensor(f"in_{name}", value.shape, mybir.dt.from_np(value.dtype), kind="ExternalInput").ap())
    args.append(nc.dram_tensor("out", _OUT_SHAPE, F32, kind="ExternalOutput").ap())
    build(nc, *args)
    return run(nc, [feed], core_ids=[0]).results[0]["out"]
```
